# Optimizing a Trainium2 kernel written in Bass

```python
import numpy as np
import jax
import jax.numpy as jnp

def _softmax(x, axis=-1):
    return jax.nn.softmax(x, axis=axis)

def _gelu(x):
    return jax.nn.gelu(x, approximate=True)

def _silu(x):
    return jax.nn.silu(x)

def _sigmoid(x):
    return jax.nn.sigmoid(x)

def _layernorm(x, axis=-1, eps=1e-05):
    m = jnp.mean(x, axis=axis, keepdims=True)
    v = jnp.var(x, axis=axis, keepdims=True)
    return (x - m) / jnp.sqrt(v + eps)

def _scatter_add(tgt, idx, src, axis=0):
    return tgt.at[idx].add(src)

def _segment_sum(src, seg, n):
    return jax.ops.segment_sum(src, seg, n)
kernel_name = 'mk_sandwich_d2_jaxref_r8_b8f403'

def setup_inputs(seed: int=0):
    np.random.seed(seed)
    _w = jnp.asarray

    def _L0_attn_setup():
        import jax, jax.numpy as jnp
        import numpy as np
        D_MODEL = 128
        EXPAND = 2
        D_EXPAND = D_MODEL * EXPAND
        D_STATE = 16
        DT_RANK = -(-D_MODEL // 16)
        BATCH = 4
        SEQ = 128

        def _mamba_forward(x, W_in, conv_w, conv_b, W_xproj, W_dt, b_dt, A_log, D, W_out):
            B, L, _ = x.shape
            d_exp = D.shape[0]
            n = A_log.shape[1]
            xz = x @ W_in.T
            u, z = jnp.split(xz, 2, axis=-1)
            uc = jax.lax.conv_general_dilated(u.transpose(0, 2, 1), conv_w, window_strides=(1,), padding=[(1, 1)], feature_group_count=d_exp, dimension_numbers=('NCH', 'OIH', 'NCH'))
            uc = jax.nn.silu(uc + conv_b[None, :, None]).transpose(0, 2, 1)
            proj = uc @ W_xproj.T
            B_ssm = proj[..., :n]
            C_ssm = proj[..., n:2 * n]
            dt = proj[..., 2 * n:]
            delta = jax.nn.softplus(dt @ W_dt.T + b_dt)
            A = -jnp.exp(A_log)

            def step(h, inp):
                u_t, d_t, b_t, c_t = inp
                dA = jnp.exp(d_t[:, :, None] * A)
                h = dA * h + (d_t * u_t)[:, :, None] * b_t[:, None, :]
                y_t = jnp.einsum('bdn,bn->bd', h, c_t)
                return (h, y_t)
            xs = (uc.transpose(1, 0, 2), delta.transpose(1, 0, 2), B_ssm.transpose(1, 0, 2), C_ssm.transpose(1, 0, 2))
            h0 = jnp.zeros((B, d_exp, n), dtype=uc.dtype)
            _, ys = jax.lax.scan(step, h0, xs)
            y = ys.transpose(1, 0, 2) + uc * D
            y = y * jax.nn.silu(z)
            return y @ W_out.T
        key = jax.random.key(seed)
        ks = jax.random.split(key, 9)
        s = 0.02
        x = jax.random.normal(ks[0], (BATCH, SEQ, D_MODEL), dtype=jnp.float32)
        W_in = jax.random.normal(ks[1], (2 * D_EXPAND, D_MODEL), dtype=jnp.float32) * s
        conv_w = jax.random.normal(ks[2], (D_EXPAND, 1, 3), dtype=jnp.float32) * 0.3
        conv_b = jax.random.normal(ks[3], (D_EXPAND,), dtype=jnp.float32) * s
        W_xproj = jax.random.normal(ks[4], (2 * D_STATE + DT_RANK, D_EXPAND), dtype=jnp.float32) * s
        dt_std = DT_RANK ** (-0.5) * 0.5
        W_dt = jax.random.uniform(ks[5], (D_EXPAND, DT_RANK), dtype=jnp.float32, minval=-dt_std, maxval=dt_std)
        b_dt = jax.random.normal(ks[6], (D_EXPAND,), dtype=jnp.float32) * s
        A_log = jnp.log(jnp.tile(jnp.arange(1, D_STATE + 1, dtype=jnp.float32), (D_EXPAND, 1)))
        D = jnp.ones((D_EXPAND,), dtype=jnp.float32)
        W_out = jax.random.normal(ks[7], (D_MODEL, D_EXPAND), dtype=jnp.float32) * s
        return {'x': x, 'W_in': W_in, 'conv_w': conv_w, 'conv_b': conv_b, 'W_xproj': W_xproj, 'W_dt': W_dt, 'b_dt': b_dt, 'A_log': A_log, 'D': D, 'W_out': W_out}
    _L0_attn_in = _L0_attn_setup()

    def _L0_ffn_setup():
        import jax, jax.numpy as jnp
        import numpy as np
        TOP_K = 2
        key = jax.random.key(seed)
        ks = jax.random.split(key, 6)
        B, S, H, F, E = (4, 256, 128, 512, 8)
        x = jax.random.normal(ks[0], (B, S, H), dtype=jnp.float32)
        gate_w = jax.random.normal(ks[1], (E, H), dtype=jnp.float32) * 0.02
        W1 = jax.random.normal(ks[2], (E, H, F), dtype=jnp.float32) * (1.0 / np.sqrt(H))
        b1 = jnp.zeros((E, F), dtype=jnp.float32)
        W2 = jax.random.normal(ks[3], (E, F, H), dtype=jnp.float32) * (1.0 / np.sqrt(F))
        b2 = jnp.zeros((E, H), dtype=jnp.float32)
        sW1 = jax.random.normal(ks[4], (H, F), dtype=jnp.float32) * (1.0 / np.sqrt(H))
        sb1 = jnp.zeros((F,), dtype=jnp.float32)
        sW2 = jax.random.normal(ks[5], (F, H), dtype=jnp.float32) * (1.0 / np.sqrt(F))
        sb2 = jnp.zeros((H,), dtype=jnp.float32)
        return {'x': x, 'gate_w': gate_w, 'W1': W1, 'b1': b1, 'W2': W2, 'b2': b2, 'sW1': sW1, 'sb1': sb1, 'sW2': sW2, 'sb2': sb2}
    _L0_ffn_in = _L0_ffn_setup()

    def _L1_attn_setup():
        import jax, jax.numpy as jnp
        import numpy as np
        import math
        H = 8
        D = 32
        DEPTH = 1
        LAMBDA_INIT = 0.8 - 0.6 * math.exp(-0.3 * DEPTH)
        EPS = 1e-08
        key = jax.random.key(seed)
        ks = jax.random.split(key, 9)
        B, T, IN_DIM, OUT_DIM = (2, 256, 128, 128)
        E = 2 * H * D
        inp = {'x': jax.random.normal(ks[0], (B, T, IN_DIM), dtype=jnp.float32), 'Wq': jax.random.normal(ks[1], (IN_DIM, E), dtype=jnp.float32) * IN_DIM ** (-0.5), 'Wkv': jax.random.normal(ks[2], (IN_DIM, 2 * E), dtype=jnp.float32) * IN_DIM ** (-0.5), 'Wout': jax.random.normal(ks[3], (E, OUT_DIM), dtype=jnp.float32) * E ** (-0.5), 'lambda_q1': 0.1 * jax.random.normal(ks[4], (D,), dtype=jnp.float32), 'lambda_k1': 0.1 * jax.random.normal(ks[5], (D,), dtype=jnp.float32), 'lambda_q2': 0.1 * jax.random.normal(ks[6], (D,), dtype=jnp.float32), 'lambda_k2': 0.1 * jax.random.normal(ks[7], (D,), dtype=jnp.float32), 'gamma': jnp.ones((2 * D,), dtype=jnp.float32)}
        return inp
    _L1_attn_in = _L1_attn_setup()

    def _L1_ffn_setup():
        import jax, jax.numpy as jnp
        import numpy as np
        B, T, C = (4, 256, 128)
        H = 128
        E_ATT = 8
        E_MOE = 8
        I = 128
        MIN_ATT = 2
        MIN_MOE = 2
        EPS_LN = 1e-05

        def _normalize(x, axis):
            n = jnp.linalg.norm(x, axis=axis, keepdims=True)
            return x / jnp.maximum(n, 1e-12)

        def _layernorm(x, w, b):
            m = jnp.mean(x, axis=-1, keepdims=True)
            v = jnp.mean(jnp.square(x - m), axis=-1, keepdims=True)
            return (x - m) / jnp.sqrt(v + EPS_LN) * w + b

        def _gating(flat_hs, sim, gates, min_experts):
            logits = _normalize(flat_hs, -1) @ _normalize(sim, 0) - jax.nn.sigmoid(gates)
            gated = jax.nn.relu(logits)
            mask = (gated > 0).astype(gated.dtype)
            inactive = jnp.sum(mask, axis=1) == 0
            _, idx = jax.lax.top_k(logits, min_experts)
            onehot = jnp.sum(jax.nn.one_hot(idx, logits.shape[-1], dtype=gated.dtype), axis=1)
            put = inactive[:, None] & (onehot > 0)
            mask = jnp.where(put, 1.0, mask)
            masked = jnp.where(mask > 0, gated, -jnp.inf)
            return jax.nn.softmax(masked, axis=-1)
        key = jax.random.key(seed)
        ks = jax.random.split(key, 12)
        d = {}
        d['x'] = jax.random.normal(ks[0], (B, T, C), dtype=jnp.float32)
        d['ln1_w'] = jnp.ones((C,), jnp.float32)
        d['ln1_b'] = jnp.zeros((C,), jnp.float32)
        d['ln2_w'] = jnp.ones((C,), jnp.float32)
        d['ln2_b'] = jnp.zeros((C,), jnp.float32)
        d['smha_sim'] = jax.random.normal(ks[1], (C, E_ATT), dtype=jnp.float32)
        d['smha_gates'] = jnp.zeros((E_ATT,), jnp.float32)
        sq = 1.0 / np.sqrt(C + H)
        d['q_proj'] = jax.random.normal(ks[2], (E_ATT, C, H), dtype=jnp.float32) * sq
        d['k_proj'] = jax.random.normal(ks[3], (E_ATT, C, H), dtype=jnp.float32) * sq
        d['v_proj'] = jax.random.normal(ks[4], (E_ATT, C, H), dtype=jnp.float32) * sq
        d['o_proj'] = jax.random.normal(ks[5], (E_ATT, H, C), dtype=jnp.float32) * sq
        d['moe_sim'] = jax.random.normal(ks[6], (C, E_MOE), dtype=jnp.float32)
        d['moe_gates'] = jnp.zeros((E_MOE,), jnp.float32)
        d['w1'] = jax.random.normal(ks[7], (E_MOE, C, I), dtype=jnp.float32) * (1.0 / np.sqrt(C))
        d['w2'] = jax.random.normal(ks[8], (E_MOE, I, C), dtype=jnp.float32) * (1.0 / np.sqrt(I))
        return d
    _L1_ffn_in = _L1_ffn_setup()
    _d = {'L0_attn_x': _L0_attn_in['x'], 'L0_attn_W_in': _L0_attn_in['W_in'], 'L0_attn_conv_w': _L0_attn_in['conv_w'], 'L0_attn_conv_b': _L0_attn_in['conv_b'], 'L0_attn_W_xproj': _L0_attn_in['W_xproj'], 'L0_attn_W_dt': _L0_attn_in['W_dt'], 'L0_attn_b_dt': _L0_attn_in['b_dt'], 'L0_attn_A_log': _L0_attn_in['A_log'], 'L0_attn_D': _L0_attn_in['D'], 'L0_attn_W_out': _L0_attn_in['W_out'], 'L0_ffn_gate_w': _L0_ffn_in['gate_w'], 'L0_ffn_W1': _L0_ffn_in['W1'], 'L0_ffn_b1': _L0_ffn_in['b1'], 'L0_ffn_W2': _L0_ffn_in['W2'], 'L0_ffn_b2': _L0_ffn_in['b2'], 'L0_ffn_sW1': _L0_ffn_in['sW1'], 'L0_ffn_sb1': _L0_ffn_in['sb1'], 'L0_ffn_sW2': _L0_ffn_in['sW2'], 'L0_ffn_sb2': _L0_ffn_in['sb2'], 'L1_attn_Wq': _L1_attn_in['Wq'], 'L1_attn_Wkv': _L1_attn_in['Wkv'], 'L1_attn_Wout': _L1_attn_in['Wout'], 'L1_attn_lambda_q1': _L1_attn_in['lambda_q1'], 'L1_attn_lambda_k1': _L1_attn_in['lambda_k1'], 'L1_attn_lambda_q2': _L1_attn_in['lambda_q2'], 'L1_attn_lambda_k2': _L1_attn_in['lambda_k2'], 'L1_attn_gamma': _L1_attn_in['gamma'], 'L1_ffn_ln1_w': _L1_ffn_in['ln1_w'], 'L1_ffn_ln1_b': _L1_ffn_in['ln1_b'], 'L1_ffn_ln2_w': _L1_ffn_in['ln2_w'], 'L1_ffn_ln2_b': _L1_ffn_in['ln2_b'], 'L1_ffn_smha_sim': _L1_ffn_in['smha_sim'], 'L1_ffn_smha_gates': _L1_ffn_in['smha_gates'], 'L1_ffn_q_proj': _L1_ffn_in['q_proj'], 'L1_ffn_k_proj': _L1_ffn_in['k_proj'], 'L1_ffn_v_proj': _L1_ffn_in['v_proj'], 'L1_ffn_o_proj': _L1_ffn_in['o_proj'], 'L1_ffn_moe_sim': _L1_ffn_in['moe_sim'], 'L1_ffn_moe_gates': _L1_ffn_in['moe_gates'], 'L1_ffn_w1': _L1_ffn_in['w1'], 'L1_ffn_w2': _L1_ffn_in['w2']}
    _x0 = _d['L0_attn_x']
    _d['L0_attn_x'] = jax.random.normal(jax.random.fold_in(jax.random.key(seed), 1), (4, 1024, 128), dtype=_x0.dtype)
    del _x0
    return _d

def reference(L0_attn_x, L0_attn_W_in, L0_attn_conv_w, L0_attn_conv_b, L0_attn_W_xproj, L0_attn_W_dt, L0_attn_b_dt, L0_attn_A_log, L0_attn_D, L0_attn_W_out, L0_ffn_gate_w, L0_ffn_W1, L0_ffn_b1, L0_ffn_W2, L0_ffn_b2, L0_ffn_sW1, L0_ffn_sb1, L0_ffn_sW2, L0_ffn_sb2, L1_attn_Wq, L1_attn_Wkv, L1_attn_Wout, L1_attn_lambda_q1, L1_attn_lambda_k1, L1_attn_lambda_q2, L1_attn_lambda_k2, L1_attn_gamma, L1_ffn_ln1_w, L1_ffn_ln1_b, L1_ffn_ln2_w, L1_ffn_ln2_b, L1_ffn_smha_sim, L1_ffn_smha_gates, L1_ffn_q_proj, L1_ffn_k_proj, L1_ffn_v_proj, L1_ffn_o_proj, L1_ffn_moe_sim, L1_ffn_moe_gates, L1_ffn_w1, L1_ffn_w2):

    def _L0_attn_ref(x, W_in, conv_w, conv_b, W_xproj, W_dt, b_dt, A_log, D, W_out):
        import jax, jax.numpy as jnp
        import numpy as np
        D_MODEL = 128
        EXPAND = 2
        D_EXPAND = D_MODEL * EXPAND
        D_STATE = 16
        DT_RANK = -(-D_MODEL // 16)
        BATCH = 4
        SEQ = 128

        def _mamba_forward(x, W_in, conv_w, conv_b, W_xproj, W_dt, b_dt, A_log, D, W_out):
            B, L, _ = x.shape
            d_exp = D.shape[0]
            n = A_log.shape[1]
            xz = x @ W_in.T
            u, z = jnp.split(xz, 2, axis=-1)
            uc = jax.lax.conv_general_dilated(u.transpose(0, 2, 1), conv_w, window_strides=(1,), padding=[(1, 1)], feature_group_count=d_exp, dimension_numbers=('NCH', 'OIH', 'NCH'))
            uc = jax.nn.silu(uc + conv_b[None, :, None]).transpose(0, 2, 1)
            proj = uc @ W_xproj.T
            B_ssm = proj[..., :n]
            C_ssm = proj[..., n:2 * n]
            dt = proj[..., 2 * n:]
            delta = jax.nn.softplus(dt @ W_dt.T + b_dt)
            A = -jnp.exp(A_log)

            def step(h, inp):
                u_t, d_t, b_t, c_t = inp
                dA = jnp.exp(d_t[:, :, None] * A)
                h = dA * h + (d_t * u_t)[:, :, None] * b_t[:, None, :]
                y_t = jnp.einsum('bdn,bn->bd', h, c_t)
                return (h, y_t)
            xs = (uc.transpose(1, 0, 2), delta.transpose(1, 0, 2), B_ssm.transpose(1, 0, 2), C_ssm.transpose(1, 0, 2))
            h0 = jnp.zeros((B, d_exp, n), dtype=uc.dtype)
            _, ys = jax.lax.scan(step, h0, xs)
            y = ys.transpose(1, 0, 2) + uc * D
            y = y * jax.nn.silu(z)
            return y @ W_out.T
        return _mamba_forward(x, W_in, conv_w, conv_b, W_xproj, W_dt, b_dt, A_log, D, W_out)

    def _L0_ffn_ref(x, gate_w, W1, b1, W2, b2, sW1, sb1, sW2, sb2):
        import jax, jax.numpy as jnp
        import numpy as np
        TOP_K = 2
        B, S, H = x.shape
        E = gate_w.shape[0]
        x_flat = x.reshape(-1, H)
        logits = x_flat @ gate_w.T
        probs = jax.nn.softmax(logits.astype(jnp.float32), axis=-1)
        top_w, sel = jax.lax.top_k(probs, TOP_K)
        top_w = top_w / jnp.sum(top_w, axis=-1, keepdims=True)
        combine = jnp.sum(jax.nn.one_hot(sel, E, dtype=top_w.dtype) * top_w[..., None], axis=1)
        combine = combine.astype(x.dtype)
        h = jax.nn.gelu(jnp.einsum('th,ehf->tef', x_flat, W1) + b1[None], approximate=False)
        y = jnp.einsum('tef,efh->teh', h, W2) + b2[None]
        out = jnp.einsum('teh,te->th', y, combine)
        sh = jax.nn.gelu(x_flat @ sW1 + sb1, approximate=False)
        out = out + sh @ sW2 + sb2
        return out.reshape(B, S, H)

    def _L1_attn_ref(x, Wq, Wkv, Wout, lambda_q1, lambda_k1, lambda_q2, lambda_k2, gamma):
        import jax, jax.numpy as jnp
        import numpy as np
        import math
        H = 8
        D = 32
        DEPTH = 1
        LAMBDA_INIT = 0.8 - 0.6 * math.exp(-0.3 * DEPTH)
        EPS = 1e-08
        B, T, _ = x.shape
        scaling = D ** (-0.5)
        q = (x @ Wq).reshape(B, T, 2 * H, D).transpose(0, 2, 1, 3) * scaling
        kv = x @ Wkv
        k, v = jnp.split(kv, 2, axis=-1)
        k = k.reshape(B, T, 2 * H, D).transpose(0, 2, 1, 3)
        v = v.reshape(B, T, H, 2 * D).transpose(0, 2, 1, 3)
        dots = jnp.einsum('bhqd,bhkd->bhqk', q, k)
        attn_w = jax.nn.softmax(dots.astype(jnp.float32), axis=-1).astype(dots.dtype)
        lam1 = jnp.exp(jnp.sum(lambda_q1 * lambda_k1))
        lam2 = jnp.exp(jnp.sum(lambda_q2 * lambda_k2))
        lam = lam1 - lam2 + LAMBDA_INIT
        attn_w = attn_w.reshape(B, H, 2, T, T)
        attn_w = attn_w[:, :, 0] - lam * attn_w[:, :, 1]
        attn = jnp.einsum('bhqk,bhkd->bhqd', attn_w, v)
        rms = jnp.sqrt(jnp.mean(attn * attn, axis=-1, keepdims=True))
        attn = gamma * (attn / (rms + EPS))
        attn = attn * (1.0 - LAMBDA_INIT)
        attn = attn.transpose(0, 2, 1, 3).reshape(B, T, 2 * H * D)
        return attn @ Wout

    def _L1_ffn_ref(x, ln1_w, ln1_b, ln2_w, ln2_b, smha_sim, smha_gates, q_proj, k_proj, v_proj, o_proj, moe_sim, moe_gates, w1, w2):
        import jax, jax.numpy as jnp
        import numpy as np
        B, T, C = (4, 256, 128)
        H = 128
        E_ATT = 8
        E_MOE = 8
        I = 128
        MIN_ATT = 2
        MIN_MOE = 2
        EPS_LN = 1e-05

        def _normalize(x, axis):
            n = jnp.linalg.norm(x, axis=axis, keepdims=True)
            return x / jnp.maximum(n, 1e-12)

        def _layernorm(x, w, b):
            m = jnp.mean(x, axis=-1, keepdims=True)
            v = jnp.mean(jnp.square(x - m), axis=-1, keepdims=True)
            return (x - m) / jnp.sqrt(v + EPS_LN) * w + b

        def _gating(flat_hs, sim, gates, min_experts):
            logits = _normalize(flat_hs, -1) @ _normalize(sim, 0) - jax.nn.sigmoid(gates)
            gated = jax.nn.relu(logits)
            mask = (gated > 0).astype(gated.dtype)
            inactive = jnp.sum(mask, axis=1) == 0
            _, idx = jax.lax.top_k(logits, min_experts)
            onehot = jnp.sum(jax.nn.one_hot(idx, logits.shape[-1], dtype=gated.dtype), axis=1)
            put = inactive[:, None] & (onehot > 0)
            mask = jnp.where(put, 1.0, mask)
            masked = jnp.where(mask > 0, gated, -jnp.inf)
            return jax.nn.softmax(masked, axis=-1)
        b, t, c = x.shape
        n1 = _layernorm(x, ln1_w, ln1_b)
        rw = _gating(n1.reshape(b * t, c), smha_sim, smha_gates, MIN_ATT).reshape(b, t, -1)
        q = jnp.einsum('btc,ech,bte->bth', n1, q_proj, rw)
        k = jnp.einsum('btc,ech,bte->bth', n1, k_proj, rw)
        v = jnp.einsum('btc,ech,bte->bth', n1, v_proj, rw)
        scale = 1.0 / jnp.sqrt(jnp.asarray(q.shape[-1], q.dtype))
        scores = jnp.einsum('bth,bsh->bts', q, k) * scale
        causal = jnp.tril(jnp.ones((t, t), dtype=bool))
        scores = jnp.where(causal, scores, -jnp.inf)
        attn = jnp.einsum('bts,bsh->bth', jax.nn.softmax(scores, axis=-1), v)
        attn_out = jnp.einsum('bth,ehc,bte->btc', attn, o_proj, rw)
        hs = x + attn_out
        n2 = _layernorm(hs, ln2_w, ln2_b)
        rw2 = _gating(n2.reshape(b * t, c), moe_sim, moe_gates, MIN_MOE).reshape(b, t, -1)
        inter = jax.nn.gelu(jnp.einsum('btc,eci->btei', n2, w1), approximate=False)
        moe_out = jnp.einsum('btei,eic,bte->btc', inter, w2, rw2)
        return hs + moe_out
    x = L0_attn_x
    x = x + _layernorm(_L0_attn_ref(_layernorm(x, axis=-1), L0_attn_W_in, L0_attn_conv_w, L0_attn_conv_b, L0_attn_W_xproj, L0_attn_W_dt, L0_attn_b_dt, L0_attn_A_log, L0_attn_D, L0_attn_W_out), axis=-1)
    x = x + _layernorm(_L0_ffn_ref(_layernorm(x, axis=-1), L0_ffn_gate_w, L0_ffn_W1, L0_ffn_b1, L0_ffn_W2, L0_ffn_b2, L0_ffn_sW1, L0_ffn_sb1, L0_ffn_sW2, L0_ffn_sb2), axis=-1)
    x = x + _layernorm(_L1_attn_ref(_layernorm(x, axis=-1), L1_attn_Wq, L1_attn_Wkv, L1_attn_Wout, L1_attn_lambda_q1, L1_attn_lambda_k1, L1_attn_lambda_q2, L1_attn_lambda_k2, L1_attn_gamma), axis=-1)
    x = x + _layernorm(_L1_ffn_ref(_layernorm(x, axis=-1), L1_ffn_ln1_w, L1_ffn_ln1_b, L1_ffn_ln2_w, L1_ffn_ln2_b, L1_ffn_smha_sim, L1_ffn_smha_gates, L1_ffn_q_proj, L1_ffn_k_proj, L1_ffn_v_proj, L1_ffn_o_proj, L1_ffn_moe_sim, L1_ffn_moe_gates, L1_ffn_w1, L1_ffn_w2), axis=-1)
    return x

_drawn_inputs = setup_inputs


def setup_inputs(seed=0):
    import zlib

    import numpy as np

    out = dict(_drawn_inputs(seed))
    spreads = {'L0_attn_D': (1.0, 0.2),
     'L0_ffn_b1': (0.0, 0.1),
     'L0_ffn_b2': (0.0, 0.1),
     'L0_ffn_sb1': (0.0, 0.1),
     'L0_ffn_sb2': (0.0, 0.1),
     'L1_attn_gamma': (1.0, 0.2),
     'L1_ffn_ln1_w': (1.0, 0.2),
     'L1_ffn_ln1_b': (0.0, 0.1),
     'L1_ffn_ln2_w': (1.0, 0.2),
     'L1_ffn_ln2_b': (0.0, 0.1),
     'L1_ffn_smha_gates': (0.0, 0.1),
     'L1_ffn_moe_gates': (0.0, 0.1)}
    factors = {'L0_attn_W_xproj': 8.0,
     'L0_attn_W_dt': 8.0,
     'L0_attn_b_dt': 8.0,
     'L0_attn_A_log': 8.0,
     'L1_attn_lambda_q2': 2.935,
     'L1_attn_lambda_k2': 2.866,
     'L1_ffn_q_proj': 4.929,
     'L1_ffn_k_proj': 4.777}
    for name, (base, spread) in spreads.items():
        noise = np.random.default_rng([zlib.crc32(name.encode()), seed]).standard_normal(out[name].shape)
        drawn = base * np.exp(spread * noise) if base else spread * noise
        out[name] = jnp.asarray(drawn.astype(out[name].dtype))
    for name, factor in factors.items():
        out[name] = (out[name] * factor).astype(out[name].dtype)
    return out
```

```python
import math
from contextlib import ExitStack

import numpy as np

import concourse.bass as bass
from concourse import mybir

F32 = mybir.dt.float32
F16 = mybir.dt.float16
BF16 = mybir.dt.bfloat16
U32 = mybir.dt.uint32
ALU = mybir.AluOpType
ACT = mybir.ActivationFunctionType
AX = mybir.AxisListType.X

NB, T, C = 4, 1024, 128
NT = T // 128
LAMBDA_INIT = 0.8 - 0.6 * math.exp(-0.3)

PARAMS = {
    "x": (NB * T, C), "winT": (128, 512), "convw": (128, 2, 3), "convb": (128, 2),
    "wx": (128, 2, 104), "wdt": (8, 256), "bdt": (128, 2), "alog": (128, 2, 16), "dcol": (128, 2),
    "woT": (128, 2, 128),
    "gwT": (128, 8), "w1": (128, 9, 512), "b1": (128, 9, 4), "w2": (128, 9, 4, 128), "b2": (9, 128),
    "wqk": (128, 1024), "wv": (128, 512), "wout": (128, 4, 128), "lam": (4, 32), "gam": (128, 1),
    "lnp": (4, 128), "sims": (128, 2, 8), "gates": (2, 8),
    "wqkv3": (128, 3, 8, 128), "wo3": (128, 8, 128), "w13": (128, 8, 128), "w23": (128, 8, 128),
    "ident": (128, 128), "iota8": (128, 8), "tri": (128, 128),
}


class Step:

    def __init__(self, queue, emit, after, sem=None):
        self.queue, self.emit, self.after, self.sem = queue, emit, after, sem
        self.awaited, self.count = False, 0


class Slot:

    def __init__(self, ap):
        self.ap, self.free = ap, []


class Ring:
    def __init__(self, aps):
        self.slots, self.n = [Slot(a) for a in aps], 0

    def take(self):
        s = self.slots[self.n % len(self.slots)]
        self.n += 1
        return s


def flat(xs):
    out = []
    for x in xs:
        if isinstance(x, (list, tuple)):
            out += flat(x)
        elif x is not None:
            out.append(x)
    return out


def program(nc, d, out, phases="MFAD"):
    ctx = ExitStack()
    with ctx:
        def sb(name, shape, dt=F32):
            return ctx.enter_context(nc.sbuf_tensor(name, shape, dt))[tuple(slice(None) for _ in shape)]

        def sem(name):
            return ctx.enter_context(nc.semaphore(name))

        ps = [ctx.enter_context(nc.psum_tensor(f"ps{i}", [128, 1024], F32)) for i in range(4)]
        bank = [Slot(ps[i // 2][:, 512 * (i % 2):512 * (i % 2) + 512]) for i in range(8)]

        queues = {q: [] for q in ("pe", "act", "dve", "pool", "sp")}
        own = {q: sem("s_" + q) for q in queues}

        def add(q, emit, *after, sem=None):
            s = Step(q, emit, flat(after), sem)
            for a in s.after:
                a.awaited = True
            queues[q].append(s)
            return s

        def mm(o, l, r, st, sp, *after):
            return add("pe", lambda e: e.matmul(o, l, r, start=st, stop=sp), *after)

        def tr(o, i, idn, *after):
            return add("pe", lambda e: e.transpose(o, i, idn), *after)

        def act(o, i, f, *after, bias=0.0, scale=1.0, acc=None):
            if f == ACT.Copy:
                return add("act", lambda e: e.activation(o, i, f, scale=scale), *after)
            return add("act", lambda e: e.activation(o, i, f, bias=bias, scale=scale, accum_out=acc), *after)

        def tt(o, a, b, op, *after, q="dve"):
            return add(q, lambda e: e.tensor_tensor(o, a, b, op), *after)

        def ts(o, a, s1, s2, op0, op1, *after, q="dve"):
            if op1 is None:
                return add(q, lambda e: e.tensor_scalar(o, a, s1, None, op0), *after)
            return add(q, lambda e: e.tensor_scalar(o, a, s1, s2, op0, op1), *after)

        def stt(o, a, s, b, op0, op1, *after):
            return add("dve", lambda e: e.scalar_tensor_tensor(out=o, in0=a, scalar=s, in1=b, op0=op0, op1=op1),
                       *after)

        def cp(o, a, *after, q="dve"):
            return add(q, lambda e: e.tensor_copy(o, a), *after)

        def red(o, a, op, *after, negate=False):
            return add("dve", lambda e: e.tensor_reduce(o, a, AX, op, negate=negate), *after)

        def recip(o, a, *after):
            return add("dve", lambda e: e.reciprocal(o, a), *after)

        def dma(o, i, s, *after, q="sp"):
            return add(q, lambda e: e.dma_start(o, i), *after, sem=s)

        def fill(o, v, *after, q="dve"):
            return add(q, lambda e: e.memset(o, v), *after)

        X = sb("X", [128, 32, 128])
        ident = sb("ident", [128, 128])
        iota8 = sb("iota8", [128, 8])
        tri = sb("tri", [128, 128])
        sel = sb("sel", [96, 32, 128], BF16)
        half = sb("half", [128, 3, 64])
        lnp = sb("lnp", [128, 4, 128])
        small = {}
        for k in ("convw", "convb", "wx", "bdt", "alog", "dcol", "gwT", "b1", "gam", "sims", "woT"):
            small[k] = sb(k, list(PARAMS[k]))
        wdt = sb("wdt", [104, 256])
        b2 = sb("b2", [9, 128])
        lam = sb("lam", [128, 4, 32])
        gts = sb("gts", [128, 2, 8])
        winT = sb("winT", [128, 512])
        BIG = sb("BIG", [128, 9216])
        WB = sb("WB", [128, 9216])

        s_x = [sem(f"s_x{b}") for b in range(NB)]
        s_c = sem("s_c")
        consts = []

        def load(dst, name, view=None):
            consts.append(dma(dst, d[name] if view is None else view, s_c))

        xin = d["x"].rearrange("(n p) c -> p n c", p=128)
        xload = [dma(X[:, 0:8, :], xin[:, 0:8, :], s_x[0])]
        load(ident[:, :], "ident")
        load(winT[:, :], "winT")
        for k in ("convw", "convb", "wx", "bdt", "alog", "dcol", "gwT", "b1", "gam", "sims", "woT"):
            ap = small[k]
            load(ap[tuple(slice(None) for _ in PARAMS[k])], k)
        load(wdt[96:104, :], "wdt")
        load(iota8[:, :], "iota8")
        load(tri[:, :], "tri")
        load(b2[:, :], "b2")
        for i in range(4):
            load(lnp[:, i, :], "lnp", d["lnp"][i:i + 1, :].partition_broadcast(128))
            load(lam[:, i, :], "lam", d["lam"][i:i + 1, :].partition_broadcast(128))
        for i in range(2):
            load(gts[:, i, :], "gates", d["gates"][i:i + 1, :].partition_broadcast(128))
        K = consts[-1]
        for b in range(1, NB):
            xload.append(dma(X[:, 8 * b:8 * b + 8, :], xin[:, 8 * b:8 * b + 8, :], s_x[b]))
        H0 = fill(half[:, 0, :], -0.5, q="pool")
        H1 = fill(half[:, 1, :], 0.5, q="pool")
        xtok = {b: [xload[b]] for b in range(NB)}

        st_ring = Ring([sb(f"st{i}", [128, 8, 10]) for i in range(4)])

        def layernorm(src, deps, dst, dst_free):
            n = len(src)
            s = st_ring.take()
            st, fr = s.ap, s.free
            a = [add("dve", (lambda j: lambda e: e.bn_stats(st[:, j, 0:6], src[j]))(j), deps[j], fr)
                 for j in range(n)]
            g = [add("dve", (lambda j: lambda e: e.bn_aggr(st[:, j, 6:8], st[:, j, 0:6]))(j), a[j])
                 for j in range(n)]
            e1 = ts(st[:, 0:n, 8:9], st[:, 0:n, 7:8], 1e-5, None, ALU.add, None, g[-1], q="pool")
            e2 = tt(st[:, 0:n, 9:10], st[:, 0:n, 8:9], half[:, 0, 0:n].rearrange("p (n o) -> p n o", o=1),
                    ALU.pow, e1, H0, q="pool")
            o = [ts(dst[j], src[j], st[:, j, 6:7], st[:, j, 9:10], ALU.subtract, ALU.mult, e2, dst_free)
                 for j in range(n)]
            s.free = [o[-1]]
            return o

        big = Ring([BIG[:, 1024 * i:1024 * i + 1024] for i in range(9)])
        ln_buf = Ring([sb(f"lnb{i}", [128, 8, 128]) for i in range(2)])
        xT_ring = Ring([sb(f"xT{i}", [128, 1024]) for i in range(2)])

        def transposes(src, deps, dstslot, banks, ev="act"):
            fr = dstslot.free
            toks = []
            n = len(src)
            for h in range((n + 3) // 4):
                bk = banks[h % len(banks)]
                m = min(4, n - 4 * h)
                t = [tr(bk.ap[:, 128 * j:128 * j + 128], src[4 * h + j], ident[:, :], deps[4 * h + j], K,
                        bk.free) for j in range(m)]
                o, i = dstslot.ap[:, 512 * h:512 * h + 128 * m], bk.ap[:, 0:128 * m]
                if ev == "act":
                    c = act(o, i, ACT.Copy, t[-1], fr)
                else:
                    c = cp(o, i, t[-1], fr)
                bk.free = [c]
                toks.append(c)
            return toks, t[-1]

        def tiles_of(b):
            return [X[:, 8 * b + j, :] for j in range(8)]

        def residual(src, deps, b, src_slots, q="dve"):
            s = ln_buf.take()
            o = layernorm(src, deps, [s.ap[:, j, :] for j in range(8)], s.free)
            for sl in src_slots:
                sl.free = [o[-1]]
            r = tt(X[:, 8 * b:8 * b + 8, :], X[:, 8 * b:8 * b + 8, :], s.ap[:, :, :], ALU.add, o[-1], xtok[b], q=q)
            s.free = [r]
            xtok[b] = [r]
            return r

        MA = sb("MA", [128, 5 * 2048 + 2052])
        zs, uc, dl, du, yy = [MA[:, 2048 * i:2048 * i + 2048].rearrange("p (c t) -> p c t", c=2) for i in range(5)]
        up = MA[:, 10240:12292].rearrange("p (c t) -> p c t", c=2)
        aneg = sb("aneg", [128, 32])
        bc = sb("bc", [96, 3, 1024], BF16)
        mfree = {k: [] for k in ("up", "zs", "uc", "dl", "du", "yy", "bc")}

        pad = [fill(up[:, c, k:k + 1], 0.0, q="pool") for c in range(2) for k in (0, 1025)][-1]
        a1 = act(aneg[:, :], small["alog"][:, :, :].rearrange("p c n -> p (c n)"), ACT.Exp, K)
        A_OK = ts(aneg[:, :], aneg[:, :], -1.0, None, ALU.mult, None, a1)

        S_OK = []
        for k in range(3):
            o, i = sel[32 * k:32 * k + 32, :, :], ident[32 * k:32 * k + 32, 32 * k:32 * k + 32].rearrange(
                "p (n o) -> p n o", o=1).to_broadcast([32, 32, 128])
            S_OK.append(cp(o, i, K) if k == 2 else act(o, i, ACT.Copy, K))

        def mamba(b):
            B = bank[0:4]
            s = ln_buf.take()
            o = layernorm(tiles_of(b), [xtok[b]] * 8, [s.ap[:, j, :] for j in range(8)], s.free)
            xs = xT_ring.take()
            xt, last = transposes([s.ap[:, j, :] for j in range(8)], o, xs, B[0:2])
            s.free = [last]
            yield
            zt, ut = [], []
            k = 0
            for c in (2, 3, 0, 1):
                for h in range(2):
                    bk = B[k % 4]
                    k += 1
                    m = mm(bk.ap, winT[:, 128 * c:128 * c + 128], xs.ap[:, 512 * h:512 * h + 512], True, True,
                           xt[h], bk.free, K)
                    if c < 2:
                        t = act(up[:, c, 1 + 512 * h:513 + 512 * h], bk.ap, ACT.Copy, m, mfree["up"])
                        ut.append(t)
                    else:
                        t = act(zs[:, c - 2, 512 * h:512 * h + 512], bk.ap, ACT.Silu, m, mfree["zs"])
                        zt.append(t)
                    bk.free = [t]
                xs.free = [m]
            yield
            cw, cb = small["convw"], small["convb"]
            cv = [big.take() for _ in range(2)]
            t = [ts(cv[c].ap, up[:, c, 0:1024], cw[:, c, 0:1], cb[:, c:c + 1], ALU.mult, ALU.add,
                    ut[2 * c + 1], pad, cv[c].free) for c in range(2)]
            t = [stt(cv[c].ap, up[:, c, 1:1025], cw[:, c, 1:2], cv[c].ap, ALU.mult, ALU.add, t[c])
                 for c in range(2)]
            t = [stt(cv[c].ap, up[:, c, 2:1026], cw[:, c, 2:3], cv[c].ap, ALU.mult, ALU.add, t[c])
                 for c in range(2)]
            mfree["up"] = [t[1]]
            u = [act(uc[:, c, :], cv[c].ap, ACT.Silu, t[c], mfree["uc"]) for c in range(2)]
            for c in range(2):
                cv[c].free = [u[c]]
            yield
            p0 = ps[0]
            for h in range(2):
                for c in range(2):
                    m = mm(p0[0:104, 512 * h:512 * h + 512], small["wx"][:, c, :], uc[:, c, 512 * h:512 * h + 512],
                           c == 0, c == 1, u[c], B[0].free, B[1].free)
            r1 = big.take()
            rr = r1.ap[0:96, :]
            hi = cp(bc[:, 1, :], p0[0:96, :], m, mfree["bc"])
            dtb = big.take()
            dt = act(dtb.ap[96:104, :], p0[96:104, :], ACT.Copy, m, dtb.free)
            x1 = tt(rr, p0[0:96, :], bc[:, 1, :], ALU.subtract, hi, r1.free)
            B[0].free = B[1].free = [x1, dt]
            mid = cp(bc[:, 2, :], rr, x1)
            lo = tt(bc[:, 0, :], rr, bc[:, 2, :], ALU.subtract, mid)
            r1.free = [lo]
            f1 = cp(bc[32:64, 0, :], bc[32:64, 2, :], lo)
            bcok = [cp(bc[0:32, 0, :], bc[0:32, 1, :], f1)]
            dts = []
            vs, es = [], []
            for c in range(2):
                pp = ps[1 - c]
                bb = B[2 - 2 * c:4 - 2 * c]
                for h in range(2):
                    m = mm(pp[:, 512 * h:512 * h + 512], wdt[96:104, 128 * c:128 * c + 128],
                           dtb.ap[96:104, 512 * h:512 * h + 512], True, True, dt, bb[0].free, bb[1].free)
                v, e = big.take(), big.take()
                bd = small["bdt"][:, c:c + 1]
                t1 = act(v.ap, pp[:, :], ACT.Identity, m, v.free, bias=bd)
                t2 = act(e.ap, pp[:, :], ACT.Abs, m, e.free, bias=bd)
                bb[0].free = bb[1].free = [t2]
                vs.append((v, t1))
                es.append((e, t2))
            dtb.free = [m]
            yield
            es = [(e, act(e.ap, e.ap, ACT.Exp, t, scale=-1.0)) for e, t in es]
            us = [big.take() for _ in range(2)]
            ls = [big.take() for _ in range(2)]
            u1 = [ts(us[c].ap, es[c][0].ap, 1.0, None, ALU.add, None, es[c][1], us[c].free) for c in range(2)]
            ll = [act(ls[c].ap, us[c].ap, ACT.Ln, u1[c], ls[c].free) for c in range(2)]
            t = [stt(us[c].ap, us[c].ap, -1.0, es[c][0].ap, ALU.add, ALU.subtract, u1[c], ll[c])
                 for c in range(2)]
            for c in range(2):
                es[c][0].free = [t[c]]
            t = [tt(us[c].ap, ls[c].ap, us[c].ap, ALU.subtract, t[c]) for c in range(2)]
            for c in range(2):
                ls[c].free = [t[c]]
            dd = [stt(dl[:, c, :], vs[c][0].ap, 0.0, us[c].ap, ALU.max, ALU.add, t[c], vs[c][1], mfree["dl"])
                  for c in range(2)]
            for c in range(2):
                vs[c][0].free = us[c].free = [dd[c]]
            dus = [tt(du[:, c, :], dl[:, c, :], uc[:, c, :], ALU.mult, dd[c]) for c in range(2)]
            yield
            yt = [None, None]
            for n in range(16):
                for h in range(2):
                    mb = mm(ps[0][:, 512 * h:512 * h + 512], sel[:, n, :], bc[:, 0, 512 * h:512 * h + 512],
                            True, True, bcok, S_OK, B[0].free, B[1].free)
                for h in range(2):
                    mc = mm(ps[1][:, 512 * h:512 * h + 512], sel[:, 16 + n, :], bc[:, 0, 512 * h:512 * h + 512],
                            True, True, B[2].free, B[3].free)
                da, db, hc = [big.take() for _ in range(2)], [big.take() for _ in range(2)], []
                ta = [act(da[c].ap, dl[:, c, :], ACT.Exp, dd[c], da[c].free, A_OK,
                          scale=aneg[:, 16 * c + n:16 * c + n + 1]) for c in range(2)]
                tb = [tt(db[c].ap, du[:, c, :], ps[0][:, :], ALU.mult, mb, dus[c], db[c].free) for c in range(2)]
                B[0].free = B[1].free = [tb[1]]

                def scan(c):
                    o, a0 = db[c].ap, da[c].ap
                    return add("dve", lambda e: e.tensor_tensor_scan(o, a0, o, 0.0, ALU.mult, ALU.add),
                               ta[c], tb[c])
                sc = [scan(c) for c in range(2)]
                for c in range(2):
                    da[c].free = [sc[c]]
                if n == 0:
                    th = [tt(yy[:, c, :], db[c].ap, ps[1][:, :], ALU.mult, mc, sc[c], mfree["yy"])
                          for c in range(2)]
                    yt = th
                    for c in range(2):
                        db[c].free = [th[c]]
                else:
                    th = [tt(db[c].ap, db[c].ap, ps[1][:, :], ALU.mult, mc, sc[c]) for c in range(2)]
                    yt = [tt(yy[:, c, :], yy[:, c, :], db[c].ap, ALU.add, th[c], yt[c], q="pool")
                          for c in range(2)]
                    for c in range(2):
                        db[c].free = [yt[c]]
                B[2].free = B[3].free = [th[1]]
                yield
            mfree["bc"], mfree["dl"], mfree["du"] = [mc], [ta[1]], [tb[1]]
            t = [stt(yy[:, c, :], uc[:, c, :], small["dcol"][:, c:c + 1], yy[:, c, :], ALU.mult, ALU.add, yt[c])
                 for c in range(2)]
            mfree["uc"] = [t[1]]
            t = [tt(yy[:, c, :], yy[:, c, :], zs[:, c, :], ALU.mult, t[c], zt) for c in range(2)]
            mfree["zs"] = [t[1]]
            deps = []
            for j in range(8):
                for c in range(2):
                    m = mm(ps[0][:, 128 * j:128 * j + 128], yy[:, c, 128 * j:128 * j + 128],
                           small["woT"][:, c, :], c == 0, c == 1, t[c], B[0].free, B[1].free)
                deps.append(m)
            mfree["yy"] = [m]
            residual([ps[0][:, 128 * j:128 * j + 128] for j in range(8)], [deps[3]] * 4 + [deps[7]] * 4, b, B[0:2])
            yield

        w1 = WB[:, 0:4608].rearrange("p (e f) -> p e f", e=9)
        w2 = WB[:, 4608:9216].rearrange("p (e f h) -> p e f h", e=9, f=4)
        hr = Ring([sb(f"hr{i}", [128, 512]) for i in range(8)])
        acc_r = Ring([sb(f"acc{i}", [128, 8, 128]) for i in range(1)])
        gbuf = Ring([sb(f"g{i}", [128, 8, 64]) for i in range(1)])
        gidx = Ring([sb(f"gi{i}", [128, 8, 8], U32) for i in range(1)])
        combT = sb("combT", [9, 1024])
        cfree = []

        def top2(lg, deps, out0, out1, mx, g8, free):
            gi = gidx.take()
            lt = []
            a = [add("dve", (lambda j: lambda e: e.max(mx[:, j, :], lg[:, j, :]))(j), deps, free)
                 for j in range(8)]
            lt = [add("dve", (lambda j: lambda e: e.max_index(gi.ap[:, j, :], mx[:, j, :], lg[:, j, :]))(j),
                      a[j], gi.free) for j in range(8)]
            f = cp(g8, gi.ap[:, :, :], lt)
            gi.free = [f]
            io = iota8[:, :].rearrange("p (o e) -> p o e", o=1).to_broadcast([128, 8, 8])
            r0 = tt(out0, io, g8[:, :, 0:1].to_broadcast([128, 8, 8]), ALU.is_equal, f, K)
            r1 = tt(out1, io, g8[:, :, 1:2].to_broadcast([128, 8, 8]), ALU.is_equal, f)
            return r0, r1, a

        def moe(b):
            MB, YB = bank[4:6], bank[6:8]
            s = ln_buf.take()
            o = layernorm(tiles_of(b), [xtok[b]] * 8, [s.ap[:, j, :] for j in range(8)], s.free)
            xs = xT_ring.take()
            xt, last = transposes([s.ap[:, j, :] for j in range(8)], o, xs, MB)
            s.free = [last]
            bk = YB[0]
            for j in range(8):
                m = mm(bk.ap[:, 8 * j:8 * j + 8], xs.ap[:, 128 * j:128 * j + 128], small["gwT"][:, :], True, True,
                       xt, bk.free)
            gs = gbuf.take()
            g = gs.ap
            G = lambda i: g[:, :, 8 * i:8 * i + 8]
            lg = cp(G(0), bk.ap[:, 0:64].rearrange("p (j e) -> p j e", e=8), m, gs.free)
            bk.free = [lg]
            t0, t1, a = top2(G(0), lg, G(2), G(3), G(1), G(4), gs.free)
            r = tt(G(5)[:, :, 0:1], G(1)[:, :, 1:2], G(1)[:, :, 0:1], ALU.subtract, a)
            r = act(G(5)[:, :, 1:2], G(5)[:, :, 0:1], ACT.Exp, r)
            r1 = ts(G(5)[:, :, 2:3], G(5)[:, :, 1:2], 1.0, None, ALU.add, None, r)
            r2 = recip(G(5)[:, :, 3:4], G(5)[:, :, 2:3], r1)
            r3 = tt(G(5)[:, :, 4:5], G(5)[:, :, 3:4], G(5)[:, :, 1:2], ALU.mult, r2)
            c1 = tt(G(2), G(2), G(5)[:, :, 3:4].to_broadcast([128, 8, 8]), ALU.mult, r2, t0)
            c2 = tt(G(3), G(3), G(5)[:, :, 4:5].to_broadcast([128, 8, 8]), ALU.mult, r3, t1)
            c3 = tt(G(6), G(2), G(3), ALU.add, c1, c2)
            c4 = fill(G(7), 1.0, gs.free)
            comb = g[:, :, 48:57]
            for h in range(2):
                bk = YB[h]
                for j in range(4):
                    m = tr(bk.ap[0:9, 128 * j:128 * j + 128], comb[:, 4 * h + j, :], ident[:, :], c3, c4, bk.free)
                ct = act(combT[:, 512 * h:512 * h + 512], bk.ap[0:9, :], ACT.Copy, m, cfree)
                bk.free = [ct]
            yield
            ac = acc_r.take()
            accs = [None] * 8
            pend = None
            plan = [(h, e) for h in range(2) for e in (8, 0, 1, 2, 3, 4, 5, 6, 7)]
            nm = [0]

            def down(h, e, hs):
                bk = YB[down.k % 2]
                down.k += 1
                for j in range(4):
                    o = bk.ap[:, 128 * j:128 * j + 128]
                    if e == 8:
                        mm(o, combT[:, 512 * h + 128 * j:512 * h + 128 * j + 128], b2[:, :], True, False, ct,
                           bk.free)
                    for f in range(4):
                        m = mm(o, hs[f][0].ap[:, 128 * j:128 * j + 128], w2[:, e, f, :], f == 0 and e != 8, f == 3,
                               hs[f][1], bk.free)
                for f in range(4):
                    hs[f][0].free = [m]
                if e == 8:
                    t = act(ac.ap[:, 4 * h:4 * h + 4, :], bk.ap.rearrange("p (j c) -> p j c", c=128), ACT.Copy,
                            m, ac.free)
                    for j in range(4):
                        accs[4 * h + j] = t
                else:
                    for j in range(4):
                        J = 4 * h + j
                        t = accs[J] = stt(ac.ap[:, J, :], bk.ap[:, 128 * j:128 * j + 128],
                                          G(6)[:, J, e:e + 1], ac.ap[:, J, :], ALU.mult, ALU.add, m, accs[J], c3)
                bk.free = [t]
                return m
            down.k = 0
            for h, e in plan:
                hs = []
                for f in range(4):
                    bk = MB[nm[0] % 2]
                    nm[0] += 1
                    m = mm(bk.ap, w1[:, e, 128 * f:128 * f + 128], xs.ap[:, 512 * h:512 * h + 512], True, True,
                           xt[h], bk.free, W_F)
                    hb = hr.take()
                    t = act(hb.ap, bk.ap, ACT.Gelu, m, hb.free, bias=small["b1"][:, e, f:f + 1])
                    bk.free = [t]
                    hs.append((hb, t))
                if pend:
                    md = down(*pend)
                pend = (h, e, hs)
                yield
            xs.free = [m]
            md = down(*pend)
            cfree[:] = [md]
            s = residual([ac.ap[:, j, :] for j in range(8)], accs, b, [ac])
            gs.free = [accs[-1]]
            wfree.append(md)
            yield

        WA = {}
        wqk = WB[:, 0:1024]
        wv = WB[:, 1024:1536]
        wout = WB[:, 1536:2048].rearrange("p (c n) -> p c n", c=4)
        lsc = sb("lsc", [128, 8])

        def attention_setup():
            j1 = tt(BIG[:, 0:32], lam[:, 0, :], lam[:, 1, :], ALU.mult, K, [s.free for s in big.slots])
            j2 = tt(BIG[:, 32:64], lam[:, 2, :], lam[:, 3, :], ALU.mult)
            r1 = red(lsc[:, 0:1], BIG[:, 0:32], ALU.add, j1)
            r2 = red(lsc[:, 1:2], BIG[:, 32:64], ALU.add, j2)
            x = act(lsc[:, 2:4], lsc[:, 0:2], ACT.Exp, r1, r2)
            y = tt(lsc[:, 4:5], lsc[:, 3:4], lsc[:, 2:3], ALU.subtract, x)
            z = ts(lsc[:, 5:6], lsc[:, 4:5], -LAMBDA_INIT, None, ALU.add, None, y)
            w = ts(wout, wout, small["gam"][:, 0:1], 1.0 - LAMBDA_INIT, ALU.mult, ALU.mult, WA["w"])
            WA["lam"], WA["wout"] = z, w
            WA["free"] = [r1, r2]

        def attention(b):
            A = WA
            pr = bank[7]
            s = ln_buf.take()
            o = layernorm(tiles_of(b), [xtok[b]] * 8, [s.ap[:, j, :] for j in range(8)], s.free)
            xs = xT_ring.take()
            xt, last = transposes([s.ap[:, j, :] for j in range(8)], o, xs, [bank[6], bank[7]])
            s.free = [last]
            V = A["V"]
            vt = []
            for j in range(8):
                bk = bank[6 + j % 2]
                m = mm(bk.ap, xs.ap[:, 128 * j:128 * j + 128], wv, True, True, xt, bk.free, A["w"])
                t = act(V.ap[:, j, :], bk.ap, ACT.Copy, m, V.free)
                bk.free = [t]
                vt.append(t)
            yield

            def project(g):
                st = A["stack"].take()
                toks = []
                for w in range(2):
                    hl = A["hl"].take()
                    hi, lo = hl.ap[:, 0, :], hl.ap[:, 1, :]
                    tl = []
                    sc = 32 ** -0.5 if w == 0 else 1.0
                    for h in range(2):
                        bk = bank[7]
                        m = mm(bk.ap, wqk[:, 512 * w + 128 * g:512 * w + 128 * g + 128],
                               xs.ap[:, 512 * h:512 * h + 512], True, True, xt[h], bk.free, A["w"])
                        t1 = act(hi[:, 512 * h:512 * h + 512], bk.ap, ACT.Copy, m, hl.free, scale=sc)
                        t2 = stt(lo[:, 512 * h:512 * h + 512], bk.ap, sc, hi[:, 512 * h:512 * h + 512], ALU.mult,
                                 ALU.subtract, t1)
                        bk.free = [t2]
                        tl += [t1, t2]
                    dm = []
                    for hh in range(4):
                        for r in range(3):
                            part = lo if r == 2 - w else hi
                            dm.append(dma(st.ap[32 * r:32 * r + 32, w, hh, :], part[32 * hh:32 * hh + 32, :],
                                          A["dsem"][st.k][w], tl, st.free))
                    hl.free = [dm[-1]]
                    toks += [dm[-1]]
                return st, toks, m

            stk = project(0)
            yield
            OB = A["O"]
            ot = {}
            for g in range(4):
                st, dm, m = stk
                for i in range(8):
                    if i == 2 and g < 3:
                        stk = project(g + 1)
                    for pp in range(2):
                        P, tP, tL = [], [], []
                        lb = A["l"].take()
                        L = lb.ap
                        for s_ in range(2):
                            hh = 2 * pp + s_
                            Sp = ps[s_]
                            b0, b1 = bank[2 * s_], bank[2 * s_ + 1]
                            for h in range(2):
                                m = mm(Sp[:, 512 * h:512 * h + 512], st.ap[0:96, 0, hh, 128 * i:128 * i + 128],
                                       st.ap[0:96, 1, hh, 512 * h:512 * h + 512], True, True, dm, b0.free, b1.free)
                            mx = red(L[:, s_:s_ + 1], Sp[:, :], ALU.max, m, lb.free, negate=True)
                            pb = A["P"].take()
                            t = act(pb.ap, Sp[:, :], ACT.Exp, mx, pb.free, bias=L[:, s_:s_ + 1],
                                    acc=L[:, 2 + s_:3 + s_])
                            b0.free = b1.free = [t]
                            P.append(pb)
                            tP.append(t)
                        A["later"].append((b, g, i, pp, P, tP, lb, st, m))
                        if len(A["later"]) > 1:
                            combine(*A["later"].pop(0), V, vt, OB, ot)
                        yield
                st.free = [m]
            while A["later"]:
                combine(*A["later"].pop(0), V, vt, OB, ot)
            xs.free = [stk[2]]
            V.free = [ot["last_mm"]]
            o = OB.ap
            ov = o.rearrange("p i (h d) -> p (i h) d", d=64)
            rb = A["rb"]
            tl = []
            for i in range(8):
                sq = big_sq.take()
                t = tt(sq.ap, o[:, i, :], o[:, i, :], ALU.mult, ot[i], sq.free, q="pool")
                t = red(rb[:, 0, 8 * i:8 * i + 8], sq.ap.rearrange("p (h d) -> p h d", d=64), ALU.add, t, A["rbf"])
                sq.free = [t]
            t = ts(rb[:, 1, :], rb[:, 0, :], 1.0 / 64, None, ALU.mult, None, t, q="pool")
            t = tt(rb[:, 2, :], rb[:, 1, :], half[:, 1, :], ALU.pow, t, H1, q="pool")
            t = ts(rb[:, 3, :], rb[:, 2, :], 1e-8, None, ALU.add, None, t)
            t = recip(rb[:, 4, :], rb[:, 3, :], t)
            deps = []
            for i in range(8):
                n = tt(o[:, i, :].rearrange("p (h d) -> p h d", d=64), o[:, i, :].rearrange("p (h d) -> p h d", d=64),
                       rb[:, 4, 8 * i:8 * i + 8].rearrange("p (h o) -> p h o", o=1).to_broadcast([128, 8, 64]),
                       ALU.mult, t)
                os = A["oT"].take()
                tk, last = transposes([o[:, i, 128 * c:128 * c + 128] for c in range(4)], [n] * 4, os,
                                      [bank[6 + i % 2]])
                Y = ps[2][:, 128 * i:128 * i + 128]
                for c in range(4):
                    m = mm(Y, os.ap[:, 128 * c:128 * c + 128], wout[:, c, :], c == 0, c == 3, tk, A["wout"],
                           bank[4].free, bank[5].free)
                os.free = [m]
                deps.append(m)
            A["rbf"] = [n]
            OB.free = [last]
            wfree.append(m)
            residual([ps[2][:, 128 * j:128 * j + 128] for j in range(8)], [deps[3]] * 4 + [deps[7]] * 4, b, [bank[4], bank[5]])
            yield

        def combine(b, g, i, pp, P, tP, lb, st, m, V, vt, OB, ot):
            L = lb.ap
            r = recip(L[:, 4:5], L[:, 3:4], tP[1])
            c = ts(L[:, 5:6], L[:, 2:3], L[:, 4:5], lsc[:, 5:6], ALU.mult, ALU.mult, r, tP[0], WA["lam"])
            r1 = recip(L[:, 6:7], L[:, 2:3], tP[0])
            D = P[0].ap
            t = stt(D, P[1].ap, L[:, 5:6], P[0].ap, ALU.mult, ALU.add, c, tP)
            P[1].free = [t]
            dt_ = WA["DT"].take()
            tk = []
            for h in range(2):
                bk = bank[4 + h]
                for j in range(4):
                    k = 4 * h + j
                    x = tr(bk.ap[:, 128 * j:128 * j + 128], D[:, 128 * k:128 * k + 128], ident[:, :], t, bk.free)
                e = act(dt_.ap[:, 512 * h:512 * h + 512], bk.ap, ACT.Copy, x, dt_.free)
                bk.free = [e]
                tk.append(e)
            P[0].free = [x]
            ob = bank[6]
            hp = 2 * g + pp
            for k in range(8):
                y = mm(ob.ap[:, 0:64], dt_.ap[:, 128 * k:128 * k + 128], V.ap[:, k, 64 * hp:64 * hp + 64], k == 0,
                       k == 7, tk[k // 4], vt, ob.free)
            dt_.free = [y]
            z = ts(OB.ap[:, i, 64 * hp:64 * hp + 64], ob.ap[:, 0:64], L[:, 6:7], None, ALU.mult, None, y, r1,
                   OB.free)
            ob.free = [z]
            lb.free = [z]
            ot[i] = z
            ot["last_mm"] = y

        wqkv3 = WB[:, 0:3072].rearrange("p (a e h) -> p a e h", a=3, e=8)
        wo3 = WB[:, 3072:4096].rearrange("p (e h) -> p e h", e=8)
        w13 = WB[:, 4096:5120].rearrange("p (e h) -> p e h", e=8)
        w23 = WB[:, 5120:6144].rearrange("p (e h) -> p e h", e=8)
        simn = sb("simn", [128, 2, 8])
        sgm = sb("sgm", [128, 2, 8])
        ones = sb("ones", [128, 128])
        WD = {}
        ones_t = fill(ones[:, :], 1.0)

        def experts_setup():
            sq = tt(lsq[:, 0:16], small["sims"][:, :, :].rearrange("p a e -> p (a e)"),
                    small["sims"][:, :, :].rearrange("p a e -> p (a e)"), ALU.mult, K)
            m = mm(bank[0].ap[:, 0:16], ones[:, :], lsq[:, 0:16], True, True, sq, ones_t, bank[0].free)
            a = act(lsq[:, 16:32], bank[0].ap[:, 0:16], ACT.Copy, m)
            bank[0].free = [a]
            p = tt(lsq[:, 32:48], lsq[:, 16:32], half[:, 1, 0:16], ALU.pow, a, H1, q="pool")
            q_ = ts(lsq[:, 48:64], lsq[:, 32:48], 1e-12, None, ALU.max, None, p)
            r = recip(lsq[:, 32:48], lsq[:, 48:64], q_)
            WD["sim"] = tt(simn[:, :, :].rearrange("p a e -> p (a e)"),
                           small["sims"][:, :, :].rearrange("p a e -> p (a e)"), lsq[:, 32:48], ALU.mult, r)
            e1 = act(sgm[:, :, :].rearrange("p a e -> p (a e)"), gts[:, :, :].rearrange("p a e -> p (a e)"), ACT.Exp,
                     K, scale=-1.0)
            e2 = ts(sgm[:, :, :], sgm[:, :, :], 1.0, None, ALU.add, None, e1)
            WD["sgm"] = recip(sgm[:, :, :], sgm[:, :, :], e2)

        lsq = sb("lsq", [128, 64])

        def affine_ln(src, deps, w, dst, free):
            o = layernorm(src, deps, [dst[:, j, :] for j in range(8)], free)
            wb = lnp[:, w:w + 1, :].to_broadcast([128, 8, 128])
            bb = lnp[:, w + 1:w + 2, :].to_broadcast([128, 8, 128])
            t = tt(dst, dst, wb, ALU.mult, o, K)
            return tt(dst, dst, bb, ALU.add, t)

        def gating(n1, dep, n1T, dT, which, bk, gs, scratch):
            g = gs.ap
            G = lambda i: g[:, :, 8 * i:8 * i + 8]
            sq = tt(scratch.ap.rearrange("p (j c) -> p j c", c=128), n1, n1, ALU.mult, dep, scratch.free, q="pool")
            r = red(G(7)[:, :, 0:1], scratch.ap.rearrange("p (j c) -> p j c", c=128), ALU.add, sq, gs.free)
            scratch.free = [r]
            r = tt(G(7)[:, :, 1:2], G(7)[:, :, 0:1], half[:, 1, 0:8].rearrange("p (n o) -> p n o", o=1), ALU.pow, r,
                   H1, q="pool")
            r = ts(G(7)[:, :, 2:3], G(7)[:, :, 1:2], 1e-12, None, ALU.max, None, r)
            r = recip(G(7)[:, :, 3:4], G(7)[:, :, 2:3], r)
            for j in range(8):
                m = mm(bk.ap[:, 8 * j:8 * j + 8], n1T[:, 128 * j:128 * j + 128], simn[:, which, :], True, True,
                       dT, bk.free, WD["sim"])
            l1 = tt(G(0), bk.ap[:, 0:64].rearrange("p (j e) -> p j e", e=8),
                    G(7)[:, :, 3:4].to_broadcast([128, 8, 8]), ALU.mult, m, r)
            bk.free = [l1]
            l2 = tt(G(0), G(0), sgm[:, which:which + 1, :].to_broadcast([128, 8, 8]), ALU.subtract, l1, WD["sgm"])
            t0, t1, a = top2(G(0), l2, G(2), G(3), G(1), G(4), gs.free)
            oh = tt(G(2), G(2), G(3), ALU.add, t0, t1)
            ina = ts(G(7)[:, :, 4:5], G(1)[:, :, 0:1], 0.0, None, ALU.is_le, None, a)
            po = tt(G(2), G(2), G(7)[:, :, 4:5].to_broadcast([128, 8, 8]), ALU.mult, oh, ina)
            mk = ts(G(3), G(0), 0.0, None, ALU.is_gt, None, oh)
            mk = tt(G(3), G(3), G(2), ALU.add, mk, po)
            mx = ts(G(7)[:, :, 5:6], G(1)[:, :, 0:1], 0.0, None, ALU.max, None, a)
            e = ts(G(4), G(0), 0.0, None, ALU.max, None, t0, t1)
            e = tt(G(4), G(4), G(7)[:, :, 5:6].to_broadcast([128, 8, 8]), ALU.subtract, e, mx)
            e = act(G(5), G(4), ACT.Exp, e)
            e = tt(G(5), G(5), G(3), ALU.mult, e, mk)
            sm = red(G(7)[:, :, 6:7], G(5), ALU.add, e)
            sm = recip(G(7)[:, :, 7:8], G(7)[:, :, 6:7], sm)
            return G(6), tt(G(6), G(5), G(7)[:, :, 7:8].to_broadcast([128, 8, 8]), ALU.mult, sm)

        def soft(b):
            R = WD
            hs, n1, q1, k1, v1 = (R[k] for k in ("hs", "n1", "q", "k", "v"))
            o = layernorm(tiles_of(b), [xtok[b]] * 8, [hs.ap[:, j, :] for j in range(8)], hs.free)
            t1 = affine_ln([hs.ap[:, j, :] for j in range(8)], o, 0, n1.ap, n1.free)
            xs = xT_ring.take()
            xt, last = transposes([n1.ap[:, j, :] for j in range(8)], [t1] * 8, xs, bank[0:2])
            gs = gbuf.take()
            rw, rt = gating(n1.ap, t1, xs.ap, xt, 0, bank[2], gs, big.take())
            xs.free = [queues["pe"][-1]]
            yield
            for h in range(2):
                qb, kb, vb = bank[0], bank[1], bank[2]
                for e in range(8):
                    sc = R["sc"].take()
                    tk = []
                    for j in range(4):
                        J = 4 * h + j
                        tk.append(ts(sc.ap[:, 128 * j:128 * j + 128], n1.ap[:, J, :], rw[:, J, e:e + 1], None, ALU.mult,
                                     None, rt, t1, sc.free))
                    sT = R["sT"].take()
                    tk, last = transposes([sc.ap[:, 128 * j:128 * j + 128] for j in range(4)], tk, sT,
                                          [bank[4 + e % 2]], ev="act" if e % 2 else "dve")
                    sc.free = [last]
                    mm(qb.ap, wqkv3[:, 0, e, :], sT.ap, e == 0, e == 7, tk, R["w"], qb.free)
                    mk_ = mm(kb.ap, wqkv3[:, 1, e, :], sT.ap, e == 0, e == 7, kb.free)
                    for j in range(4):
                        mv = add("pe", (lambda j, e, s_: lambda en: en.matmul(
                            vb.ap[:, 128 * j:128 * j + 128], s_.ap[:, 128 * j:128 * j + 128], wqkv3[:, 2, e, :],
                            start=(e == 0 and j == 0), stop=(e == 7), skip_group_check=True))(j, e, sT), vb.free)
                    sT.free = [mv]
                    yield
                tq = act(q1.ap[:, 512 * h:512 * h + 512], qb.ap, ACT.Copy, mk_, q1.free)
                tk_ = act(k1.ap[:, 512 * h:512 * h + 512], kb.ap, ACT.Copy, mk_, k1.free)
                tv = cp(v1.ap[:, 4 * h:4 * h + 4, :], vb.ap.rearrange("p (j c) -> p j c", c=128), mv, v1.free)
                qb.free, kb.free, vb.free = [tq], [tk_], [tv]
            qk = [tq, tk_]
            SC = 128 ** -0.5
            L = R["L"]
            lf = R["Lfree"]
            at, atk = n1, []
            for i in range(8):
                w = 128 * (i + 1)
                p = i % 2
                Sp = ps[p]
                b0, b1 = bank[2 * p], bank[2 * p + 1]
                for h in range((w + 511) // 512):
                    ww = min(512, w - 512 * h)
                    m = mm(Sp[:, 512 * h:512 * h + ww], q1.ap[:, 128 * i:128 * i + 128],
                           k1.ap[:, 512 * h:512 * h + ww], True, True, qk, b0.free, b1.free)
                dg = tt(Sp[:, 128 * i:128 * i + 128], Sp[:, 128 * i:128 * i + 128], tri[:, :], ALU.add, m)
                mx = red(L[:, i:i + 1], Sp[:, 0:w], ALU.max, dg, lf, negate=True)
                mx = ts(L[:, 8 + i:9 + i], L[:, i:i + 1], SC, None, ALU.mult, None, mx)
                pb = R["P"].take()
                t = act(pb.ap[:, 0:w], Sp[:, 0:w], ACT.Exp, mx, pb.free, bias=L[:, 8 + i:9 + i], scale=SC,
                        acc=L[:, 16 + i:17 + i])
                b0.free = b1.free = [t]
                rl = recip(L[:, 24 + i:25 + i], L[:, 16 + i:17 + i], t)
                pt = R["PT"].take()
                tk, last = transposes([pb.ap[:, 128 * k:128 * k + 128] for k in range(i + 1)], [t] * (i + 1), pt,
                                      [bank[4], bank[5]], ev="dve" if i % 2 else "act")
                pb.free = [last]
                ab = bank[6 + i % 2]
                for k in range(i + 1):
                    y = mm(ab.ap[:, 0:128], pt.ap[:, 128 * k:128 * k + 128], v1.ap[:, k, :], k == 0, k == i, tk, tv,
                           ab.free)
                pt.free = [y]
                z = ts(at.ap[:, i, :], ab.ap[:, 0:128], L[:, 24 + i:25 + i], None, ALU.mult, None, y, rl)
                ab.free = [z]
                atk.append(z)
                yield
            q1.free = k1.free = [m]
            v1.free = [y]
            R["Lfree"] = [z]
            xs = xT_ring.take()
            xt, last = transposes([at.ap[:, j, :] for j in range(8)], atk, xs, bank[0:2])
            n1.free = [last]
            ht = [None] * 8
            for j in range(8):
                pp = ps[2 + j % 2]
                b0, b1 = bank[4 + 2 * (j % 2)], bank[5 + 2 * (j % 2)]
                for h in range(2):
                    m = mm(pp[:, 512 * h:512 * h + 512], xs.ap[:, 128 * j:128 * j + 128],
                           wo3[:, 4 * h:4 * h + 4, :].rearrange("p e c -> p (e c)"), True, True, xt, b0.free, b1.free)
                t = None
                for e in range(8):
                    t = stt(hs.ap[:, j, :], pp[:, 128 * e:128 * e + 128], rw[:, j, e:e + 1], hs.ap[:, j, :], ALU.mult,
                            ALU.add, m, t)
                b0.free = b1.free = [t]
                ht[j] = t
            xs.free = [m]
            gs.free = [t]
            yield
            t1 = affine_ln([hs.ap[:, j, :] for j in range(8)], ht, 2, n1.ap, n1.free)
            xs = xT_ring.take()
            xt, last = transposes([n1.ap[:, j, :] for j in range(8)], [t1] * 8, xs, bank[0:2])
            gs = gbuf.take()
            rw, rt = gating(n1.ap, t1, xs.ap, xt, 1, bank[2], gs, big.take())
            n1.free = [rt, last]
            accs = list(ht)
            pend = None

            def down(h, e, hb, th):
                bk = bank[6 + e % 2]
                for j in range(4):
                    m = mm(bk.ap[:, 128 * j:128 * j + 128], hb.ap[:, 128 * j:128 * j + 128], w23[:, e, :], True, True,
                           th, bk.free)
                hb.free = [m]
                for j in range(4):
                    J = 4 * h + j
                    accs[J] = t = stt(hs.ap[:, J, :], bk.ap[:, 128 * j:128 * j + 128], rw[:, J, e:e + 1],
                                      hs.ap[:, J, :], ALU.mult, ALU.add, m, accs[J], rt, t1)
                bk.free = [t]
                return m
            for h in range(2):
                for e in range(8):
                    bk = bank[4 + e % 2]
                    m = mm(bk.ap, w13[:, e, :], xs.ap[:, 512 * h:512 * h + 512], True, True, xt[h], bk.free)
                    hb = hr.take()
                    th = act(hb.ap, bk.ap, ACT.Gelu, m, hb.free)
                    bk.free = [th]
                    if pend:
                        down(*pend)
                    pend = (h, e, hb, th)
                    yield
            xs.free = [m]
            md = down(*pend)
            gs.free = [accs[-1]]
            residual([hs.ap[:, j, :] for j in range(8)], accs, b, [hs])
            yield

        def run(g):
            for _ in g:
                pass

        wfree = []
        W_F = None
        w_sem = sem("w_sem")
        if "F" in phases:
            dma(WB[:, 0:4608], d["w1"].rearrange("p e f -> p (e f)"), w_sem)
            W_F = dma(WB[:, 4608:9216], d["w2"].rearrange("p e f h -> p (e f h)"), w_sem)

        def barrier_tokens():
            return [q[-1] for k, q in queues.items() if k != "sp" and q]

        if "M" in phases and "F" in phases:
            run(mamba(0))
            for b in range(1, NB):
                ga, gb = mamba(b), moe(b - 1)
                la = lb_ = True
                while la or lb_:
                    if la:
                        la = next(ga, 0) is None
                    if lb_:
                        lb_ = next(gb, 0) is None
            run(moe(NB - 1))
        else:
            for b in range(NB):
                if "M" in phases:
                    run(mamba(b))
                if "F" in phases:
                    run(moe(b))

        if "A" in phases:
            bt = barrier_tokens()
            w_sem2 = sem("w_sem2")
            dma(wqk, d["wqk"], w_sem2, bt)
            dma(wv, d["wv"], w_sem2)
            WA["w"] = dma(WB[:, 1536:2048], d["wout"].rearrange("p c n -> p (c n)"), w_sem2)
            WA["dsem"] = [[sem(f"dq{i}{j}") for j in range(2)] for i in range(2)]

            def sl(ap):
                s = Slot(ap)
                s.free = list(bt)
                return s

            def rg(aps):
                r = Ring([])
                r.slots = [sl(a) for a in aps]
                return r
            stv = [BIG[:, 4096 * i:4096 * i + 4096].bitcast(F16).rearrange("p (w h t) -> p w h t", w=2, h=4)
                   for i in range(2)]
            WA["stack"] = rg(stv)
            for i, s in enumerate(WA["stack"].slots):
                s.k = i
            WA["hl"] = rg([WB[:, 2048 + 1024 * i:3072 + 1024 * i].bitcast(F16).rearrange("p (a t) -> p a t", a=2)
                           for i in range(2)])
            WA["V"] = sl(WB[:, 5120:9216].rearrange("p (j n) -> p j n", j=8))
            WA["P"] = rg([MA[:, 0 + 0:0 + 1024], MA[:, 0 + 1024:0 + 2048], MA[:, 2048 + 0:2048 + 1024], MA[:, 2048 + 1024:2048 + 2048]])
            WA["DT"] = rg([MA[:, 4096 + 0:4096 + 1024], MA[:, 4096 + 1024:4096 + 2048]])
            WA["oT"] = rg([hr.slots[i].ap[:, :] for i in range(2)])
            big_sq = rg([hr.slots[2 + i].ap[:, :] for i in range(2)])
            WA["O"] = sl(MA[:, 6144:10240].rearrange("p (i n) -> p i n", i=8))
            WA["rb"] = MA[:, 10240:10560].rearrange("p (a b) -> p a b", b=64)
            WA["rbf"] = bt
            WA["l"] = rg([MA[:, 10560 + 8 * i:10568 + 8 * i] for i in range(6)])
            WA["later"] = []
            attention_setup()
            WA["stack"].slots[0].free += WA["free"]
            for b in range(NB):
                run(attention(b))

        if "D" in phases:
            bt = barrier_tokens()
            w_sem3 = sem("w_sem3")
            dma(WB[:, 0:3072], d["wqkv3"].rearrange("p a e h -> p (a e h)"), w_sem3, bt)
            dma(WB[:, 3072:4096], d["wo3"].rearrange("p e h -> p (e h)"), w_sem3)
            dma(WB[:, 4096:5120], d["w13"].rearrange("p e h -> p (e h)"), w_sem3)
            WD["w"] = dma(WB[:, 5120:6144], d["w23"].rearrange("p e h -> p (e h)"), w_sem3)

            def sl(ap):
                s = Slot(ap)
                s.free = list(bt)
                return s

            def rg(aps):
                r = Ring([])
                r.slots = [sl(a) for a in aps]
                return r
            for s in big.slots:
                s.free = s.free + list(bt)
            j8 = lambda ap: ap.rearrange("p (j c) -> p j c", c=128)
            WD["hs"] = sl(j8(MA[:, 0 + 0:0 + 1024]))
            WD["n1"] = sl(j8(MA[:, 0 + 1024:0 + 2048]))
            WD["q"] = sl(MA[:, 2048 + 0:2048 + 1024])
            WD["k"] = sl(MA[:, 2048 + 1024:2048 + 2048])
            WD["v"] = sl(j8(MA[:, 4096 + 0:4096 + 1024]))
            WD["sc"] = rg([MA[:, 6144 + 512 * i:6144 + 512 * i + 512] for i in range(4)])
            WD["sT"] = rg([MA[:, 8192 + 512 * i:8192 + 512 * i + 512] for i in range(4)])
            WD["P"] = rg([MA[:, 4096 + 1024:4096 + 2048], WB[:, 6144:7168]])
            WD["PT"] = rg([WB[:, 7168:8192], WB[:, 8192:9216]])
            WD["L"] = small["alog"][:, :, :].rearrange("p c n -> p (c n)")
            WD["Lfree"] = bt
            experts_setup()
            s_o = sem("s_o")
            ov = out.rearrange("(n p) c -> p n c", p=128)
            outs = []
            for b in range(NB):
                run(soft(b))
                outs.append(dma(ov[:, 8 * b:8 * b + 8, :], X[:, 8 * b:8 * b + 8, :], s_o, xtok[b]))
        else:
            s_o = sem("s_o")
            ov = out.rearrange("(n p) c -> p n c", p=128)
            outs = [dma(ov[:, 8 * b:8 * b + 8, :], X[:, 8 * b:8 * b + 8, :], s_o, xtok[b]) for b in range(NB)]

        sems = {}
        for q, steps in queues.items():
            n = 0
            for s in steps:
                if s.sem is not None:
                    sems[id(s.sem)] = s.count = sems.get(id(s.sem), 0) + 16
                elif s.awaited:
                    n += 1
                    s.count = n

        block = ctx.enter_context(nc.Block())

        def play(q, e):
            seen = {}
            for s in queues[q]:
                need = {}
                for a in s.after:
                    k = a.sem if a.sem is not None else own[a.queue]
                    if a.count > need.get(id(k), (0,))[0]:
                        need[id(k)] = (a.count, k)
                for i, (v, k) in need.items():
                    if v > seen.get(i, 0):
                        e.wait_ge(k, v)
                        seen[i] = v
                ins = s.emit(e)
                if s.sem is not None:
                    ins.then_inc(s.sem, 16)
                elif s.awaited:
                    ins.then_inc(own[q], 1)

        @block.tensor
        def _(e):
            play("pe", e)

        @block.scalar
        def _(e):
            play("act", e)

        @block.vector
        def _(e):
            play("dve", e)

        @block.gpsimd
        def _(e):
            play("pool", e)

        @block.sync
        def _(e):
            play("sp", e)
            e.wait_ge(s_o, 16 * len(outs))


def layout(i):
    a = {k: np.asarray(v) for k, v in i.items()}
    asc = np.ascontiguousarray
    r = {}
    r["x"] = a["L0_attn_x"].reshape(NB * T, C)
    r["winT"] = a["L0_attn_W_in"].T
    r["convw"] = a["L0_attn_conv_w"].reshape(2, 128, 3).transpose(1, 0, 2)
    r["convb"] = a["L0_attn_conv_b"].reshape(2, 128).T
    wx = a["L0_attn_W_xproj"].reshape(40, 2, 128).transpose(2, 1, 0)
    r["wx"] = np.concatenate([wx[:, :, 0:32]] * 3 + [wx[:, :, 32:40]], axis=2)
    r["wdt"] = a["L0_attn_W_dt"].T
    r["bdt"] = a["L0_attn_b_dt"].reshape(2, 128).T
    r["alog"] = a["L0_attn_A_log"].reshape(2, 128, 16).transpose(1, 0, 2)
    r["dcol"] = a["L0_attn_D"].reshape(2, 128).T
    r["woT"] = a["L0_attn_W_out"].reshape(128, 2, 128).transpose(2, 1, 0)
    r["gwT"] = a["L0_ffn_gate_w"].T
    r["w1"] = np.concatenate([a["L0_ffn_W1"], a["L0_ffn_sW1"][None]], 0).transpose(1, 0, 2)
    r["b1"] = np.concatenate([a["L0_ffn_b1"], a["L0_ffn_sb1"][None]], 0).reshape(9, 4, 128).transpose(2, 0, 1)
    r["w2"] = np.concatenate([a["L0_ffn_W2"], a["L0_ffn_sW2"][None]], 0).reshape(9, 4, 128, 128).transpose(2, 0, 1, 3)
    r["b2"] = np.concatenate([a["L0_ffn_b2"], a["L0_ffn_sb2"][None]], 0)
    r["wqk"] = np.concatenate([a["L1_attn_Wq"], a["L1_attn_Wkv"][:, 0:512]], 1)
    r["wv"] = a["L1_attn_Wkv"][:, 512:]
    r["wout"] = a["L1_attn_Wout"].reshape(4, 128, 128).transpose(1, 0, 2)
    r["lam"] = np.stack([a["L1_attn_lambda_" + k] for k in ("q1", "k1", "q2", "k2")])
    r["gam"] = np.concatenate([a["L1_attn_gamma"]] * 2)[:, None]
    r["lnp"] = np.stack([a["L1_ffn_ln1_w"], a["L1_ffn_ln1_b"], a["L1_ffn_ln2_w"], a["L1_ffn_ln2_b"]])
    r["sims"] = np.stack([a["L1_ffn_smha_sim"], a["L1_ffn_moe_sim"]], 1)
    r["gates"] = np.stack([a["L1_ffn_smha_gates"], a["L1_ffn_moe_gates"]])
    r["wqkv3"] = np.stack([a["L1_ffn_q_proj"], a["L1_ffn_k_proj"], a["L1_ffn_v_proj"]]).transpose(2, 0, 1, 3)
    r["wo3"] = a["L1_ffn_o_proj"].transpose(1, 0, 2)
    r["w13"] = a["L1_ffn_w1"].transpose(1, 0, 2)
    r["w23"] = a["L1_ffn_w2"].transpose(1, 0, 2)
    r["ident"] = np.eye(128, dtype=np.float32)
    r["iota8"] = np.broadcast_to(np.arange(8, dtype=np.float32), (128, 8))
    r["tri"] = np.where(np.tril(np.ones((128, 128), bool)), np.float32(0), np.float32(-1e30)).astype(np.float32)
    return {k: asc(v) for k, v in r.items()}


def kernel(**inputs):
    import concourse.bacc as _bacc
    from concourse.bass_utils import run_bass_kernel_spmd as _run

    nc = _bacc.Bacc("TRN2", target_bir_lowering=False, num_devices=1)
    arrays = layout(inputs)
    d = {k: nc.dram_tensor(k + "_dram", v.shape, mybir.dt.from_np(v.dtype), kind="ExternalInput").ap()
         for k, v in arrays.items()}
    o = nc.dram_tensor("out_dram", (NB * T, C), F32, kind="ExternalOutput").ap()
    program(nc, d, o)
    r = _run(nc, [{k + "_dram": v for k, v in arrays.items()}], core_ids=[0])
    return r.results[0]["out_dram"].reshape(NB, T, C)
```

```python
import math
from contextlib import ExitStack

import numpy as np

import concourse.bass as bass
from concourse import mybir

F32 = mybir.dt.float32
F16 = mybir.dt.float16
BF16 = mybir.dt.bfloat16
U32 = mybir.dt.uint32
ALU = mybir.AluOpType
ACT = mybir.ActivationFunctionType
AX = mybir.AxisListType.X

NB, T, C = 4, 1024, 128
NT = T // 128
LAMBDA_INIT = 0.8 - 0.6 * math.exp(-0.3)

PARAMS = {
    "x": (NB * T, C), "winT": (128, 512), "convw": (128, 2, 3), "convb": (128, 2),
    "wx": (128, 2, 104), "wdt": (8, 256), "bdt": (128, 2), "alog": (128, 2, 16), "dcol": (128, 2),
    "woT": (128, 2, 128),
    "gwT": (128, 8), "w1": (128, 9, 512), "b1": (128, 9, 4), "w2": (128, 9, 4, 128), "b2": (9, 128),
    "wqk": (128, 1024), "wv": (128, 512), "wout": (128, 4, 128), "lam": (4, 32), "gam": (128, 1),
    "lnp": (4, 128), "sims": (128, 2, 8), "gates": (2, 8),
    "wqkv3": (128, 3, 8, 128), "wo3": (128, 8, 128), "w13": (128, 8, 128), "w23": (128, 8, 128),
    "ident": (128, 128), "iota8": (128, 8), "tri": (128, 128),
}


class Step:

    def __init__(self, queue, emit, after, sem=None):
        self.queue, self.emit, self.after, self.sem = queue, emit, after, sem
        self.awaited, self.count = False, 0


class Slot:

    def __init__(self, ap):
        self.ap, self.free = ap, []


class Ring:
    def __init__(self, aps):
        self.slots, self.n = [Slot(a) for a in aps], 0

    def take(self):
        s = self.slots[self.n % len(self.slots)]
        self.n += 1
        return s


def flat(xs):
    out = []
    for x in xs:
        if isinstance(x, (list, tuple)):
            out += flat(x)
        elif x is not None:
            out.append(x)
    return out


def program(nc, d, out, phases="MFAD"):
    ctx = ExitStack()
    with ctx:
        def sb(name, shape, dt=F32):
            return ctx.enter_context(nc.sbuf_tensor(name, shape, dt))[tuple(slice(None) for _ in shape)]

        def sem(name):
            return ctx.enter_context(nc.semaphore(name))

        ps = [ctx.enter_context(nc.psum_tensor(f"ps{i}", [128, 1024], F32)) for i in range(4)]
        bank = [Slot(ps[i // 2][:, 512 * (i % 2):512 * (i % 2) + 512]) for i in range(8)]

        queues = {q: [] for q in ("pe", "act", "dve", "pool", "sp")}
        own = {q: sem("s_" + q) for q in queues}

        def add(q, emit, *after, sem=None):
            s = Step(q, emit, flat(after), sem)
            for a in s.after:
                a.awaited = True
            queues[q].append(s)
            return s

        def mm(o, l, r, st, sp, *after):
            return add("pe", lambda e: e.matmul(o, l, r, start=st, stop=sp), *after)

        def tr(o, i, idn, *after):
            return add("pe", lambda e: e.transpose(o, i, idn), *after)

        def act(o, i, f, *after, bias=0.0, scale=1.0, acc=None):
            if f == ACT.Copy:
                return add("act", lambda e: e.activation(o, i, f, scale=scale), *after)
            return add("act", lambda e: e.activation(o, i, f, bias=bias, scale=scale, accum_out=acc), *after)

        def tt(o, a, b, op, *after, q="dve"):
            return add(q, lambda e: e.tensor_tensor(o, a, b, op), *after)

        def ts(o, a, s1, s2, op0, op1, *after, q="dve"):
            if op1 is None:
                return add(q, lambda e: e.tensor_scalar(o, a, s1, None, op0), *after)
            return add(q, lambda e: e.tensor_scalar(o, a, s1, s2, op0, op1), *after)

        def stt(o, a, s, b, op0, op1, *after):
            return add("dve", lambda e: e.scalar_tensor_tensor(out=o, in0=a, scalar=s, in1=b, op0=op0, op1=op1),
                       *after)

        def cp(o, a, *after, q="dve"):
            return add(q, lambda e: e.tensor_copy(o, a), *after)

        def red(o, a, op, *after, negate=False):
            return add("dve", lambda e: e.tensor_reduce(o, a, AX, op, negate=negate), *after)

        def recip(o, a, *after):
            return add("dve", lambda e: e.reciprocal(o, a), *after)

        def dma(o, i, s, *after, q="sp"):
            return add(q, lambda e: e.dma_start(o, i), *after, sem=s)

        def fill(o, v, *after, q="dve"):
            return add(q, lambda e: e.memset(o, v), *after)

        X = sb("X", [128, 32, 128])
        ident = sb("ident", [128, 128])
        iota8 = sb("iota8", [128, 8])
        tri = sb("tri", [128, 128])
        SEL = sb("sel", [128, 4096], BF16)
        sel = SEL[0:96, :].rearrange("p (n c) -> p n c", n=32)
        half = sb("half", [128, 3, 64])
        lnp = sb("lnp", [128, 4, 128])
        small = {}
        for k in ("convw", "convb", "wx", "bdt", "alog", "dcol", "gwT", "b1", "gam", "sims", "woT"):
            small[k] = sb(k, list(PARAMS[k]))
        wdt = sb("wdt", [104, 256])
        b2 = sb("b2", [9, 128])
        lam = sb("lam", [128, 4, 32])
        gts = sb("gts", [128, 2, 8])
        winT = sb("winT", [128, 512])
        BIG = sb("BIG", [128, 9216])
        WB = sb("WB", [128, 9216])

        s_x = [sem(f"s_x{b}") for b in range(NB)]
        s_c = sem("s_c")
        consts = []

        def load(dst, name, view=None):
            consts.append(dma(dst, d[name] if view is None else view, s_c))

        xin = d["x"].rearrange("(n p) c -> p n c", p=128)
        xload = [dma(X[:, 0:8, :], xin[:, 0:8, :], s_x[0])]
        load(ident[:, :], "ident")
        load(winT[:, :], "winT")
        for k in ("convw", "convb", "wx", "bdt", "alog", "dcol", "gwT", "b1", "gam", "sims", "woT"):
            ap = small[k]
            load(ap[tuple(slice(None) for _ in PARAMS[k])], k)
        load(wdt[96:104, :], "wdt")
        load(iota8[:, :], "iota8")
        load(tri[:, :], "tri")
        load(b2[:, :], "b2")
        for i in range(4):
            load(lnp[:, i, :], "lnp", d["lnp"][i:i + 1, :].partition_broadcast(128))
            load(lam[:, i, :], "lam", d["lam"][i:i + 1, :].partition_broadcast(128))
        for i in range(2):
            load(gts[:, i, :], "gates", d["gates"][i:i + 1, :].partition_broadcast(128))
        K = consts[-1]
        for b in range(1, NB):
            xload.append(dma(X[:, 8 * b:8 * b + 8, :], xin[:, 8 * b:8 * b + 8, :], s_x[b]))
        H0 = fill(half[:, 0, :], -0.5, q="pool")
        H1 = fill(half[:, 1, :], 0.5, q="pool")
        xtok = {b: [xload[b]] for b in range(NB)}

        st_ring = Ring([sb(f"st{i}", [128, 8, 10]) for i in range(4)])

        def layernorm(src, deps, dst, dst_free):
            n = len(src)
            s = st_ring.take()
            st, fr = s.ap, s.free
            a = [add("dve", (lambda j: lambda e: e.bn_stats(st[:, j, 0:6], src[j]))(j), deps[j], fr)
                 for j in range(n)]
            g = [add("dve", (lambda j: lambda e: e.bn_aggr(st[:, j, 6:8], st[:, j, 0:6]))(j), a[j])
                 for j in range(n)]
            e1 = ts(st[:, 0:n, 8:9], st[:, 0:n, 7:8], 1e-5, None, ALU.add, None, g[-1], q="pool")
            e2 = tt(st[:, 0:n, 9:10], st[:, 0:n, 8:9], half[:, 0, 0:n].rearrange("p (n o) -> p n o", o=1),
                    ALU.pow, e1, H0, q="pool")
            o = [ts(dst[j], src[j], st[:, j, 6:7], st[:, j, 9:10], ALU.subtract, ALU.mult, e2, dst_free)
                 for j in range(n)]
            s.free = [o[-1]]
            return o

        big = Ring([BIG[:, 1024 * i:1024 * i + 1024] for i in range(9)])
        ln_buf = Ring([sb(f"lnb{i}", [128, 8, 128]) for i in range(2)])
        xT_ring = Ring([sb(f"xT{i}", [128, 1024]) for i in range(2)])

        def transposes(src, deps, dstslot, banks, ev="act"):
            fr = dstslot.free
            toks = []
            n = len(src)
            for h in range((n + 3) // 4):
                bk = banks[h % len(banks)]
                m = min(4, n - 4 * h)
                t = [tr(bk.ap[:, 128 * j:128 * j + 128], src[4 * h + j], ident[:, :], deps[4 * h + j], K,
                        bk.free) for j in range(m)]
                o, i = dstslot.ap[:, 512 * h:512 * h + 128 * m], bk.ap[:, 0:128 * m]
                if ev == "act":
                    c = act(o, i, ACT.Copy, t[-1], fr)
                else:
                    c = cp(o, i, t[-1], fr)
                bk.free = [c]
                toks.append(c)
            return toks, t[-1]

        def tiles_of(b):
            return [X[:, 8 * b + j, :] for j in range(8)]

        def residual(src, deps, b, src_slots, q="dve"):
            s = ln_buf.take()
            o = layernorm(src, deps, [s.ap[:, j, :] for j in range(8)], s.free)
            for sl in src_slots:
                sl.free = [o[-1]]
            r = tt(X[:, 8 * b:8 * b + 8, :], X[:, 8 * b:8 * b + 8, :], s.ap[:, :, :], ALU.add, o[-1], xtok[b], q=q)
            s.free = [r]
            xtok[b] = [r]
            return r

        MA = sb("MA", [128, 5 * 2048 + 2052])
        zs, uc, dl, du, yy = [MA[:, 2048 * i:2048 * i + 2048].rearrange("p (c t) -> p c t", c=2) for i in range(5)]
        up = MA[:, 10240:12292].rearrange("p (c t) -> p c t", c=2)
        aneg = sb("aneg", [128, 32])
        bc = sb("bc", [96, 3, 1024], BF16)
        mfree = {k: [] for k in ("up", "zs", "uc", "dl", "du", "yy", "bc")}

        pad = [fill(up[:, c, k:k + 1], 0.0, q="pool") for c in range(2) for k in (0, 1025)][-1]
        a1 = act(aneg[:, :], small["alog"][:, :, :].rearrange("p c n -> p (c n)"), ACT.Exp, K)
        A_OK = ts(aneg[:, :], aneg[:, :], -1.0, None, ALU.mult, None, a1)

        S_OK = []
        for k in range(3):
            o, i = sel[32 * k:32 * k + 32, :, :], ident[32 * k:32 * k + 32, 32 * k:32 * k + 32].rearrange(
                "p (n o) -> p n o", o=1).to_broadcast([32, 32, 128])
            S_OK.append(cp(o, i, K) if k == 2 else act(o, i, ACT.Copy, K))

        def mamba(b):
            B = bank[0:4]
            s = ln_buf.take()
            o = layernorm(tiles_of(b), [xtok[b]] * 8, [s.ap[:, j, :] for j in range(8)], s.free)
            xs = xT_ring.take()
            xt, last = transposes([s.ap[:, j, :] for j in range(8)], o, xs, B[0:2])
            s.free = [last]
            yield
            zt, ut = [], []
            k = 0
            for c in (2, 3, 0, 1):
                for h in range(2):
                    bk = B[k % 4]
                    k += 1
                    m = mm(bk.ap, winT[:, 128 * c:128 * c + 128], xs.ap[:, 512 * h:512 * h + 512], True, True,
                           xt[h], bk.free, K)
                    if c < 2:
                        t = act(up[:, c, 1 + 512 * h:513 + 512 * h], bk.ap, ACT.Copy, m, mfree["up"])
                        ut.append(t)
                    else:
                        t = act(zs[:, c - 2, 512 * h:512 * h + 512], bk.ap, ACT.Silu, m, mfree["zs"])
                        zt.append(t)
                    bk.free = [t]
                xs.free = [m]
            yield
            cw, cb = small["convw"], small["convb"]
            cv = [big.take() for _ in range(2)]
            t = [ts(cv[c].ap, up[:, c, 0:1024], cw[:, c, 0:1], cb[:, c:c + 1], ALU.mult, ALU.add,
                    ut[2 * c + 1], pad, cv[c].free) for c in range(2)]
            t = [stt(cv[c].ap, up[:, c, 1:1025], cw[:, c, 1:2], cv[c].ap, ALU.mult, ALU.add, t[c])
                 for c in range(2)]
            t = [stt(cv[c].ap, up[:, c, 2:1026], cw[:, c, 2:3], cv[c].ap, ALU.mult, ALU.add, t[c])
                 for c in range(2)]
            mfree["up"] = [t[1]]
            u = [act(uc[:, c, :], cv[c].ap, ACT.Silu, t[c], mfree["uc"]) for c in range(2)]
            for c in range(2):
                cv[c].free = [u[c]]
            yield
            p0 = ps[0]
            for h in range(2):
                for c in range(2):
                    m = mm(p0[0:104, 512 * h:512 * h + 512], small["wx"][:, c, :], uc[:, c, 512 * h:512 * h + 512],
                           c == 0, c == 1, u[c], B[0].free, B[1].free)
            r1 = big.take()
            rr = r1.ap[0:96, :]
            hi = cp(bc[:, 1, :], p0[0:96, :], m, mfree["bc"])
            dtb = big.take()
            dt = act(dtb.ap[96:104, :], p0[96:104, :], ACT.Copy, m, dtb.free)
            x1 = tt(rr, p0[0:96, :], bc[:, 1, :], ALU.subtract, hi, r1.free)
            B[0].free = B[1].free = [x1, dt]
            mid = cp(bc[:, 2, :], rr, x1)
            lo = tt(bc[:, 0, :], rr, bc[:, 2, :], ALU.subtract, mid)
            r1.free = [lo]
            f1 = cp(bc[32:64, 0, :], bc[32:64, 2, :], lo)
            bcok = [cp(bc[0:32, 0, :], bc[0:32, 1, :], f1)]
            dts = []
            vs, es = [], []
            for c in range(2):
                pp = ps[1 - c]
                bb = B[2 - 2 * c:4 - 2 * c]
                for h in range(2):
                    m = mm(pp[:, 512 * h:512 * h + 512], wdt[96:104, 128 * c:128 * c + 128],
                           dtb.ap[96:104, 512 * h:512 * h + 512], True, True, dt, bb[0].free, bb[1].free)
                v, e = big.take(), big.take()
                bd = small["bdt"][:, c:c + 1]
                t1 = act(v.ap, pp[:, :], ACT.Identity, m, v.free, bias=bd)
                t2 = act(e.ap, pp[:, :], ACT.Abs, m, e.free, bias=bd)
                bb[0].free = bb[1].free = [t2]
                vs.append((v, t1))
                es.append((e, t2))
            dtb.free = [m]
            yield
            es = [(e, act(e.ap, e.ap, ACT.Exp, t, scale=-1.0)) for e, t in es]
            us = [big.take() for _ in range(2)]
            ls = [big.take() for _ in range(2)]
            u1 = [ts(us[c].ap, es[c][0].ap, 1.0, None, ALU.add, None, es[c][1], us[c].free) for c in range(2)]
            ll = [act(ls[c].ap, us[c].ap, ACT.Ln, u1[c], ls[c].free) for c in range(2)]
            t = [stt(us[c].ap, us[c].ap, -1.0, es[c][0].ap, ALU.add, ALU.subtract, u1[c], ll[c])
                 for c in range(2)]
            for c in range(2):
                es[c][0].free = [t[c]]
            t = [tt(us[c].ap, ls[c].ap, us[c].ap, ALU.subtract, t[c]) for c in range(2)]
            for c in range(2):
                ls[c].free = [t[c]]
            dd = [stt(dl[:, c, :], vs[c][0].ap, 0.0, us[c].ap, ALU.max, ALU.add, t[c], vs[c][1], mfree["dl"])
                  for c in range(2)]
            for c in range(2):
                vs[c][0].free = us[c].free = [dd[c]]
            dus = [tt(du[:, c, :], dl[:, c, :], uc[:, c, :], ALU.mult, dd[c]) for c in range(2)]
            yield
            yt = [None, None]
            for n in range(16):
                for h in range(2):
                    mb = mm(ps[0][:, 512 * h:512 * h + 512], sel[:, n, :], bc[:, 0, 512 * h:512 * h + 512],
                            True, True, bcok, S_OK, B[0].free, B[1].free)
                for h in range(2):
                    mc = mm(ps[1][:, 512 * h:512 * h + 512], sel[:, 16 + n, :], bc[:, 0, 512 * h:512 * h + 512],
                            True, True, B[2].free, B[3].free)
                da, db, hc = [big.take() for _ in range(2)], [big.take() for _ in range(2)], []
                ta = [act(da[c].ap, dl[:, c, :], ACT.Exp, dd[c], da[c].free, A_OK,
                          scale=aneg[:, 16 * c + n:16 * c + n + 1]) for c in range(2)]
                tb = [tt(db[c].ap, du[:, c, :], ps[0][:, :], ALU.mult, mb, dus[c], db[c].free) for c in range(2)]
                B[0].free = B[1].free = [tb[1]]

                def scan(c):
                    o, a0 = db[c].ap, da[c].ap
                    return add("dve", lambda e: e.tensor_tensor_scan(o, a0, o, 0.0, ALU.mult, ALU.add),
                               ta[c], tb[c])
                sc = [scan(c) for c in range(2)]
                for c in range(2):
                    da[c].free = [sc[c]]
                if n == 0:
                    th = [tt(yy[:, c, :], db[c].ap, ps[1][:, :], ALU.mult, mc, sc[c], mfree["yy"])
                          for c in range(2)]
                    yt = th
                    for c in range(2):
                        db[c].free = [th[c]]
                else:
                    th = [tt(db[c].ap, db[c].ap, ps[1][:, :], ALU.mult, mc, sc[c]) for c in range(2)]
                    yt = [tt(yy[:, c, :], yy[:, c, :], db[c].ap, ALU.add, th[c], yt[c], q="pool")
                          for c in range(2)]
                    for c in range(2):
                        db[c].free = [yt[c]]
                B[2].free = B[3].free = [th[1]]
                yield
            mfree["bc"], mfree["dl"], mfree["du"] = [mc], [ta[1]], [tb[1]]
            t = [stt(yy[:, c, :], uc[:, c, :], small["dcol"][:, c:c + 1], yy[:, c, :], ALU.mult, ALU.add, yt[c])
                 for c in range(2)]
            mfree["uc"] = [t[1]]
            t = [tt(yy[:, c, :], yy[:, c, :], zs[:, c, :], ALU.mult, t[c], zt) for c in range(2)]
            mfree["zs"] = [t[1]]
            deps = []
            for j in range(8):
                for c in range(2):
                    m = mm(ps[0][:, 128 * j:128 * j + 128], yy[:, c, 128 * j:128 * j + 128],
                           small["woT"][:, c, :], c == 0, c == 1, t[c], B[0].free, B[1].free)
                deps.append(m)
            mfree["yy"] = [m]
            residual([ps[0][:, 128 * j:128 * j + 128] for j in range(8)], [deps[3]] * 4 + [deps[7]] * 4, b, B[0:2])
            yield

        w1 = WB[:, 0:4608].rearrange("p (e f) -> p e f", e=9)
        w2 = WB[:, 4608:9216].rearrange("p (e f h) -> p e f h", e=9, f=4)
        HR = sb("HR", [128, 4096])
        OS = sb("OS", [128, 256])
        hr = Ring([HR[:, 512 * i:512 * i + 512] for i in range(8)])
        acc_r = Ring([sb(f"acc{i}", [128, 8, 128]) for i in range(1)])
        gbuf = Ring([sb(f"g{i}", [128, 8, 64]) for i in range(1)])
        gidx = Ring([sb(f"gi{i}", [128, 8, 8], U32) for i in range(2)])
        combT = sb("combT", [9, 1024])
        cfree = []

        def top2(lg, deps, out0, out1, mx, g8, free):
            gi = gidx.take()
            lt = []
            a = [add("dve", (lambda j: lambda e: e.max(mx[:, j, :], lg[:, j, :]))(j), deps, free)
                 for j in range(8)]
            lt = [add("dve", (lambda j: lambda e: e.max_index(gi.ap[:, j, :], mx[:, j, :], lg[:, j, :]))(j),
                      a[j], gi.free) for j in range(8)]
            f = cp(g8, gi.ap[:, :, :], lt)
            gi.free = [f]
            io = iota8[:, :].rearrange("p (o e) -> p o e", o=1).to_broadcast([128, 8, 8])
            r0 = tt(out0, io, g8[:, :, 0:1].to_broadcast([128, 8, 8]), ALU.is_equal, f, K)
            r1 = tt(out1, io, g8[:, :, 1:2].to_broadcast([128, 8, 8]), ALU.is_equal, f)
            return r0, r1, a

        def moe(b):
            MB, YB = bank[4:6], bank[6:8]
            s = ln_buf.take()
            o = layernorm(tiles_of(b), [xtok[b]] * 8, [s.ap[:, j, :] for j in range(8)], s.free)
            xs = xT_ring.take()
            xt, last = transposes([s.ap[:, j, :] for j in range(8)], o, xs, MB)
            s.free = [last]
            bk = YB[0]
            for j in range(8):
                m = mm(bk.ap[:, 8 * j:8 * j + 8], xs.ap[:, 128 * j:128 * j + 128], small["gwT"][:, :], True, True,
                       xt, bk.free)
            gs = gbuf.take()
            g = gs.ap
            G = lambda i: g[:, :, 8 * i:8 * i + 8]
            lg = cp(G(0), bk.ap[:, 0:64].rearrange("p (j e) -> p j e", e=8), m, gs.free)
            bk.free = [lg]
            t0, t1, a = top2(G(0), lg, G(2), G(3), G(1), G(4), gs.free)
            r = tt(G(5)[:, :, 0:1], G(1)[:, :, 1:2], G(1)[:, :, 0:1], ALU.subtract, a)
            r = act(G(5)[:, :, 1:2], G(5)[:, :, 0:1], ACT.Exp, r)
            r1 = ts(G(5)[:, :, 2:3], G(5)[:, :, 1:2], 1.0, None, ALU.add, None, r)
            r2 = recip(G(5)[:, :, 3:4], G(5)[:, :, 2:3], r1)
            r3 = tt(G(5)[:, :, 4:5], G(5)[:, :, 3:4], G(5)[:, :, 1:2], ALU.mult, r2)
            c1 = tt(G(2), G(2), G(5)[:, :, 3:4].to_broadcast([128, 8, 8]), ALU.mult, r2, t0)
            c2 = tt(G(3), G(3), G(5)[:, :, 4:5].to_broadcast([128, 8, 8]), ALU.mult, r3, t1)
            c3 = tt(G(6), G(2), G(3), ALU.add, c1, c2)
            c4 = fill(G(7), 1.0, gs.free)
            comb = g[:, :, 48:57]
            for h in range(2):
                bk = YB[h]
                for j in range(4):
                    m = tr(bk.ap[0:9, 128 * j:128 * j + 128], comb[:, 4 * h + j, :], ident[:, :], c3, c4, bk.free)
                ct = act(combT[:, 512 * h:512 * h + 512], bk.ap[0:9, :], ACT.Copy, m, cfree)
                bk.free = [ct]
            yield
            ac = acc_r.take()
            accs = [None] * 8
            pend = None
            plan = [(h, e) for h in range(2) for e in (8, 0, 1, 2, 3, 4, 5, 6, 7)]
            nm = [0]

            def down(h, e, hs):
                bk = YB[down.k % 2]
                down.k += 1
                for j in range(4):
                    o = bk.ap[:, 128 * j:128 * j + 128]
                    if e == 8:
                        mm(o, combT[:, 512 * h + 128 * j:512 * h + 128 * j + 128], b2[:, :], True, False, ct,
                           bk.free)
                    for f in range(4):
                        m = mm(o, hs[f][0].ap[:, 128 * j:128 * j + 128], w2[:, e, f, :], f == 0 and e != 8, f == 3,
                               hs[f][1], bk.free)
                for f in range(4):
                    hs[f][0].free = [m]
                if e == 8:
                    t = act(ac.ap[:, 4 * h:4 * h + 4, :], bk.ap.rearrange("p (j c) -> p j c", c=128), ACT.Copy,
                            m, ac.free)
                    for j in range(4):
                        accs[4 * h + j] = t
                else:
                    for j in range(4):
                        J = 4 * h + j
                        t = accs[J] = stt(ac.ap[:, J, :], bk.ap[:, 128 * j:128 * j + 128],
                                          G(6)[:, J, e:e + 1], ac.ap[:, J, :], ALU.mult, ALU.add, m, accs[J], c3)
                bk.free = [t]
                return m
            down.k = 0
            for h, e in plan:
                hs = []
                for f in range(4):
                    bk = MB[nm[0] % 2]
                    nm[0] += 1
                    m = mm(bk.ap, w1[:, e, 128 * f:128 * f + 128], xs.ap[:, 512 * h:512 * h + 512], True, True,
                           xt[h], bk.free, W_F)
                    hb = hr.take()
                    t = act(hb.ap, bk.ap, ACT.Gelu, m, hb.free, bias=small["b1"][:, e, f:f + 1])
                    bk.free = [t]
                    hs.append((hb, t))
                if pend:
                    md = down(*pend)
                pend = (h, e, hs)
                yield
            xs.free = [m]
            md = down(*pend)
            cfree[:] = [md]
            s = residual([ac.ap[:, j, :] for j in range(8)], accs, b, [ac])
            gs.free = [accs[-1]]
            wfree.append(md)
            yield

        WA = {}
        wqk = WB[:, 0:1024]
        wv = WB[:, 1024:1536]
        wout = WB[:, 1536:2048].rearrange("p (c n) -> p c n", c=4)
        lsc = sb("lsc", [128, 8])

        def attention_setup():
            j1 = tt(BIG[:, 0:32], lam[:, 0, :], lam[:, 1, :], ALU.mult, K, [s.free for s in big.slots])
            j2 = tt(BIG[:, 32:64], lam[:, 2, :], lam[:, 3, :], ALU.mult)
            r1 = red(lsc[:, 0:1], BIG[:, 0:32], ALU.add, j1)
            r2 = red(lsc[:, 1:2], BIG[:, 32:64], ALU.add, j2)
            x = act(lsc[:, 2:4], lsc[:, 0:2], ACT.Exp, r1, r2)
            y = tt(lsc[:, 4:5], lsc[:, 3:4], lsc[:, 2:3], ALU.subtract, x)
            z = ts(lsc[:, 5:6], lsc[:, 4:5], -LAMBDA_INIT, None, ALU.add, None, y)
            w = ts(wout, wout, small["gam"][:, 0:1], 1.0 - LAMBDA_INIT, ALU.mult, ALU.mult, WA["w"])
            WA["lam"], WA["wout"] = z, w
            WA["free"] = [r1, r2]

        def score_operands(g, xs, xt):
            st = WA["stack"].take()
            st.ready = []
            for w in range(2):
                hl = WA["hl"].take()
                hi, lo = hl.ap[:, 0, :], hl.ap[:, 1, :]
                tl = []
                sc = 32 ** -0.5 if w == 0 else 1.0
                for h in range(2):
                    bk = WA["ob"].take()
                    m = mm(bk.ap, wqk[:, 512 * w + 128 * g:512 * w + 128 * g + 128],
                           xs.ap[:, 512 * h:512 * h + 512], True, True, xt[h], bk.free, WA["w"])
                    t1 = act(hi[:, 512 * h:512 * h + 512], bk.ap, ACT.Copy, m, hl.free, scale=sc)
                    t2 = stt(lo[:, 512 * h:512 * h + 512], bk.ap, sc, hi[:, 512 * h:512 * h + 512], ALU.mult,
                             ALU.subtract, t1)
                    bk.free = [t2]
                    tl += [t1, t2]
                    yield
                for hh in range(4):
                    for r in range(3):
                        part = lo if r == 2 - w else hi
                        dm = dma(st.ap[32 * r:32 * r + 32, w, hh, :], part[32 * hh:32 * hh + 32, :],
                                 WA["dsem"][st.k][w], tl, st.free)
                hl.free = [dm]
                st.ready.append(dm)
            WA["xs_last"] = m
            WA["next"] = st

        def attention_head(b):
            s = ln_buf.take()
            o = layernorm(tiles_of(b), [xtok[b]] * 8, [s.ap[:, j, :] for j in range(8)], s.free)
            yield
            xs = xT_ring.take()
            xt = []
            for h in range(2):
                bk = WA["ob"].take()
                t = [tr(bk.ap[:, 128 * j:128 * j + 128], s.ap[:, 4 * h + j, :], ident[:, :], o[4 * h + j], K,
                        bk.free) for j in range(4)]
                xt.append(act(xs.ap[:, 512 * h:512 * h + 512], bk.ap, ACT.Copy, t[-1], xs.free))
                bk.free = [xt[-1]]
                yield
            s.free = [t[-1]]
            WA["x", b] = (xs, xt)
            yield from score_operands(0, xs, xt)

        def values(b):
            xs, xt = WA["x", b]
            V = WA["V"]
            vt = []
            for j in range(8):
                bk = bank[6 + j % 2]
                m = mm(bk.ap, xs.ap[:, 128 * j:128 * j + 128], wv, True, True, xt, bk.free, WA["w"])
                t = act(V.ap[:, j, :], bk.ap, ACT.Copy, m, V.free)
                bk.free = [t]
                vt.append(t)
            return vt

        def attention_tail(b, O, ot):
            o = O.ap
            k = b % 2
            rb = WA["rb"][k]
            for i in range(8):
                sq = WA["sq"].take()
                t = tt(sq.ap, o[:, i, :], o[:, i, :], ALU.mult, ot[i], sq.free, q="pool")
                t = red(rb[:, 0, 8 * i:8 * i + 8], sq.ap.rearrange("p (h d) -> p h d", d=64), ALU.add, t,
                        WA["rbf"][k])
                sq.free = [t]
                yield
            t = ts(rb[:, 1, :], rb[:, 0, :], 1.0 / 64, None, ALU.mult, None, t, q="pool")
            t = tt(rb[:, 2, :], rb[:, 1, :], half[:, 1, :], ALU.pow, t, H1, q="pool")
            yield
            yield
            t = ts(rb[:, 3, :], rb[:, 2, :], 1e-8, None, ALU.add, None, t)
            t = recip(rb[:, 4, :], rb[:, 3, :], t)
            yield
            y = acc_r.take()
            deps = []
            for i in range(8):
                n = tt(o[:, i, :].rearrange("p (h d) -> p h d", d=64), o[:, i, :].rearrange("p (h d) -> p h d", d=64),
                       rb[:, 4, 8 * i:8 * i + 8].rearrange("p (h o) -> p h o", o=1).to_broadcast([128, 8, 64]),
                       ALU.mult, t)
                yield
                os = WA["oT"].take()
                bk = WA["ob"].take()
                for c in range(4):
                    x = tr(bk.ap[:, 128 * c:128 * c + 128], o[:, i, 128 * c:128 * c + 128], ident[:, :], n, bk.free)
                tk = act(os.ap, bk.ap, ACT.Copy, x, os.free)
                bk.free = [tk]
                yield
                bk = WA["ob"].take()
                for c in range(4):
                    m = mm(bk.ap[:, 0:128], os.ap[:, 128 * c:128 * c + 128], wout[:, c, :], c == 0, c == 3, tk,
                           WA["wout"], bk.free)
                os.free = [m]
                deps.append(act(y.ap[:, i, :], bk.ap[:, 0:128], ACT.Copy, m, y.free))
                bk.free = [deps[-1]]
                yield
            WA["rbf"][k] = [n]
            O.free = [x]
            residual([y.ap[:, j, :] for j in range(8)], deps, b, [y])

        def attention():
            units = [(b, g, i, pp) for b in range(NB) for g in range(4) for i in range(8) for pp in range(2)]
            per = 64
            run(attention_head(0))
            O, ots, extra, rec = {}, {}, [], {}

            def scores(n, s_):
                b, g, i, pp = units[n]
                r = rec[n]
                st, L = r["st"], r["L"].ap
                hh = 2 * pp + s_
                Sp = ps[s_]
                b0, b1 = bank[2 * s_], bank[2 * s_ + 1]
                for h in range(2):
                    m = mm(Sp[:, 512 * h:512 * h + 512], st.ap[0:96, 0, hh, 128 * i:128 * i + 128],
                           st.ap[0:96, 1, hh, 512 * h:512 * h + 512], True, True, st.ready, b0.free, b1.free)
                mx = red(L[:, 2 * s_ + pp:2 * s_ + pp + 1], Sp[:, :], ALU.max, m, r["L"].free, negate=True)
                pb = WA["P"].take()
                t = act(pb.ap, Sp[:, :], ACT.Exp, mx, pb.free, bias=L[:, 2 * s_ + pp:2 * s_ + pp + 1],
                        acc=L[:, 4 + 2 * s_ + pp:5 + 2 * s_ + pp])
                b0.free = b1.free = [t]
                st.free = [m]
                r["P"].append(pb)
                r["e"].append(t)

            def sums(n):
                r, q = rec[n], rec[n - 1]
                L = r["L"].ap
                r["r"] = q["r"] = recip(L[:, 8:12], L[:, 4:8], r["e"], q["e"])
                c = tt(L[:, 12:14], L[:, 4:6], L[:, 10:12], ALU.mult, r["r"], q="pool")
                r["c"] = q["c"] = ts(L[:, 14:16], L[:, 12:14], lsc[:, 5:6], None, ALU.mult, None, c, WA["lam"],
                                     q="pool")

            def difference(n):
                r = rec[n]
                L, P, pp = r["L"].ap, r["P"], n % 2
                r["D"] = stt(P[0].ap, P[1].ap, L[:, 14 + pp:15 + pp], P[0].ap, ALU.mult, ALU.add, r["c"])
                P[1].free = [r["D"]]

            def turn(n):
                r = rec[n]
                D = r["P"][0].ap
                dt_ = r["DT"] = WA["DT"].take()
                for k in range(8):
                    x = tr(ps[2][:, 128 * k:128 * k + 128], D[:, 128 * k:128 * k + 128], ident[:, :], r["D"],
                           bank[4].free, bank[5].free)
                e = act(dt_.ap, ps[2][:, :], ACT.Copy, x, dt_.free)
                bank[4].free = bank[5].free = [e]
                r["tk"] = e
                r["P"][0].free = [x]

            def weigh(n):
                b, g, i, pp = units[n]
                r = rec[n]
                if n % per == 0:
                    vt[0] = values(b)
                ob = bank[6]
                hp = 2 * g + pp
                for k in range(8):
                    y = mm(ob.ap[64 * pp:64 * pp + 64, 0:128], WA["V"].ap[:, k, 64 * hp:64 * hp + 64],
                           r["DT"].ap[:, 128 * k:128 * k + 128], k == 0, k == 7, r["tk"], vt[0], ob.free)
                r["DT"].free = [y]
                r["y"] = y
                if n % per == per - 1:
                    WA["V"].free = [y]
                    WA["x", b][0].free = [WA["xs_last_of", b], y]

            def gather(n):
                os = WA["os"].take()
                e = act(os.ap, bank[6].ap[:, 0:128], ACT.Copy, rec[n]["y"], rec[n - 1]["y"], os.free)
                bank[6].free = [e]
                rec[n]["os"] = (os, e)

            def settle(n):
                b, g, i, pp = units[n]
                r = rec.pop(n)
                rec.pop(n - 1)
                if n % per == 1:
                    O[b], ots[b] = WA["O"][b % 2], {}
                bk = WA["ob"].take()
                os, e = r["os"]
                x = tr(bk.ap[:, 0:128], os.ap, ident[:, :], e, bk.free)
                os.free = [x]
                z = tt(O[b].ap[:, i, 128 * g:128 * g + 128].rearrange("p (a d) -> p a d", a=2),
                       bk.ap[:, 0:128].rearrange("p (a d) -> p a d", a=2),
                       r["L"].ap[:, 8:10].rearrange("p (a o) -> p a o", o=1).to_broadcast([128, 2, 64]), ALU.mult,
                       x, r["r"], O[b].free)
                bk.free = [z]
                r["L"].free = [z]
                ots[b][i] = z
                if n % per == per - 1:
                    extra.append(attention_tail(b, O[b], ots[b]))

            vt = [None]
            N = len(units)
            for n in range(N + 6):
                if 0 <= n - 5 < N and n % 2 == 0:
                    gather(n - 5)
                if 0 <= n - 1 < N and n % 2 == 0:
                    sums(n - 1)
                if n < N:
                    b, g, i, pp = units[n]
                    if i == 0 and pp == 0:
                        st = WA["next"]
                        if g == 3:
                            WA["xs_last_of", b] = WA["xs_last"]
                            nxt = attention_head(b + 1) if b + 1 < NB else None
                        else:
                            nxt = score_operands(g + 1, *WA["x", b])
                        WA["next"] = None
                        if nxt:
                            WA["want"] = nxt
                    rec[n] = {"st": st, "L": WA["l"].take() if pp == 0 else rec[n - 1]["L"], "P": [], "e": []}
                    scores(n, 0)
                if 0 <= n - 3 < N:
                    turn(n - 3)
                if 0 <= n - 2 < N:
                    difference(n - 2)
                if n < N:
                    scores(n, 1)
                if 0 <= n - 5 < N and n % 2 == 0:
                    settle(n - 5)
                if 0 <= n - 4 < N:
                    weigh(n - 4)
                w = WA.get("want")
                if w is not None and n % 2 == 1:
                    if next(w, 1) == 1:
                        WA["want"] = None
                if n % 16 == 15 or n >= N:
                    while WA.get("want") is not None:
                        if next(WA["want"], 1) == 1:
                            WA["want"] = None
                if extra and next(extra[0], 1) == 1:
                    extra.pop(0)
            for x in extra:
                run(x)

        wqkv3 = WB[:, 0:3072].rearrange("p (a e h) -> p a e h", a=3, e=8)
        wo3 = WB[:, 3072:4096].rearrange("p (e h) -> p e h", e=8)
        w13 = WB[:, 4096:5120].rearrange("p (e h) -> p e h", e=8)
        w23 = WB[:, 5120:6144].rearrange("p (e h) -> p e h", e=8)
        simn = sb("simn", [128, 2, 8])
        sgm = sb("sgm", [128, 2, 8])
        ones = sb("ones", [128, 128])
        WD = {}
        ones_t = fill(ones[:, :], 1.0)

        def experts_setup():
            sq = tt(lsq[:, 0:16], small["sims"][:, :, :].rearrange("p a e -> p (a e)"),
                    small["sims"][:, :, :].rearrange("p a e -> p (a e)"), ALU.mult, K)
            m = mm(bank[0].ap[:, 0:16], ones[:, :], lsq[:, 0:16], True, True, sq, ones_t, bank[0].free)
            a = act(lsq[:, 16:32], bank[0].ap[:, 0:16], ACT.Copy, m)
            bank[0].free = [a]
            p = tt(lsq[:, 32:48], lsq[:, 16:32], half[:, 1, 0:16], ALU.pow, a, H1, q="pool")
            q_ = ts(lsq[:, 48:64], lsq[:, 32:48], 1e-12, None, ALU.max, None, p)
            r = recip(lsq[:, 32:48], lsq[:, 48:64], q_)
            WD["sim"] = tt(simn[:, :, :].rearrange("p a e -> p (a e)"),
                           small["sims"][:, :, :].rearrange("p a e -> p (a e)"), lsq[:, 32:48], ALU.mult, r)
            e1 = act(sgm[:, :, :].rearrange("p a e -> p (a e)"), gts[:, :, :].rearrange("p a e -> p (a e)"), ACT.Exp,
                     K, scale=-1.0)
            e2 = ts(sgm[:, :, :], sgm[:, :, :], 1.0, None, ALU.add, None, e1)
            WD["sgm"] = recip(sgm[:, :, :], sgm[:, :, :], e2)

        lsq = sb("lsq", [128, 64])

        def affine_ln(src, deps, w, dst, free):
            o = layernorm(src, deps, [dst[:, j, :] for j in range(8)], free)
            wb = lnp[:, w:w + 1, :].to_broadcast([128, 8, 128])
            bb = lnp[:, w + 1:w + 2, :].to_broadcast([128, 8, 128])
            t = tt(dst, dst, wb, ALU.mult, o, K)
            return tt(dst, dst, bb, ALU.add, t)

        def gating(n1, dep, n1T, dT, which, bk, gs, scratch):
            g = gs.ap
            G = lambda i: g[:, :, 8 * i:8 * i + 8]
            sq = tt(scratch.ap.rearrange("p (j c) -> p j c", c=128), n1, n1, ALU.mult, dep, scratch.free, q="pool")
            r = red(G(7)[:, :, 0:1], scratch.ap.rearrange("p (j c) -> p j c", c=128), ALU.add, sq, gs.free)
            scratch.free = [r]
            r = tt(G(7)[:, :, 1:2], G(7)[:, :, 0:1], half[:, 1, 0:8].rearrange("p (n o) -> p n o", o=1), ALU.pow, r,
                   H1, q="pool")
            r = ts(G(7)[:, :, 2:3], G(7)[:, :, 1:2], 1e-12, None, ALU.max, None, r)
            r = recip(G(7)[:, :, 3:4], G(7)[:, :, 2:3], r)
            for j in range(8):
                m = mm(bk.ap[:, 8 * j:8 * j + 8], n1T[:, 128 * j:128 * j + 128], simn[:, which, :], True, True,
                       dT, bk.free, WD["sim"])
            l1 = tt(G(0), bk.ap[:, 0:64].rearrange("p (j e) -> p j e", e=8),
                    G(7)[:, :, 3:4].to_broadcast([128, 8, 8]), ALU.mult, m, r)
            bk.free = [l1]
            l2 = tt(G(0), G(0), sgm[:, which:which + 1, :].to_broadcast([128, 8, 8]), ALU.subtract, l1, WD["sgm"])
            t0, t1, a = top2(G(0), l2, G(2), G(3), G(1), G(4), gs.free)
            oh = tt(G(2), G(2), G(3), ALU.add, t0, t1)
            ina = ts(G(7)[:, :, 4:5], G(1)[:, :, 0:1], 0.0, None, ALU.is_le, None, a)
            po = tt(G(2), G(2), G(7)[:, :, 4:5].to_broadcast([128, 8, 8]), ALU.mult, oh, ina)
            mk = ts(G(3), G(0), 0.0, None, ALU.is_gt, None, oh)
            mk = tt(G(3), G(3), G(2), ALU.add, mk, po)
            mx = ts(G(7)[:, :, 5:6], G(1)[:, :, 0:1], 0.0, None, ALU.max, None, a)
            e = ts(G(4), G(0), 0.0, None, ALU.max, None, t0, t1)
            e = tt(G(4), G(4), G(7)[:, :, 5:6].to_broadcast([128, 8, 8]), ALU.subtract, e, mx)
            e = act(G(5), G(4), ACT.Exp, e)
            e = tt(G(5), G(5), G(3), ALU.mult, e, mk)
            sm = red(G(7)[:, :, 6:7], G(5), ALU.add, e)
            sm = recip(G(7)[:, :, 7:8], G(7)[:, :, 6:7], sm)
            return G(6), tt(G(6), G(5), G(7)[:, :, 7:8].to_broadcast([128, 8, 8]), ALU.mult, sm)

        def soft(b, k):
            R = WD["stream"][k]
            hs, n1, q1, k1, v1, xs, gs, L = (R[x] for x in ("hs", "n1", "q", "k", "v", "xT", "g", "L"))
            B, S0, S1 = bank[4 * k:4 * k + 4], ps[2 * k], ps[2 * k + 1]
            n1t = [n1.ap[:, j, :] for j in range(8)]
            hst = [hs.ap[:, j, :] for j in range(8)]
            o = layernorm(tiles_of(b), [xtok[b]] * 8, hst, hs.free)
            yield 4
            t1 = affine_ln(hst, o, 0, n1.ap, n1.free)
            yield 5
            xt, last = transposes(n1t, [t1] * 8, xs, B[0:2])
            yield 1
            rw, rt = gating(n1.ap, t1, xs.ap, xt, 0, B[2], gs, big.take())
            xs.free = [queues["pe"][-1]]
            yield 5
            for h in range(2):
                qb, kb, vb = B[0:3]

                def scaled(e):
                    sc = R["sc"].take()
                    ss = tt(sc.ap.rearrange("p (j c) -> p j c", c=128), n1.ap[:, 4 * h:4 * h + 4, :],
                            rw[:, 4 * h:4 * h + 4, e:e + 1].to_broadcast([128, 4, 128]), ALU.mult, rt, t1, sc.free,
                            q="pool")
                    sT = R["sT"].take()
                    tk, last = transposes([sc.ap[:, 128 * j:128 * j + 128] for j in range(4)], [ss] * 4, sT, [B[3]])
                    sc.free = [last]
                    return sT, tk

                nxt = scaled(0)
                yield 1
                for e in range(8):
                    sT, tk = nxt
                    if e < 7:
                        nxt = scaled(e + 1)
                    mm(qb.ap, wqkv3[:, 0, e, :], sT.ap, e == 0, e == 7, tk, WD["w"], qb.free)
                    yield 0.9
                    mk_ = mm(kb.ap, wqkv3[:, 1, e, :], sT.ap, e == 0, e == 7, kb.free)
                    yield 0.9
                    for j in range(4):
                        mv = add("pe", (lambda j, e, s_: lambda en: en.matmul(
                            vb.ap[:, 128 * j:128 * j + 128], s_.ap[:, 128 * j:128 * j + 128], wqkv3[:, 2, e, :],
                            start=(e == 0 and j == 0), stop=(e == 7), skip_group_check=True))(j, e, sT), vb.free)
                    sT.free = [mv]
                    yield 1.3
                tq = act(q1.ap[:, 512 * h:512 * h + 512], qb.ap, ACT.Copy, mk_, q1.free, scale=128 ** -0.5)
                tk_ = act(k1.ap[:, 512 * h:512 * h + 512], kb.ap, ACT.Copy, mk_, k1.free)
                tv = act(v1.ap[:, 4 * h:4 * h + 4, :], vb.ap.rearrange("p (j c) -> p j c", c=128), ACT.Copy, mv,
                         v1.free)
                qb.free, kb.free, vb.free = [tq], [tk_], [tv]
            qk = [tq, tk_]
            lf = R["Lfree"]
            atk = []
            b0, b1 = B[0:2]

            def scores(i):
                w = 128 * (i + 1)
                for h in range((w + 511) // 512):
                    ww = min(512, w - 512 * h)
                    m = mm(S0[:, 512 * h:512 * h + ww], q1.ap[:, 128 * i:128 * i + 128],
                           k1.ap[:, 512 * h:512 * h + ww], True, True, qk, b0.free, b1.free)
                return m

            m = scores(0)
            for i in range(8):
                w = 128 * (i + 1)
                dg = tt(S0[:, 128 * i:128 * i + 128], S0[:, 128 * i:128 * i + 128], tri[:, :], ALU.add, m)
                mx = red(L[:, i:i + 1], S0[:, 0:w], ALU.max, dg, lf, negate=True)
                pb = WD["P"].take()
                t = act(pb.ap[:, 0:w], S0[:, 0:w], ACT.Exp, mx, pb.free, bias=L[:, i:i + 1],
                        acc=L[:, 16 + i:17 + i])
                b0.free = b1.free = [t]
                yield 1.5
                if i < 7:
                    m = scores(i + 1)
                rl = recip(L[:, 24 + i:25 + i], L[:, 16 + i:17 + i], t)
                pt = WD["PT"].take()
                tk, last = transposes([pb.ap[:, 128 * x:128 * x + 128] for x in range(i + 1)], [t] * (i + 1), pt,
                                      [B[2]])
                pb.free = [last]
                yield 1
                ab = B[3]
                for x in range(i + 1):
                    y = mm(ab.ap[:, 0:128], pt.ap[:, 128 * x:128 * x + 128], v1.ap[:, x, :], x == 0, x == i, tk, tv,
                           ab.free)
                pt.free = [y]
                z = ts(n1.ap[:, i, :], ab.ap[:, 0:128], L[:, 24 + i:25 + i], None, ALU.mult, None, y, rl)
                ab.free = [z]
                atk.append(z)
                yield 1 + 0.2 * i
            q1.free = k1.free = [m]
            v1.free = [y]
            R["Lfree"] = [z]
            xt, last = transposes(n1t, atk, xs, B[0:2])
            n1.free = [last]
            yield 1
            ht = [None] * 8
            for j in range(8):
                pp = (S0, S1)[j % 2]
                c0, c1 = B[2 * (j % 2):2 * (j % 2) + 2]
                for h in range(2):
                    m = mm(pp[:, 512 * h:512 * h + 512], xs.ap[:, 128 * j:128 * j + 128],
                           wo3[:, 4 * h:4 * h + 4, :].rearrange("p e c -> p (e c)"), True, True, xt, c0.free, c1.free)
                t = None
                for e in range(8):
                    t = stt(hs.ap[:, j, :], pp[:, 128 * e:128 * e + 128], rw[:, j, e:e + 1], hs.ap[:, j, :], ALU.mult,
                            ALU.add, m, t)
                    if e % 2:
                        yield 0.6
                c0.free = c1.free = [t]
                ht[j] = t
            xs.free = [m]
            gs.free = [t]
            t1 = affine_ln(hst, ht, 2, n1.ap, n1.free)
            yield 5
            xt, last = transposes(n1t, [t1] * 8, xs, B[0:2])
            rw, rt = gating(n1.ap, t1, xs.ap, xt, 1, B[2], gs, big.take())
            n1.free = [rt, last]
            yield 5
            accs = list(ht)
            pend = None

            def down(h, e, hb, th):
                bk = B[2 + e % 2]
                for j in range(4):
                    m = mm(bk.ap[:, 128 * j:128 * j + 128], hb.ap[:, 128 * j:128 * j + 128], w23[:, e, :], True, True,
                           th, bk.free)
                hb.free = [m]
                for j in range(4):
                    J = 4 * h + j
                    accs[J] = t = stt(hs.ap[:, J, :], bk.ap[:, 128 * j:128 * j + 128], rw[:, J, e:e + 1],
                                      hs.ap[:, J, :], ALU.mult, ALU.add, m, accs[J], rt, t1)
                bk.free = [t]
            for h in range(2):
                for e in range(8):
                    bk = B[e % 2]
                    m = mm(bk.ap, w13[:, e, :], xs.ap[:, 512 * h:512 * h + 512], True, True, xt[h], bk.free)
                    hb = hr.take()
                    th = act(hb.ap, bk.ap, ACT.Gelu, m, hb.free)
                    bk.free = [th]
                    yield 1
                    if pend:
                        down(*pend)
                    pend = (h, e, hb, th)
                    yield 1
            xs.free = [m]
            down(*pend)
            gs.free = [accs[-1]]
            residual(hst, accs, b, [hs])
            outs.append(dma(ov[:, 8 * b:8 * b + 8, :], X[:, 8 * b:8 * b + 8, :], s_o, xtok[b]))
            yield 3

        def run(g):
            for _ in g:
                pass

        def chain(*gs):
            for g in gs:
                yield from g

        def merge(*streams):
            live = [[t0, i, g] for i, (t0, g) in enumerate(streams)]
            while live:
                s = min(live)
                c = next(s[2], None)
                if c is None:
                    live.remove(s)
                else:
                    s[0] += c

        wfree = []
        W_F = None
        w_sem = sem("w_sem")
        if "F" in phases:
            dma(WB[:, 0:4608], d["w1"].rearrange("p e f -> p (e f)"), w_sem)
            W_F = dma(WB[:, 4608:9216], d["w2"].rearrange("p e f h -> p (e f h)"), w_sem)

        def barrier_tokens():
            return [q[-1] for k, q in queues.items() if k != "sp" and q]

        if "M" in phases and "F" in phases:
            run(mamba(0))
            for b in range(1, NB):
                ga, gb = mamba(b), moe(b - 1)
                la = lb_ = True
                while la or lb_:
                    if la:
                        la = next(ga, 0) is None
                    if lb_:
                        lb_ = next(gb, 0) is None
            run(moe(NB - 1))
        else:
            for b in range(NB):
                if "M" in phases:
                    run(mamba(b))
                if "F" in phases:
                    run(moe(b))

        if "A" in phases:
            bt = barrier_tokens()
            w_sem2 = sem("w_sem2")
            dma(wqk, d["wqk"], w_sem2, bt)
            dma(wv, d["wv"], w_sem2)
            WA["w"] = dma(WB[:, 1536:2048], d["wout"].rearrange("p c n -> p (c n)"), w_sem2)
            WA["dsem"] = [[sem(f"dq{i}{j}") for j in range(2)] for i in range(2)]

            def sl(ap):
                s = Slot(ap)
                s.free = list(bt)
                return s

            def rg(aps):
                r = Ring([])
                r.slots = [sl(a) for a in aps]
                return r
            stv = [BIG[:, 4096 * i:4096 * i + 4096].bitcast(F16).rearrange("p (w h t) -> p w h t", w=2, h=4)
                   for i in range(2)]
            WA["stack"] = rg(stv)
            for i, x in enumerate(WA["stack"].slots):
                x.k = i
            WA["hl"] = rg([BIG[:, 8192:9216].bitcast(F16).rearrange("p (a t) -> p a t", a=2)])
            WA["V"] = sl(WB[:, 2048:6144].rearrange("p (j n) -> p j n", j=8))
            WA["P"] = rg([WB[:, 6144 + 1024 * i:7168 + 1024 * i] for i in range(3)]
                         + [MA[:, 1024 * i:1024 * i + 1024] for i in range(3)]
                         + [SEL[:, 2048 * i:2048 * i + 2048].bitcast(F32) for i in range(2)])
            WA["os"] = rg([OS[:, 128 * i:128 * i + 128] for i in range(2)])
            WA["DT"] = rg([MA[:, 3072 + 1024 * i:4096 + 1024 * i] for i in range(2)])
            WA["O"] = [sl(MA[:, 5120:9216].rearrange("p (i n) -> p i n", i=8)),
                       sl(HR[:, :].rearrange("p (i n) -> p i n", i=8))]
            WA["oT"] = rg([MA[:, 9216 + 512 * i:9728 + 512 * i] for i in range(2)])
            WA["sq"] = rg([MA[:, 10240 + 512 * i:10752 + 512 * i] for i in range(2)])
            WA["rb"] = [MA[:, 11264 + 320 * i:11584 + 320 * i].rearrange("p (a b) -> p a b", b=64) for i in range(2)]
            WA["rbf"] = [bt, bt]
            WA["l"] = rg([MA[:, 11904 + 16 * i:11920 + 16 * i] for i in range(8)])
            WA["ob"] = Ring([])
            WA["ob"].slots = [bank[7]]
            attention_setup()
            WA["stack"].slots[0].free += WA["free"]
            attention()

        if "D" in phases:
            bt = barrier_tokens()
            w_sem3 = sem("w_sem3")
            dma(WB[:, 0:3072], d["wqkv3"].rearrange("p a e h -> p (a e h)"), w_sem3, bt)
            dma(WB[:, 3072:4096], d["wo3"].rearrange("p e h -> p (e h)"), w_sem3)
            dma(WB[:, 4096:5120], d["w13"].rearrange("p e h -> p (e h)"), w_sem3)
            WD["w"] = dma(WB[:, 5120:6144], d["w23"].rearrange("p e h -> p (e h)"), w_sem3)

            def sl(ap):
                s = Slot(ap)
                s.free = list(bt)
                return s

            def rg(aps):
                r = Ring([])
                r.slots = [sl(a) for a in aps]
                return r
            for s in big.slots + hr.slots:
                s.free = s.free + list(bt)
            j8 = lambda ap: ap.rearrange("p (j c) -> p j c", c=128)
            big.slots = big.slots[0:2]
            at_ = lambda k: BIG[:, 1024 * k:1024 * k + 1024]
            WD["stream"] = []
            for k in range(2):
                m0 = 5120 * k
                r = {x: sl(MA[:, m0 + 1024 * i:m0 + 1024 * i + 1024]) for i, x in enumerate(("hs", "n1", "q", "k", "v"))}
                for x in ("hs", "n1", "v"):
                    r[x].ap = j8(r[x].ap)
                r["sc"] = rg([at_(2 + k)[:, 512 * i:512 * i + 512] for i in range(2)])
                r["sT"] = rg([at_(4 + k)[:, 512 * i:512 * i + 512] for i in range(2)])
                r["g"] = sl(at_(7)[:, 512 * k:512 * k + 512].rearrange("p (j n) -> p j n", j=8))
                r["L"] = at_(8)[:, 32 * k:32 * k + 32]
                r["Lfree"] = bt
                r["xT"] = xT_ring.slots[k]
                WD["stream"].append(r)
            WD["P"] = rg([WB[:, 6144:7168], WB[:, 7168:8192]])
            WD["PT"] = rg([WB[:, 8192:9216], at_(6)])
            experts_setup()
            s_o = sem("s_o")
            ov = out.rearrange("(n p) c -> p n c", p=128)
            outs = []
            merge((0, chain(soft(0, 0), soft(2, 0))), (40, chain(soft(1, 1), soft(3, 1))))
        else:
            s_o = sem("s_o")
            ov = out.rearrange("(n p) c -> p n c", p=128)
            outs = [dma(ov[:, 8 * b:8 * b + 8, :], X[:, 8 * b:8 * b + 8, :], s_o, xtok[b]) for b in range(NB)]

        sems = {}
        for q, steps in queues.items():
            n = 0
            for s in steps:
                if s.sem is not None:
                    sems[id(s.sem)] = s.count = sems.get(id(s.sem), 0) + 16
                elif s.awaited:
                    n += 1
                    s.count = n

        block = ctx.enter_context(nc.Block())

        def play(q, e):
            seen = {}
            for s in queues[q]:
                need = {}
                for a in s.after:
                    k = a.sem if a.sem is not None else own[a.queue]
                    if a.count > need.get(id(k), (0,))[0]:
                        need[id(k)] = (a.count, k)
                for i, (v, k) in need.items():
                    if v > seen.get(i, 0):
                        e.wait_ge(k, v)
                        seen[i] = v
                ins = s.emit(e)
                if s.sem is not None:
                    ins.then_inc(s.sem, 16)
                elif s.awaited:
                    ins.then_inc(own[q], 1)

        @block.tensor
        def _(e):
            play("pe", e)

        @block.scalar
        def _(e):
            play("act", e)

        @block.vector
        def _(e):
            play("dve", e)

        @block.gpsimd
        def _(e):
            play("pool", e)

        @block.sync
        def _(e):
            play("sp", e)
            e.wait_ge(s_o, 16 * len(outs))


def layout(i):
    a = {k: np.asarray(v) for k, v in i.items()}
    asc = np.ascontiguousarray
    r = {}
    r["x"] = a["L0_attn_x"].reshape(NB * T, C)
    r["winT"] = a["L0_attn_W_in"].T
    r["convw"] = a["L0_attn_conv_w"].reshape(2, 128, 3).transpose(1, 0, 2)
    r["convb"] = a["L0_attn_conv_b"].reshape(2, 128).T
    wx = a["L0_attn_W_xproj"].reshape(40, 2, 128).transpose(2, 1, 0)
    r["wx"] = np.concatenate([wx[:, :, 0:32]] * 3 + [wx[:, :, 32:40]], axis=2)
    r["wdt"] = a["L0_attn_W_dt"].T
    r["bdt"] = a["L0_attn_b_dt"].reshape(2, 128).T
    r["alog"] = a["L0_attn_A_log"].reshape(2, 128, 16).transpose(1, 0, 2)
    r["dcol"] = a["L0_attn_D"].reshape(2, 128).T
    r["woT"] = a["L0_attn_W_out"].reshape(128, 2, 128).transpose(2, 1, 0)
    r["gwT"] = a["L0_ffn_gate_w"].T
    r["w1"] = np.concatenate([a["L0_ffn_W1"], a["L0_ffn_sW1"][None]], 0).transpose(1, 0, 2)
    r["b1"] = np.concatenate([a["L0_ffn_b1"], a["L0_ffn_sb1"][None]], 0).reshape(9, 4, 128).transpose(2, 0, 1)
    r["w2"] = np.concatenate([a["L0_ffn_W2"], a["L0_ffn_sW2"][None]], 0).reshape(9, 4, 128, 128).transpose(2, 0, 1, 3)
    r["b2"] = np.concatenate([a["L0_ffn_b2"], a["L0_ffn_sb2"][None]], 0)
    r["wqk"] = np.concatenate([a["L1_attn_Wq"], a["L1_attn_Wkv"][:, 0:512]], 1)
    r["wv"] = a["L1_attn_Wkv"][:, 512:]
    r["wout"] = a["L1_attn_Wout"].reshape(4, 128, 128).transpose(1, 0, 2)
    r["lam"] = np.stack([a["L1_attn_lambda_" + k] for k in ("q1", "k1", "q2", "k2")])
    r["gam"] = np.concatenate([a["L1_attn_gamma"]] * 2)[:, None]
    r["lnp"] = np.stack([a["L1_ffn_ln1_w"], a["L1_ffn_ln1_b"], a["L1_ffn_ln2_w"], a["L1_ffn_ln2_b"]])
    r["sims"] = np.stack([a["L1_ffn_smha_sim"], a["L1_ffn_moe_sim"]], 1)
    r["gates"] = np.stack([a["L1_ffn_smha_gates"], a["L1_ffn_moe_gates"]])
    r["wqkv3"] = np.stack([a["L1_ffn_q_proj"], a["L1_ffn_k_proj"], a["L1_ffn_v_proj"]]).transpose(2, 0, 1, 3)
    r["wo3"] = a["L1_ffn_o_proj"].transpose(1, 0, 2)
    r["w13"] = a["L1_ffn_w1"].transpose(1, 0, 2)
    r["w23"] = a["L1_ffn_w2"].transpose(1, 0, 2)
    r["ident"] = np.eye(128, dtype=np.float32)
    r["iota8"] = np.broadcast_to(np.arange(8, dtype=np.float32), (128, 8))
    r["tri"] = np.where(np.tril(np.ones((128, 128), bool)), np.float32(0), np.float32(-1e30)).astype(np.float32)
    return {k: asc(v) for k, v in r.items()}


def kernel(**inputs):
    import concourse.bacc as _bacc
    from concourse.bass_utils import run_bass_kernel_spmd as _run

    nc = _bacc.Bacc("TRN2", target_bir_lowering=False, num_devices=1)
    arrays = layout(inputs)
    d = {k: nc.dram_tensor(k + "_dram", v.shape, mybir.dt.from_np(v.dtype), kind="ExternalInput").ap()
         for k, v in arrays.items()}
    o = nc.dram_tensor("out_dram", (NB * T, C), F32, kind="ExternalOutput").ap()
    program(nc, d, o)
    r = _run(nc, [{k + "_dram": v for k, v in arrays.items()}], core_ids=[0])
    return r.results[0]["out_dram"].reshape(NB, T, C)
```

```python
import math
from contextlib import ExitStack

import numpy as np

import concourse.bass as bass
from concourse import mybir

F32 = mybir.dt.float32
F16 = mybir.dt.float16
BF16 = mybir.dt.bfloat16
U32 = mybir.dt.uint32
ALU = mybir.AluOpType
ACT = mybir.ActivationFunctionType
AX = mybir.AxisListType.X

NB, T, C = 4, 1024, 128
NT = T // 128
LAMBDA_INIT = 0.8 - 0.6 * math.exp(-0.3)

PARAMS = {
    "x": (NB * T, C), "winT": (128, 512), "convw": (128, 2, 3), "convb": (128, 2),
    "wx": (128, 2, 104), "wdt": (8, 256), "bdt": (128, 2), "alog": (128, 2, 16), "dcol": (128, 2),
    "woT": (128, 2, 128),
    "gwT": (128, 8), "w1": (128, 9, 512), "b1": (128, 9, 4), "w2": (128, 9, 4, 128), "b2": (9, 128),
    "wqk": (128, 1024), "wv": (128, 512), "wout": (128, 4, 128), "lam": (4, 32), "gam": (128, 1),
    "lnp": (4, 128), "sims": (128, 2, 8), "gates": (2, 8),
    "wqkv3": (128, 3, 8, 128), "wo3": (128, 8, 128), "w13": (128, 8, 128), "w23": (128, 8, 128),
    "ident": (128, 128), "iota8": (128, 8), "tri": (128, 128),
}


class Step:

    def __init__(self, queue, emit, after, sem=None):
        self.queue, self.emit, self.after, self.sem = queue, emit, after, sem
        self.awaited, self.count = False, 0


class Slot:

    def __init__(self, ap):
        self.ap, self.free = ap, []


class Ring:
    def __init__(self, aps):
        self.slots, self.n = [Slot(a) for a in aps], 0

    def take(self):
        s = self.slots[self.n % len(self.slots)]
        self.n += 1
        return s


def flat(xs):
    out = []
    for x in xs:
        if isinstance(x, (list, tuple)):
            out += flat(x)
        elif x is not None:
            out.append(x)
    return out


def program(nc, d, out, phases="MFAD"):
    ctx = ExitStack()
    with ctx:
        def sb(name, shape, dt=F32):
            return ctx.enter_context(nc.sbuf_tensor(name, shape, dt))[tuple(slice(None) for _ in shape)]

        def sem(name):
            return ctx.enter_context(nc.semaphore(name))

        ps = [ctx.enter_context(nc.psum_tensor(f"ps{i}", [128, 1024], F32)) for i in range(4)]
        bank = [Slot(ps[i // 2][:, 512 * (i % 2):512 * (i % 2) + 512]) for i in range(8)]

        queues = {q: [] for q in ("pe", "act", "dve", "pool", "sp")}
        own = {q: sem("s_" + q) for q in queues}

        def add(q, emit, *after, sem=None):
            s = Step(q, emit, flat(after), sem)
            for a in s.after:
                a.awaited = True
            queues[q].append(s)
            return s

        def mm(o, l, r, st, sp, *after):
            return add("pe", lambda e: e.matmul(o, l, r, start=st, stop=sp), *after)

        def tr(o, i, idn, *after):
            return add("pe", lambda e: e.transpose(o, i, idn), *after)

        def act(o, i, f, *after, bias=0.0, scale=1.0, acc=None):
            if f == ACT.Copy:
                return add("act", lambda e: e.activation(o, i, f, scale=scale), *after)
            return add("act", lambda e: e.activation(o, i, f, bias=bias, scale=scale, accum_out=acc), *after)

        def tt(o, a, b, op, *after, q="dve"):
            return add(q, lambda e: e.tensor_tensor(o, a, b, op), *after)

        def ts(o, a, s1, s2, op0, op1, *after, q="dve"):
            if op1 is None:
                return add(q, lambda e: e.tensor_scalar(o, a, s1, None, op0), *after)
            return add(q, lambda e: e.tensor_scalar(o, a, s1, s2, op0, op1), *after)

        def stt(o, a, s, b, op0, op1, *after):
            return add("dve", lambda e: e.scalar_tensor_tensor(out=o, in0=a, scalar=s, in1=b, op0=op0, op1=op1),
                       *after)

        def cp(o, a, *after, q="dve"):
            return add(q, lambda e: e.tensor_copy(o, a), *after)

        def red(o, a, op, *after, negate=False):
            return add("dve", lambda e: e.tensor_reduce(o, a, AX, op, negate=negate), *after)

        def recip(o, a, *after):
            return add("dve", lambda e: e.reciprocal(o, a), *after)

        def dma(o, i, s, *after, q="sp"):
            return add(q, lambda e: e.dma_start(o, i), *after, sem=s)

        def fill(o, v, *after, q="dve"):
            return add(q, lambda e: e.memset(o, v), *after)

        X = sb("X", [128, 32, 128])
        ident = sb("ident", [128, 128])
        iota8 = sb("iota8", [128, 8])
        tri = sb("tri", [128, 128])
        SEL = sb("sel", [128, 4096], BF16)
        sel = SEL[0:96, :].rearrange("p (n c) -> p n c", n=32)
        half = sb("half", [128, 3, 64])
        lnp = sb("lnp", [128, 4, 128])
        small = {}
        for k in ("convw", "convb", "wx", "bdt", "alog", "dcol", "gwT", "b1", "gam", "sims", "woT"):
            small[k] = sb(k, list(PARAMS[k]))
        wdt = sb("wdt", [104, 256])
        b2 = sb("b2", [9, 128])
        lam = sb("lam", [128, 4, 32])
        gts = sb("gts", [128, 2, 8])
        winT = sb("winT", [128, 512])
        BIG = sb("BIG", [128, 9216])
        WB = sb("WB", [128, 9216])

        s_x = [sem(f"s_x{b}") for b in range(NB)]
        s_c = sem("s_c")
        consts = []

        def load(dst, name, view=None):
            consts.append(dma(dst, d[name] if view is None else view, s_c))

        xin = d["x"].rearrange("(n p) c -> p n c", p=128)
        xload = [dma(X[:, 0:8, :], xin[:, 0:8, :], s_x[0])]
        load(ident[:, :], "ident")
        load(winT[:, :], "winT")
        for k in ("convw", "convb", "wx", "bdt", "alog", "dcol", "gwT", "b1", "gam", "sims", "woT"):
            ap = small[k]
            load(ap[tuple(slice(None) for _ in PARAMS[k])], k)
        load(wdt[96:104, :], "wdt")
        load(iota8[:, :], "iota8")
        load(tri[:, :], "tri")
        load(b2[:, :], "b2")
        for i in range(4):
            load(lnp[:, i, :], "lnp", d["lnp"][i:i + 1, :].partition_broadcast(128))
            load(lam[:, i, :], "lam", d["lam"][i:i + 1, :].partition_broadcast(128))
        for i in range(2):
            load(gts[:, i, :], "gates", d["gates"][i:i + 1, :].partition_broadcast(128))
        K = consts[-1]
        for b in range(1, NB):
            xload.append(dma(X[:, 8 * b:8 * b + 8, :], xin[:, 8 * b:8 * b + 8, :], s_x[b]))
        H0 = fill(half[:, 0, :], -0.5, q="pool")
        H1 = fill(half[:, 1, :], 0.5, q="pool")
        xtok = {b: [xload[b]] for b in range(NB)}

        st_ring = Ring([sb(f"st{i}", [128, 8, 10]) for i in range(4)])

        def layernorm(src, deps, dst, dst_free):
            n = len(src)
            s = st_ring.take()
            st, fr = s.ap, s.free
            a = [add("dve", (lambda j: lambda e: e.bn_stats(st[:, j, 0:6], src[j]))(j), deps[j], fr)
                 for j in range(n)]
            g = [add("dve", (lambda j: lambda e: e.bn_aggr(st[:, j, 6:8], st[:, j, 0:6]))(j), a[j])
                 for j in range(n)]
            e1 = ts(st[:, 0:n, 8:9], st[:, 0:n, 7:8], 1e-5, None, ALU.add, None, g[-1], q="pool")
            e2 = tt(st[:, 0:n, 9:10], st[:, 0:n, 8:9], half[:, 0, 0:n].rearrange("p (n o) -> p n o", o=1),
                    ALU.pow, e1, H0, q="pool")
            yield 3
            o = [ts(dst[j], src[j], st[:, j, 6:7], st[:, j, 9:10], ALU.subtract, ALU.mult, e2, dst_free)
                 for j in range(n)]
            s.free = [o[-1]]
            return o

        big = Ring([BIG[:, 1024 * i:1024 * i + 1024] for i in range(9)])
        ln_buf = Ring([sb(f"lnb{i}", [128, 8, 128]) for i in range(2)])
        xT_ring = Ring([sb(f"xT{i}", [128, 1024]) for i in range(2)])

        def transposes(src, deps, dstslot, banks, ev="act"):
            fr = dstslot.free
            toks = []
            n = len(src)
            for h in range((n + 3) // 4):
                bk = banks[h % len(banks)]
                m = min(4, n - 4 * h)
                t = [tr(bk.ap[:, 128 * j:128 * j + 128], src[4 * h + j], ident[:, :], deps[4 * h + j], K,
                        bk.free) for j in range(m)]
                o, i = dstslot.ap[:, 512 * h:512 * h + 128 * m], bk.ap[:, 0:128 * m]
                if ev == "act":
                    c = act(o, i, ACT.Copy, t[-1], fr)
                else:
                    c = cp(o, i, t[-1], fr)
                bk.free = [c]
                toks.append(c)
            return toks, t[-1]

        def split(hi, lo, src, scale, deps, free):
            t1 = act(hi, src, ACT.Copy, deps, free, scale=scale)
            return t1, stt(lo, src, scale, hi, ALU.mult, ALU.subtract, t1)

        def transposes_split(src, deps, dst, free, banks):
            toks = []
            n = len(src)
            for h in range((n + 3) // 4):
                bk = banks[h % len(banks)]
                m = min(4, n - 4 * h)
                t = [tr(bk.ap[:, 128 * j:128 * j + 128], src[4 * h + j], ident[:, :], deps[4 * h + j], K,
                        bk.free) for j in range(m)]
                c = slice(512 * h, 512 * h + 128 * m)
                t1, t2 = split(dst[:, 0, c], dst[:, 1, c], bk.ap[:, 0:128 * m], XS, t[-1], free)
                bk.free = [t2]
                toks.append([t1, t2])
            return toks, t[-1]

        def product(o, w, x, st, sp, *after):
            mm(o, w[0], x[0], st, False, *after)
            mm(o, w[0], x[1], False, False, *after)
            return mm(o, w[1], x[0], False, sp, *after)

        XS, WS = 16.0, 256.0
        BACK = 1.0 / (XS * WS)

        def tiles_of(b):
            return [X[:, 8 * b + j, :] for j in range(8)]

        def residual(src, deps, b, src_slots, q="dve"):
            s = ln_buf.take()
            o = yield from layernorm(src, deps, [s.ap[:, j, :] for j in range(8)], s.free)
            for sl in src_slots:
                sl.free = [o[-1]]
            r = tt(X[:, 8 * b:8 * b + 8, :], X[:, 8 * b:8 * b + 8, :], s.ap[:, :, :], ALU.add, o[-1], xtok[b], q='pool')
            s.free = [r]
            xtok[b] = [r]
            return r

        MA = sb("MA", [128, 5 * 2048 + 2052])
        zs, uc, dl, du, yy = [MA[:, 2048 * i:2048 * i + 2048].rearrange("p (c t) -> p c t", c=2) for i in range(5)]
        up = MA[:, 10240:12292].rearrange("p (c t) -> p c t", c=2)
        aneg = sb("aneg", [128, 32])
        BC = sb("bc", [128, 3072], BF16)
        bc = BC[0:96, :].rearrange("p (k t) -> p k t", k=3)
        mfree = {k: [] for k in ("up", "zs", "uc", "dl", "du", "yy", "bc")}

        pad = [fill(up[:, c, k:k + 1], 0.0, q="pool") for c in range(2) for k in (0, 1025)][-1]
        a1 = act(aneg[:, :], small["alog"][:, :, :].rearrange("p c n -> p (c n)"), ACT.Exp, K)
        A_OK = ts(aneg[:, :], aneg[:, :], -1.0, None, ALU.mult, None, a1)

        S_OK = []
        for k in range(3):
            o, i = sel[32 * k:32 * k + 32, :, :], ident[32 * k:32 * k + 32, 32 * k:32 * k + 32].rearrange(
                "p (n o) -> p n o", o=1).to_broadcast([32, 32, 128])
            S_OK.append(cp(o, i, K) if k == 2 else act(o, i, ACT.Copy, K))

        done = set()

        def mamba(b):
            B = bank[0:4]
            s = ln_buf.take()
            o = yield from layernorm(tiles_of(b), [xtok[b]] * 8, [s.ap[:, j, :] for j in range(8)], s.free)
            yield 5
            xs = xT_ring.take()
            xt, last = transposes([s.ap[:, j, :] for j in range(8)], o, xs, B[0:2])
            s.free = [last]
            yield 2
            zt, ut = [], []
            k = 0
            for c in (2, 3, 0, 1):
                for h in range(2):
                    bk = B[k % 4]
                    k += 1
                    m = mm(bk.ap, winT[:, 128 * c:128 * c + 128], xs.ap[:, 512 * h:512 * h + 512], True, True,
                           xt[h], bk.free, K)
                    if c < 2:
                        t = act(up[:, c, 1 + 512 * h:513 + 512 * h], bk.ap, ACT.Copy, m, mfree["up"])
                        ut.append(t)
                    else:
                        t = act(zs[:, c - 2, 512 * h:512 * h + 512], bk.ap, ACT.Silu, m, mfree["zs"])
                        zt.append(t)
                    bk.free = [t]
                    yield 0.9
                xs.free = [m]
            cw, cb = small["convw"], small["convb"]
            cv = [big.take() for _ in range(2)]
            u = []
            for c in range(2):
                t = ts(cv[c].ap, up[:, c, 0:1024], cw[:, c, 0:1], cb[:, c:c + 1], ALU.mult, ALU.add,
                       ut[2 * c + 1], pad, cv[c].free)
                yield 1.2
                t = stt(cv[c].ap, up[:, c, 1:1025], cw[:, c, 1:2], cv[c].ap, ALU.mult, ALU.add, t)
                yield 1.2
                t = stt(cv[c].ap, up[:, c, 2:1026], cw[:, c, 2:3], cv[c].ap, ALU.mult, ALU.add, t)
                yield 1.2
                u.append(act(uc[:, c, :], cv[c].ap, ACT.Silu, t, mfree["uc"]))
                cv[c].free = [u[c]]
            mfree["up"] = [t]
            yield 1
            p0 = ps[0]
            for h in range(2):
                for c in range(2):
                    m = mm(p0[0:104, 512 * h:512 * h + 512], small["wx"][:, c, :], uc[:, c, 512 * h:512 * h + 512],
                           c == 0, c == 1, u[c], B[0].free, B[1].free)
                    yield 0.9
            r1 = big.take()
            rr = r1.ap[0:96, :]
            hi = cp(bc[:, 1, :], p0[0:96, :], m, mfree["bc"])
            dtb = big.take()
            dt = act(dtb.ap[96:104, :], p0[96:104, :], ACT.Copy, m, dtb.free)
            x1 = tt(rr, p0[0:96, :], bc[:, 1, :], ALU.subtract, hi, r1.free)
            B[0].free = B[1].free = [x1, dt]
            yield 2.2
            mid = cp(bc[:, 2, :], rr, x1)
            lo = tt(bc[:, 0, :], rr, bc[:, 2, :], ALU.subtract, mid)
            r1.free = [lo]
            yield 2
            f1 = cp(bc[32:64, 0, :], bc[32:64, 2, :], lo)
            bcok = [cp(bc[0:32, 0, :], bc[0:32, 1, :], f1)]
            dts = []
            vs, es = [], []
            for c in range(2):
                pp = ps[1 - c]
                bb = B[2 - 2 * c:4 - 2 * c]
                for h in range(2):
                    m = mm(pp[:, 512 * h:512 * h + 512], wdt[96:104, 128 * c:128 * c + 128],
                           dtb.ap[96:104, 512 * h:512 * h + 512], True, True, dt, bb[0].free, bb[1].free)
                v, e = big.take(), big.take()
                bd = small["bdt"][:, c:c + 1]
                t1 = act(v.ap, pp[:, :], ACT.Identity, m, v.free, bias=bd)
                t2 = act(e.ap, pp[:, :], ACT.Abs, m, e.free, bias=bd)
                bb[0].free = bb[1].free = [t2]
                vs.append((v, t1))
                es.append((e, t2))
                yield 2
            dtb.free = [m]
            yield 2
            es = [(e, act(e.ap, e.ap, ACT.Exp, t, scale=-1.0)) for e, t in es]
            us = [big.take() for _ in range(2)]
            ls = [big.take() for _ in range(2)]
            u1 = [ts(us[c].ap, es[c][0].ap, 1.0, None, ALU.add, None, es[c][1], us[c].free) for c in range(2)]
            ll = [act(ls[c].ap, us[c].ap, ACT.Ln, u1[c], ls[c].free) for c in range(2)]
            t = [stt(us[c].ap, us[c].ap, -1.0, es[c][0].ap, ALU.add, ALU.subtract, u1[c], ll[c])
                 for c in range(2)]
            yield 4
            for c in range(2):
                es[c][0].free = [t[c]]
            t = [tt(us[c].ap, ls[c].ap, us[c].ap, ALU.subtract, t[c]) for c in range(2)]
            for c in range(2):
                ls[c].free = [t[c]]
            dd = [stt(dl[:, c, :], vs[c][0].ap, 0.0, us[c].ap, ALU.max, ALU.add, t[c], vs[c][1], mfree["dl"])
                  for c in range(2)]
            yield 4
            for c in range(2):
                vs[c][0].free = us[c].free = [dd[c]]
            dus = [tt(du[:, c, :], dl[:, c, :], uc[:, c, :], ALU.mult, dd[c]) for c in range(2)]
            yt = [None, None]

            def row(n, k):
                for h in range(2):
                    m = mm(ps[k][:, 512 * h:512 * h + 512], sel[:, 16 * k + n, :], bc[:, 0, 512 * h:512 * h + 512],
                           True, True, bcok, S_OK, B[2 * k].free, B[2 * k + 1].free)
                return m

            def decay(n):
                da = [big.take() for _ in range(2)]
                return da, [act(da[c].ap, dl[:, c, :], ACT.Exp, dd[c], da[c].free, A_OK,
                                scale=aneg[:, 16 * c + n:16 * c + n + 1]) for c in range(2)]

            mb, mc, (da, ta) = row(0, 0), row(0, 1), decay(0)
            yield 2.4
            for n in range(16):
                db = [big.take() for _ in range(2)]
                tb = [tt(db[c].ap, du[:, c, :], ps[0][:, :], ALU.mult, mb, dus[c], db[c].free) for c in range(2)]
                B[0].free = B[1].free = [tb[1]]

                def scan(c):
                    o, a0 = db[c].ap, da[c].ap
                    return add("dve", lambda e: e.tensor_tensor_scan(o, a0, o, 0.0, ALU.mult, ALU.add),
                               ta[c], tb[c])
                sc = [scan(c) for c in range(2)]
                for c in range(2):
                    da[c].free = [sc[c]]
                yield 2.3
                if n < 15:
                    mb, (da, ta) = row(n + 1, 0), decay(n + 1)
                yield 2.3
                if n == 0:
                    th = [tt(yy[:, c, :], db[c].ap, ps[1][:, :], ALU.mult, mc, sc[c], mfree["yy"])
                          for c in range(2)]
                    yt = th
                    for c in range(2):
                        db[c].free = [th[c]]
                else:
                    th = [tt(db[c].ap, db[c].ap, ps[1][:, :], ALU.mult, mc, sc[c]) for c in range(2)]
                    yt = [tt(yy[:, c, :], yy[:, c, :], db[c].ap, ALU.add, th[c], yt[c], q="pool")
                          for c in range(2)]
                    for c in range(2):
                        db[c].free = [yt[c]]
                B[2].free = B[3].free = [th[1]]
                yield 2.2
                if n < 15:
                    mc = row(n + 1, 1)
            mfree["bc"], mfree["dl"], mfree["du"] = [mc], [ta[1]], [tb[1]]
            t = [stt(yy[:, c, :], uc[:, c, :], small["dcol"][:, c:c + 1], yy[:, c, :], ALU.mult, ALU.add, yt[c])
                 for c in range(2)]
            mfree["uc"] = [t[1]]
            yield 4
            t = [tt(yy[:, c, :], yy[:, c, :], zs[:, c, :], ALU.mult, t[c], zt) for c in range(2)]
            yield 2
            mfree["zs"] = [t[1]]
            deps = []
            for j in range(8):
                for c in range(2):
                    m = mm(ps[0][:, 128 * j:128 * j + 128], yy[:, c, 128 * j:128 * j + 128],
                           small["woT"][:, c, :], c == 0, c == 1, t[c], B[0].free, B[1].free)
                deps.append(m)
                if j % 2:
                    yield 0.9
            mfree["yy"] = [m]
            yield 2
            yield from residual([ps[0][:, 128 * j:128 * j + 128] for j in range(8)], [deps[3]] * 4 + [deps[7]] * 4, b, B[0:2])
            done.add(b)
            yield 8

        w1 = WB[:, 0:4608].bitcast(F16).rearrange("p (a e f) -> p a e f", a=2, e=9)
        gw = sb("gw", [128, 2, 8], F16)
        w2 = WB[:, 4608:9216].rearrange("p (e f h) -> p e f h", e=9, f=4)
        HR = sb("HR", [128, 4096])
        OS = sb("OS", [128, 256])
        hr = Ring([HR[:, 512 * i:512 * i + 512] for i in range(8)])
        acc_r = Ring([sb(f"acc{i}", [128, 8, 128]) for i in range(1)])
        gbuf = Ring([sb(f"g{i}", [128, 8, 64]) for i in range(1)])
        gidx = Ring([sb(f"gi{i}", [128, 8, 8], U32) for i in range(2)])
        combT = sb("combT", [9, 1024])
        cfree = []

        def top2(lg, deps, out0, out1, mx, g8, free):
            gi = gidx.take()
            lt = []
            a = [add("dve", (lambda j: lambda e: e.max(mx[:, j, :], lg[:, j, :]))(j), deps, free)
                 for j in range(8)]
            lt = [add("dve", (lambda j: lambda e: e.max_index(gi.ap[:, j, :], mx[:, j, :], lg[:, j, :]))(j),
                      a[j], gi.free) for j in range(8)]
            f = cp(g8, gi.ap[:, :, :], lt)
            gi.free = [f]
            io = iota8[:, :].rearrange("p (o e) -> p o e", o=1).to_broadcast([128, 8, 8])
            r0 = tt(out0, io, g8[:, :, 0:1].to_broadcast([128, 8, 8]), ALU.is_equal, f, K)
            r1 = tt(out1, io, g8[:, :, 1:2].to_broadcast([128, 8, 8]), ALU.is_equal, f)
            return r0, r1, a

        def moe(b):
            MB, YB = bank[4:6], bank[6:8]
            while b not in done:
                yield 1
            s = ln_buf.take()
            o = yield from layernorm(tiles_of(b), [xtok[b]] * 8, [s.ap[:, j, :] for j in range(8)], s.free)
            yield 6
            xs = xT_ring.take()
            xp = xs.ap.bitcast(F16).rearrange("p (a t) -> p a t", a=2)
            xt, last = transposes_split([s.ap[:, j, :] for j in range(8)], o, xp, xs.free, MB)
            s.free = [last]
            yield 2
            bk = YB[0]
            for j in range(8):
                c = slice(128 * j, 128 * j + 128)
                m = product(bk.ap[:, 8 * j:8 * j + 8], (xp[:, 0, c], xp[:, 1, c]), (gw[:, 0, :], gw[:, 1, :]), True,
                            True, xt, WF, bk.free)
            gs = gbuf.take()
            g = gs.ap
            G = lambda i: g[:, :, 8 * i:8 * i + 8]
            lg = ts(G(0), bk.ap[:, 0:64].rearrange("p (j e) -> p j e", e=8), BACK, None, ALU.mult, None, m, gs.free)
            bk.free = [lg]
            yield 2
            t0, t1, a = top2(G(0), lg, G(2), G(3), G(1), G(4), gs.free)
            r = tt(G(5)[:, :, 0:1], G(1)[:, :, 1:2], G(1)[:, :, 0:1], ALU.subtract, a)
            r = act(G(5)[:, :, 1:2], G(5)[:, :, 0:1], ACT.Exp, r)
            yield 3
            r1 = ts(G(5)[:, :, 2:3], G(5)[:, :, 1:2], 1.0, None, ALU.add, None, r)
            r2 = recip(G(5)[:, :, 3:4], G(5)[:, :, 2:3], r1)
            r3 = tt(G(5)[:, :, 4:5], G(5)[:, :, 3:4], G(5)[:, :, 1:2], ALU.mult, r2)
            c1 = tt(G(2), G(2), G(5)[:, :, 3:4].to_broadcast([128, 8, 8]), ALU.mult, r2, t0)
            c2 = tt(G(3), G(3), G(5)[:, :, 4:5].to_broadcast([128, 8, 8]), ALU.mult, r3, t1)
            c3 = tt(G(6), G(2), G(3), ALU.add, c1, c2)
            c4 = fill(G(7), 1.0, gs.free)
            comb = g[:, :, 48:57]
            for h in range(2):
                bk = YB[h]
                for j in range(4):
                    m = tr(bk.ap[0:9, 128 * j:128 * j + 128], comb[:, 4 * h + j, :], ident[:, :], c3, c4, bk.free)
                ct = act(combT[:, 512 * h:512 * h + 512], bk.ap[0:9, :], ACT.Copy, m, cfree)
                bk.free = [ct]
            yield 2
            ac = acc_r.take()
            accs = [None] * 8
            plan = [(h, e) for h in range(2) for e in (8, 0, 1, 2, 3, 4, 5, 6, 7)]

            def down(k):
                h, e = plan[k]
                hs, bk = hid.pop(k), YB[k % 2]
                for j in range(4):
                    o = bk.ap[:, 128 * j:128 * j + 128]
                    if e == 8:
                        mm(o, combT[:, 512 * h + 128 * j:512 * h + 128 * j + 128], b2[:, :], True, False, ct,
                           bk.free)
                    for f in range(4):
                        m = mm(o, hs[f][0].ap[:, 128 * j:128 * j + 128], w2[:, e, f, :], f == 0 and e != 8, f == 3,
                               hs[f][1], bk.free)
                    if j < 3:
                        yield 1.3
                for f in range(4):
                    hs[f][0].free = [m]
                got[k] = m

            def combine(k):
                h, e = plan[k]
                bk, m = YB[k % 2], got[k]
                if e == 8:
                    t = act(ac.ap[:, 4 * h:4 * h + 4, :], bk.ap.rearrange("p (j c) -> p j c", c=128), ACT.Copy,
                            m, ac.free)
                    for j in range(4):
                        accs[4 * h + j] = t
                else:
                    for j in range(4):
                        J = 4 * h + j
                        t = accs[J] = stt(ac.ap[:, J, :], bk.ap[:, 128 * j:128 * j + 128],
                                          G(6)[:, J, e:e + 1], ac.ap[:, J, :], ALU.mult, ALU.add, m, accs[J], c3)
                bk.free = [t]

            hid, got = {}, {}
            for k, (h, e) in enumerate(plan + [(None, None)] * 2):
                if k < 18:
                    hid[k] = []
                    for f in range(4):
                        bk = MB[f % 2]
                        c, x = slice(128 * f, 128 * f + 128), slice(512 * h, 512 * h + 512)
                        m = product(bk.ap, (w1[:, 0, e, c], w1[:, 1, e, c]), (xp[:, 0, x], xp[:, 1, x]), True, True,
                                    xt[h], bk.free, WF, W_F)
                        hb = hr.take()
                        t = act(hb.ap, bk.ap, ACT.Gelu, m, hb.free, bias=small["b1"][:, e, f:f + 1], scale=BACK)
                        bk.free = [t]
                        hid[k].append((hb, t))
                        yield 0.9
                    xs.free = [m]
                if k > 1:
                    combine(k - 2)
                if 1 <= k <= 18:
                    yield from down(k - 1)
                yield 1.3
            md = got[17]
            cfree[:] = [md]
            yield from residual([ac.ap[:, j, :] for j in range(8)], accs, b, [ac])
            gs.free = [accs[-1]]
            yield 6

        WA = {}
        wqk = WB[:, 0:1024]
        wv = WB[:, 1024:1536]
        wout = WB[:, 1536:2048].rearrange("p (c n) -> p c n", c=4)
        lsc = sb("lsc", [128, 8])

        def attention_setup():
            j1 = tt(BIG[:, 0:32], lam[:, 0, :], lam[:, 1, :], ALU.mult, K, [s.free for s in big.slots])
            j2 = tt(BIG[:, 32:64], lam[:, 2, :], lam[:, 3, :], ALU.mult)
            r1 = red(lsc[:, 0:1], BIG[:, 0:32], ALU.add, j1)
            r2 = red(lsc[:, 1:2], BIG[:, 32:64], ALU.add, j2)
            x = act(lsc[:, 2:4], lsc[:, 0:2], ACT.Exp, r1, r2)
            y = tt(lsc[:, 4:5], lsc[:, 3:4], lsc[:, 2:3], ALU.subtract, x)
            z = ts(lsc[:, 5:6], lsc[:, 4:5], -LAMBDA_INIT, None, ALU.add, None, y)
            w = ts(wout, wout, small["gam"][:, 0:1], 1.0 - LAMBDA_INIT, ALU.mult, ALU.mult, WA["w"])
            WA["lam"], WA["wout"] = z, w
            WA["free"] = [r1, r2]

        def score_operands(b, g):
            xs, xt = WA["x", b]
            st = WA["stack"].take()
            st.ready = []
            for w in range(2):
                hl = WA["hl"].take()
                hi, lo = hl.ap[:, 0, :], hl.ap[:, 1, :]
                tl = []
                sc = 32 ** -0.5 if w == 0 else 1.0
                for h in range(2):
                    bk = WA["ob"].take()
                    m = mm(bk.ap, wqk[:, 512 * w + 128 * g:512 * w + 128 * g + 128],
                           xs.ap[:, 512 * h:512 * h + 512], True, True, xt[h], bk.free, WA["w"])
                    t1 = act(hi[:, 512 * h:512 * h + 512], bk.ap, ACT.Copy, m, hl.free, scale=sc)
                    yield
                    t2 = stt(lo[:, 512 * h:512 * h + 512], bk.ap, sc, hi[:, 512 * h:512 * h + 512], ALU.mult,
                             ALU.subtract, t1)
                    bk.free = [t2]
                    tl += [t1, t2]
                    if h == 0:
                        yield
                for hh in range(4):
                    for r in range(3):
                        part = lo if r == 2 - w else hi
                        dm = dma(st.ap[32 * r:32 * r + 32, w, hh, :], part[32 * hh:32 * hh + 32, :],
                                 WA["dsem"][st.k][w], tl, st.free)
                hl.free = [dm]
                st.ready.append(dm)
                yield
            V = WA["V"].take()
            V.ready = []
            for h in range(2):
                bk = WA["ob"].take()
                for j in range(4):
                    m = mm(bk.ap[:, 128 * j:128 * j + 128], xs.ap[:, 512 * h + 128 * j:512 * h + 128 * j + 128],
                           wv[:, 128 * g:128 * g + 128], True, True, xt, bk.free)
                t = act(V.ap[:, 4 * h:4 * h + 4, :], bk.ap.rearrange("p (j n) -> p j n", j=4), ACT.Copy, m, V.free)
                bk.free = [t]
                V.ready.append(t)
                yield
                if h == 0:
                    yield
            if g == 3:
                xs.free = [m]
            WA["ops", b, g] = (st, V)

        def attention_norm(b):
            s = ln_buf.take()
            src = tiles_of(b)
            sr = st_ring.take()
            st, fr = sr.ap, sr.free
            a = []
            for j in range(8):
                a.append(add("dve", (lambda j: lambda e: e.bn_stats(st[:, j, 0:6], src[j]))(j), xtok[b], fr))
            yield
            g = [add("dve", (lambda j: lambda e: e.bn_aggr(st[:, j, 6:8], st[:, j, 0:6]))(j), a[j])
                 for j in range(8)]
            e1 = ts(st[:, :, 8:9], st[:, :, 7:8], 1e-5, None, ALU.add, None, g[-1], q="pool")
            e2 = tt(st[:, :, 9:10], st[:, :, 8:9], half[:, 0, 0:8].rearrange("p (n o) -> p n o", o=1),
                    ALU.pow, e1, H0, q="pool")
            yield
            o = [ts(s.ap[:, j, :], src[j], st[:, j, 6:7], st[:, j, 9:10], ALU.subtract, ALU.mult, e2, s.free)
                 for j in range(8)]
            sr.free = [o[-1]]
            WA["n", b] = (s, o)
            yield

        def attention_turn(b):
            s, o = WA["n", b]
            xs = xT_ring.take()
            xt = []
            for h in range(2):
                bk = WA["ob"].take()
                t = [tr(bk.ap[:, 128 * j:128 * j + 128], s.ap[:, 4 * h + j, :], ident[:, :], o[4 * h + j], K,
                        bk.free) for j in range(4)]
                xt.append(act(xs.ap[:, 512 * h:512 * h + 512], bk.ap, ACT.Copy, t[-1], xs.free))
                bk.free = [xt[-1]]
                yield
                if h == 0:
                    yield
            s.free = [t[-1]]
            WA["x", b] = (xs, xt)

        def preparation():
            def at(u, g):
                yield u
                for _ in g:
                    yield 0

            yield from at(0, attention_norm(0))
            yield from at(0, attention_turn(0))
            yield from at(0, score_operands(0, 0))
            for b in range(NB):
                for g in range(1, 4):
                    yield from at(64 * b + 16 * (g - 1), score_operands(b, g))
                    if g > 1 and b + 1 < NB:
                        yield from at(0, attention_norm(b + 1) if g == 2 else attention_turn(b + 1))
                if b + 1 < NB:
                    yield from at(64 * b + 48, score_operands(b + 1, 0))

        def attention_tail(b, O, ot):
            o = O.ap
            y = acc_r.take()
            deps, q = [], {}

            def a0(i):
                sq = WA["sq"].take()
                q[i] = [sq, tt(sq.ap, o[:, i, :], o[:, i, :], ALU.mult, ot[i], sq.free, q="pool")]

            def a1(i):
                rb = WA["rb"].take()
                sq, t = q[i]
                t = red(rb.ap[:, 0, :], sq.ap.rearrange("p (h d) -> p h d", d=64), ALU.add, t, rb.free)
                sq.free = [t]
                t = ts(rb.ap[:, 1, :], rb.ap[:, 0, :], 1.0 / 64, None, ALU.mult, None, t, q="pool")
                t = tt(rb.ap[:, 2, :], rb.ap[:, 1, :], half[:, 1, 0:8], ALU.pow, t, H1, q="pool")
                t = ts(rb.ap[:, 3, :], rb.ap[:, 2, :], 1e-8, None, ALU.add, None, t, q="pool")
                q[i] = [rb, t]

            def a2(i):
                rb, t = q[i]
                t = recip(rb.ap[:, 4, :], rb.ap[:, 3, :], t)
                t = tt(o[:, i, :].rearrange("p (h d) -> p h d", d=64), o[:, i, :].rearrange("p (h d) -> p h d", d=64),
                       rb.ap[:, 4, :].rearrange("p (h o) -> p h o", o=1).to_broadcast([128, 8, 64]), ALU.mult, t)
                rb.free = [t]
                q[i] = t

            def a3(i):
                os = WA["oT"].take()
                bk = WA["ob"].take()
                for c in range(4):
                    x = tr(bk.ap[:, 128 * c:128 * c + 128], o[:, i, 128 * c:128 * c + 128], ident[:, :], q[i], bk.free)
                tk = act(os.ap, bk.ap, ACT.Copy, x, os.free)
                bk.free = [tk]
                q[i] = [os, tk, x]

            def a4(i):
                os, tk, x = q[i]
                bk = WA["ob"].take()
                for c in range(4):
                    m = mm(bk.ap[:, 0:128], os.ap[:, 128 * c:128 * c + 128], wout[:, c, :], c == 0, c == 3, tk,
                           WA["wout"], bk.free)
                os.free = [m]
                deps.append(act(y.ap[:, i, :], bk.ap[:, 0:128], ACT.Copy, m, y.free))
                bk.free = [deps[-1]]
                q[i] = x
            for k in range(8 + 4):
                if k < 8:
                    yield k, False
                    a0(k)
                if 0 <= k - 1 < 8:
                    yield 0, False
                    a1(k - 1)
                if 0 <= k - 2 < 8:
                    yield 0, False
                    a2(k - 2)
                if 0 <= k - 3 < 8:
                    yield 0, True
                    a3(k - 3)
                if 0 <= k - 4 < 8:
                    yield 0, True
                    a4(k - 4)
            O.free = [q[7]]
            yield 0, False
            for _ in residual([y.ap[:, j, :] for j in range(8)], deps, b, [y]):
                yield 0, False

        def attention():
            units = [(b, g, i, pp) for b in range(NB) for g in range(4) for i in range(8) for pp in range(2)]
            per = 64
            O, ots, extra, rec = {}, {}, [], {}

            def scores(n, s_):
                b, g, i, pp = units[n]
                r = rec[n]
                st, L = r["st"], r["L"].ap
                hh = 2 * pp + s_
                Sp = ps[s_]
                b0, b1 = bank[2 * s_], bank[2 * s_ + 1]
                for h in range(2):
                    m = mm(Sp[:, 512 * h:512 * h + 512], st.ap[0:96, 0, hh, 128 * i:128 * i + 128],
                           st.ap[0:96, 1, hh, 512 * h:512 * h + 512], True, True, st.ready, b0.free, b1.free)
                mx = red(L[:, 2 * s_ + pp:2 * s_ + pp + 1], Sp[:, :], ALU.max, m, r["L"].free, negate=True)
                pb = WA["P"].take()
                t = act(pb.ap, Sp[:, :], ACT.Exp, mx, pb.free, bias=L[:, 2 * s_ + pp:2 * s_ + pp + 1],
                        acc=L[:, 4 + 2 * s_ + pp:5 + 2 * s_ + pp])
                b0.free = b1.free = [t]
                st.free = [m]
                r["P"].append(pb)
                r["e"].append(t)

            def sums(n):
                r, q = rec[n], rec[n - 1]
                L = r["L"].ap
                r["r"] = q["r"] = recip(L[:, 8:12], L[:, 4:8], r["e"], q["e"])
                c = tt(L[:, 12:14], L[:, 4:6], L[:, 10:12], ALU.mult, r["r"], q="pool")
                r["c"] = q["c"] = ts(L[:, 14:16], L[:, 12:14], lsc[:, 5:6], None, ALU.mult, None, c, WA["lam"],
                                     q="pool")

            def difference(n):
                r = rec[n]
                L, P, pp = r["L"].ap, r["P"], n % 2
                a, z, c = P[0].ap, P[1].ap, L[:, 14 + pp:15 + pp]
                x = ts(z[:, W:1024], z[:, W:1024], c, None, ALU.mult, None, r["c"], q="pool")
                x = tt(a[:, W:1024], a[:, W:1024], z[:, W:1024], ALU.add, x, q="pool")
                y = stt(a[:, 0:W], z[:, 0:W], c, a[:, 0:W], ALU.mult, ALU.add, r["c"])
                P[1].free = [x, y]
                r["D"] = [y] * (W // 128) + [x] * (8 - W // 128)

            def turn(n):
                r = rec[n]
                D = r["P"][0].ap
                dt_ = r["DT"] = WA["DT"].take()
                for k in range(8):
                    x = tr(ps[2][:, 128 * k:128 * k + 128], D[:, 128 * k:128 * k + 128], ident[:, :], r["D"][k],
                           bank[4].free, bank[5].free)
                e = act(dt_.ap, ps[2][:, :], ACT.Copy, x, dt_.free)
                bank[4].free = bank[5].free = [e]
                r["tk"] = e
                r["P"][0].free = [x]

            def weigh(n):
                b, g, i, pp = units[n]
                r = rec[n]
                V = r["V"]
                ob = bank[6]
                for k in range(8):
                    y = mm(ob.ap[64 * pp:64 * pp + 64, 0:128], V.ap[:, k, 64 * pp:64 * pp + 64],
                           r["DT"].ap[:, 128 * k:128 * k + 128], k == 0, k == 7, r["tk"], V.ready, ob.free)
                r["DT"].free = [y]
                r["y"] = y
                V.free = [y]

            def gather(n):
                os = WA["os"].take()
                e = act(os.ap, bank[6].ap[:, 0:128], ACT.Copy, rec[n]["y"], rec[n - 1]["y"], os.free)
                bank[6].free = [e]
                rec[n]["os"] = (os, e)

            def settle(n):
                b, g, i, pp = units[n]
                r = rec.pop(n)
                rec.pop(n - 1)
                if n % per == 1:
                    O[b], ots[b] = WA["O"][b % 2], {}
                bk = WA["ob"].take()
                os, e = r["os"]
                x = tr(bk.ap[:, 0:128], os.ap, ident[:, :], e, bk.free)
                os.free = [x]
                z = tt(O[b].ap[:, i, 128 * g:128 * g + 128].rearrange("p (a d) -> p a d", a=2),
                       bk.ap[:, 0:128].rearrange("p (a d) -> p a d", a=2),
                       r["L"].ap[:, 8:10].rearrange("p (a o) -> p a o", o=1).to_broadcast([128, 2, 64]), ALU.mult,
                       x, r["r"], O[b].free)
                bk.free = [z]
                r["L"].free = [z]
                ots[b][i] = z
                if g == 3:
                    settled[b] = i + 1
                    if i == 0:
                        e = attention_tail(b, O[b], ots[b])
                        extra.append([b, e, next(e)])

            N = len(units)
            W, TL = 640, 4
            settled = {}
            prep = preparation()
            want = 0

            def advance(n):
                nonlocal want
                if want is None or want > n:
                    return False
                want = next(prep, None)
                return True

            def tail(odd):
                if not extra:
                    return
                b, g, (i, ob) = extra[0]
                if settled[b] <= i and i or (ob and not odd):
                    return
                v = next(g, None)
                if v is None:
                    extra.pop(0)
                else:
                    extra[0][2] = v

            for n in range(N + 8):
                if 0 <= n - 6 < N and n % 2 == 1:
                    gather(n - 6)
                if n < N:
                    b, g, i, pp = units[n]
                    if i == 0 and pp == 0:
                        while ("ops", b, g) not in WA:
                            assert advance(n)
                        st, V = WA["ops", b, g]
                    rec[n] = {"st": st, "V": V, "L": WA["l"].take() if pp == 0 else rec[n - 1]["L"], "P": [], "e": []}
                    scores(n, 0)
                if 0 <= n - 1 < N and n % 2 == 0:
                    sums(n - 1)
                if 0 <= n - TL < N:
                    turn(n - TL)
                if n < N:
                    scores(n, 1)
                if 0 <= n - 7 < N and n % 2 == 0:
                    settle(n - 7)
                if 0 <= n - TL - 1 < N:
                    weigh(n - TL - 1)
                if 0 <= n - 2 < N:
                    difference(n - 2)
                advance(n)
                tail(n % 2 == 1)
                if n % 64 < 8 or n % 64 > 52:
                    tail(n % 2 == 1)
            assert want is None
            WA["ob"].slots = [bank[i] for i in (7, 0, 1, 2, 3)]
            while extra:
                tail(True)

        wqkv3 = WB[:, 0:3072].bitcast(F16).rearrange("p (k a e h) -> p k a e h", k=2, a=3, e=8)
        wo3 = WB[:, 3072:4096].rearrange("p (e h) -> p e h", e=8)
        w13 = WB[:, 4096:5120].rearrange("p (e h) -> p e h", e=8)
        w23 = WB[:, 5120:6144].rearrange("p (e h) -> p e h", e=8)
        simn = sb("simn", [128, 2, 8])
        sgm = sb("sgm", [128, 2, 8])
        ones = sb("ones", [128, 128])
        WD = {}
        ones_t = fill(ones[:, :], 1.0)

        def experts_setup():
            sq = tt(lsq[:, 0:16], small["sims"][:, :, :].rearrange("p a e -> p (a e)"),
                    small["sims"][:, :, :].rearrange("p a e -> p (a e)"), ALU.mult, K)
            m = mm(bank[0].ap[:, 0:16], ones[:, :], lsq[:, 0:16], True, True, sq, ones_t, bank[0].free)
            a = act(lsq[:, 16:32], bank[0].ap[:, 0:16], ACT.Copy, m)
            bank[0].free = [a]
            p = tt(lsq[:, 32:48], lsq[:, 16:32], half[:, 1, 0:16], ALU.pow, a, H1, q="pool")
            q_ = ts(lsq[:, 48:64], lsq[:, 32:48], 1e-12, None, ALU.max, None, p)
            r = recip(lsq[:, 32:48], lsq[:, 48:64], q_)
            WD["sim"] = tt(simn[:, :, :].rearrange("p a e -> p (a e)"),
                           small["sims"][:, :, :].rearrange("p a e -> p (a e)"), lsq[:, 32:48], ALU.mult, r)
            e1 = act(sgm[:, :, :].rearrange("p a e -> p (a e)"), gts[:, :, :].rearrange("p a e -> p (a e)"), ACT.Exp,
                     K, scale=-1.0)
            e2 = ts(sgm[:, :, :], sgm[:, :, :], 1.0, None, ALU.add, None, e1)
            WD["sgm"] = recip(sgm[:, :, :], sgm[:, :, :], e2)

        lsq = sb("lsq", [128, 64])

        def affine_ln(src, deps, w, dst, free):
            o = yield from layernorm(src, deps, [dst[:, j, :] for j in range(8)], free)
            wb = lnp[:, w:w + 1, :].to_broadcast([128, 8, 128])
            bb = lnp[:, w + 1:w + 2, :].to_broadcast([128, 8, 128])
            t = tt(dst, dst, wb, ALU.mult, o, K)
            return tt(dst, dst, bb, ALU.add, t)

        def gating(n1, dep, n1T, dT, which, bk, gs, scratch):
            g = gs.ap
            G = lambda i: g[:, :, 8 * i:8 * i + 8]
            sq = tt(scratch.ap.rearrange("p (j c) -> p j c", c=128), n1, n1, ALU.mult, dep, scratch.free, q="pool")
            yield 3
            r = red(G(7)[:, :, 0:1], scratch.ap.rearrange("p (j c) -> p j c", c=128), ALU.add, sq, gs.free)
            scratch.free = [r]
            yield 3
            r = tt(G(7)[:, :, 1:2], G(7)[:, :, 0:1], half[:, 1, 0:8].rearrange("p (n o) -> p n o", o=1), ALU.pow, r,
                   H1, q="pool")
            r = ts(G(7)[:, :, 2:3], G(7)[:, :, 1:2], 1e-12, None, ALU.max, None, r)
            r = recip(G(7)[:, :, 3:4], G(7)[:, :, 2:3], r)
            for j in range(8):
                m = mm(bk.ap[:, 8 * j:8 * j + 8], n1T[:, 128 * j:128 * j + 128], simn[:, which, :], True, True,
                       dT, bk.free, WD["sim"])
            l1 = tt(G(0), bk.ap[:, 0:64].rearrange("p (j e) -> p j e", e=8),
                    G(7)[:, :, 3:4].to_broadcast([128, 8, 8]), ALU.mult, m, r)
            bk.free = [l1]
            WD["logits"] = m
            l2 = tt(G(0), G(0), sgm[:, which:which + 1, :].to_broadcast([128, 8, 8]), ALU.subtract, l1, WD["sgm"])
            t0, t1, a = top2(G(0), l2, G(2), G(3), G(1), G(4), gs.free)
            oh = tt(G(2), G(2), G(3), ALU.add, t0, t1)
            ina = ts(G(7)[:, :, 4:5], G(1)[:, :, 0:1], 0.0, None, ALU.is_le, None, a)
            po = tt(G(2), G(2), G(7)[:, :, 4:5].to_broadcast([128, 8, 8]), ALU.mult, oh, ina)
            mk = ts(G(3), G(0), 0.0, None, ALU.is_gt, None, oh)
            mk = tt(G(3), G(3), G(2), ALU.add, mk, po)
            mx = ts(G(7)[:, :, 5:6], G(1)[:, :, 0:1], 0.0, None, ALU.max, None, a)
            e = ts(G(4), G(0), 0.0, None, ALU.max, None, t0, t1)
            e = tt(G(4), G(4), G(7)[:, :, 5:6].to_broadcast([128, 8, 8]), ALU.subtract, e, mx)
            e = act(G(5), G(4), ACT.Exp, e)
            yield 2
            e = tt(G(5), G(5), G(3), ALU.mult, e, mk)
            sm = red(G(7)[:, :, 6:7], G(5), ALU.add, e)
            sm = recip(G(7)[:, :, 7:8], G(7)[:, :, 6:7], sm)
            return G(6), tt(G(6), G(5), G(7)[:, :, 7:8].to_broadcast([128, 8, 8]), ALU.mult, sm)

        def soft(b, k):
            R = WD["stream"][k]
            hs, n1, q1, k1, v1, xs, gs, L = (R[x] for x in ("hs", "n1", "q", "k", "v", "xT", "g", "L"))
            B, S0, S1 = bank[4 * k:4 * k + 4], ps[2 * k], ps[2 * k + 1]
            n1t = [n1.ap[:, j, :] for j in range(8)]
            hst = [hs.ap[:, j, :] for j in range(8)]
            o = yield from layernorm(tiles_of(b), [xtok[b]] * 8, hst, hs.free)
            yield 2
            t1 = yield from affine_ln(hst, o, 0, n1.ap, n1.free)
            yield 3
            xt, last = transposes(n1t, [t1] * 8, xs, B[0:2])
            yield 2
            rw, rt = yield from gating(n1.ap, t1, xs.ap, xt, 0, B[2], gs, big.take())
            xs.free = [WD["logits"]]
            yield 3
            for h in range(2):
                qb, kb, vb = B[0:3]

                def scaled(e):
                    sc = R["sc"].take()
                    ss = tt(sc.ap.rearrange("p (j c) -> p j c", c=128), n1.ap[:, 4 * h:4 * h + 4, :],
                            rw[:, 4 * h:4 * h + 4, e:e + 1].to_broadcast([128, 4, 128]), ALU.mult, rt, t1, sc.free,
                            q="pool")
                    sT = R["sT"].take()
                    p = sT.ap.bitcast(F16).rearrange("p (a t) -> p a t", a=2)
                    tk, last = transposes_split([sc.ap[:, 128 * j:128 * j + 128] for j in range(4)], [ss] * 4, p,
                                                sT.free, [B[3]])
                    sc.free = [last]
                    return sT, p, tk

                nxt = scaled(0)
                yield 1
                for e in range(8):
                    sT, p, tk = nxt
                    x = (p[:, 0, :], p[:, 1, :])
                    w = lambda a: (wqkv3[:, 0, a, e, :], wqkv3[:, 1, a, e, :])
                    if e < 7:
                        nxt = scaled(e + 1)
                    product(qb.ap, w(0), x, e == 0, e == 7, tk, WD["wqkv"], qb.free)
                    yield 0.9
                    mk_ = product(kb.ap, w(1), x, e == 0, e == 7, kb.free)
                    yield 0.9
                    for j in range(4):
                        for q_, (k_, l_) in enumerate(((0, 0), (0, 1), (1, 0))):
                            mv = add("pe", (lambda o, s_, w_, st, sp: lambda en: en.matmul(
                                o, s_, w_, start=st, stop=sp, skip_group_check=True))(
                                vb.ap[:, 128 * j:128 * j + 128], p[:, k_, 128 * j:128 * j + 128],
                                wqkv3[:, l_, 2, e, :], (e, j, q_) == (0, 0, 0), (e, q_) == (7, 2)), vb.free)
                    sT.free = [mv]
                    yield 1.35
                tq = act(q1.ap[:, 512 * h:512 * h + 512], qb.ap, ACT.Copy, mk_, q1.free,
                         scale=128 ** -0.5 * BACK)
                tk_ = act(k1.ap[:, 512 * h:512 * h + 512], kb.ap, ACT.Copy, mk_, k1.free, scale=BACK)
                tv = act(v1.ap[:, 4 * h:4 * h + 4, :], vb.ap.rearrange("p (j c) -> p j c", c=128), ACT.Copy, mv,
                         v1.free, scale=BACK)
                qb.free, kb.free, vb.free = [tq], [tk_], [tv]
            qk = [tq, tk_]
            lf = R["Lfree"]
            atk = []
            b0, b1 = B[0:2]

            def scores(i):
                w = 128 * (i + 1)
                for h in range((w + 511) // 512):
                    ww = min(512, w - 512 * h)
                    m = mm(S0[:, 512 * h:512 * h + ww], q1.ap[:, 128 * i:128 * i + 128],
                           k1.ap[:, 512 * h:512 * h + ww], True, True, qk, b0.free, b1.free)
                return m

            rl = {}

            def weighed(i):
                z = ts(n1.ap[:, i, :], B[3].ap[:, 0:128], L[:, 24 + i:25 + i], None, ALU.mult, None, y, rl[i])
                B[3].free = [z]
                atk.append(z)

            m = scores(0)
            for i in range(8):
                w = 128 * (i + 1)
                dg = tt(S0[:, 128 * i:128 * i + 128], S0[:, 128 * i:128 * i + 128], tri[:, :], ALU.add, m)
                mx = red(L[:, i:i + 1], S0[:, 0:w], ALU.max, dg, lf, negate=True)
                pb = WD["P"].take()
                t = act(pb.ap[:, 0:w], S0[:, 0:w], ACT.Exp, mx, pb.free, bias=L[:, i:i + 1],
                        acc=L[:, 16 + i:17 + i])
                b0.free = b1.free = [t]
                if i:
                    weighed(i - 1)
                yield 1.5
                if i < 7:
                    m = scores(i + 1)
                rl[i] = recip(L[:, 24 + i:25 + i], L[:, 16 + i:17 + i], t)
                pt = WD["PT"].take()
                tk, last = transposes([pb.ap[:, 128 * x:128 * x + 128] for x in range(i + 1)], [t] * (i + 1), pt,
                                      [B[2]])
                pb.free = [last]
                yield 1
                for x in range(i + 1):
                    y = mm(B[3].ap[:, 0:128], pt.ap[:, 128 * x:128 * x + 128], v1.ap[:, x, :], x == 0, x == i, tk, tv,
                           B[3].free)
                pt.free = [y]
                yield 1 + 0.2 * i
            weighed(7)
            q1.free = k1.free = [m]
            v1.free = [y]
            R["Lfree"] = [atk[-1]]
            xt, last = transposes(n1t, atk, xs, B[0:2])
            n1.free = [last]
            yield 1
            ht = [None] * 8
            om = {}
            for j in range(9):
                if j < 8:
                    pp = (S0, S1)[j % 2]
                    c0, c1 = B[2 * (j % 2):2 * (j % 2) + 2]
                    for h in range(2):
                        om[j] = mm(pp[:, 512 * h:512 * h + 512], xs.ap[:, 128 * j:128 * j + 128],
                                   wo3[:, 4 * h:4 * h + 4, :].rearrange("p e c -> p (e c)"), True, True, xt, WD["w"], c0.free,
                                   c1.free)
                        yield 0.9
                if j == 0:
                    continue
                j, m = j - 1, om[j - 1]
                pp = (S0, S1)[j % 2]
                c0, c1 = B[2 * (j % 2):2 * (j % 2) + 2]
                t = None
                for e in range(8):
                    t = stt(hs.ap[:, j, :], pp[:, 128 * e:128 * e + 128], rw[:, j, e:e + 1], hs.ap[:, j, :], ALU.mult,
                            ALU.add, m, t)
                c0.free = c1.free = [t]
                ht[j] = t
            xs.free = [m]
            gs.free = [t]
            t1 = yield from affine_ln(hst, ht, 2, n1.ap, n1.free)
            yield 3
            xt, last = transposes(n1t, [t1] * 8, xs, B[0:2])
            rw, rt = yield from gating(n1.ap, t1, xs.ap, xt, 1, B[2], gs, big.take())
            n1.free = [rt, last]
            yield 3
            accs = list(ht)
            plan = [(h, e) for h in range(2) for e in range(8)]
            hid, got = {}, {}
            for k in range(18):
                if k < 16:
                    h, e = plan[k]
                    bk = B[k % 2]
                    m = mm(bk.ap, w13[:, e, :], xs.ap[:, 512 * h:512 * h + 512], True, True, xt[h], bk.free)
                    hb = hr.take()
                    th = act(hb.ap, bk.ap, ACT.Gelu, m, hb.free)
                    bk.free = [th]
                    hid[k] = (hb, th)
                    xs.free = [m]
                if k > 1:
                    h, e = plan[k - 2]
                    bk = B[2 + k % 2]
                    for j in range(4):
                        J = 4 * h + j
                        accs[J] = t = stt(hs.ap[:, J, :], bk.ap[:, 128 * j:128 * j + 128], rw[:, J, e:e + 1],
                                          hs.ap[:, J, :], ALU.mult, ALU.add, got[k - 2], accs[J], rt, t1)
                    bk.free = [t]
                yield 0.8
                if 1 <= k <= 16:
                    h, e = plan[k - 1]
                    bk = B[2 + (k - 1) % 2]
                    hb, th = hid.pop(k - 1)
                    for j in range(4):
                        m2 = mm(bk.ap[:, 128 * j:128 * j + 128], hb.ap[:, 128 * j:128 * j + 128], w23[:, e, :], True,
                                True, th, bk.free)
                    hb.free = [m2]
                    got[k - 1] = m2
                yield 0.8
            gs.free = [accs[-1]]
            yield from residual(hst, accs, b, [hs])
            outs.append(dma(ov[:, 8 * b:8 * b + 8, :], X[:, 8 * b:8 * b + 8, :], s_o, xtok[b]))
            yield 3

        def run(g):
            for _ in g:
                pass

        def chain(*gs):
            for g in gs:
                yield from g

        def merge(*streams):
            live = [[t0, i, g] for i, (t0, g) in enumerate(streams)]
            while live:
                s = min(live)
                c = next(s[2], None)
                if c is None:
                    live.remove(s)
                else:
                    s[0] += c

        W_F = None
        w_sem, w2_sem = sem("w_sem"), sem("w2_sem")
        if "F" in phases:
            w1d = d["w1"].rearrange("p e f -> p (e f)")
            dma(HR[:, :], w1d[:, 0:4096], w_sem)
            last = dma(acc_r.slots[0].ap.rearrange("p j c -> p (j c)")[:, 0:512], w1d[:, 4096:4608], w_sem)
            WF = []
            for e in range(9):
                src = hr.slots[e].ap if e < 8 else acc_r.slots[0].ap.rearrange("p j c -> p (j c)")[:, 0:512]
                WF += split(w1[:, 0, e, :], w1[:, 1, e, :], src, WS, last, None)
                (hr.slots[e] if e < 8 else acc_r.slots[0]).free = [WF[-1]]
            WF += split(gw[:, 0, :], gw[:, 1, :], small["gwT"][:, :], WS, K, None)
            W_F = dma(WB[:, 4608:9216], d["w2"].rearrange("p e f h -> p (e f h)"), w2_sem)

        def barrier_tokens():
            return [q[-1] for k, q in queues.items() if k != "sp" and q]

        if "M" in phases and "F" in phases:
            merge((0, chain(*(mamba(b) for b in range(NB)))), (0, chain(*(moe(b) for b in range(NB)))))
        elif "M" in phases:
            run(chain(*(mamba(b) for b in range(NB))))
        elif "F" in phases:
            done.update(range(NB))
            run(chain(*(moe(b) for b in range(NB))))

        if "A" in phases:
            bt = barrier_tokens()
            w_sem2 = sem("w_sem2")
            dma(wqk, d["wqk"], w_sem2, bt)
            dma(wv, d["wv"], w_sem2)
            WA["w"] = dma(WB[:, 1536:2048], d["wout"].rearrange("p c n -> p (c n)"), w_sem2)
            WA["dsem"] = [[sem(f"dq{i}{j}") for j in range(2)] for i in range(2)]

            def sl(ap):
                s = Slot(ap)
                s.free = list(bt)
                return s

            def rg(aps):
                r = Ring([])
                r.slots = [sl(a) for a in aps]
                return r
            stv = [BIG[:, 4096 * i:4096 * i + 4096].bitcast(F16).rearrange("p (w h t) -> p w h t", w=2, h=4)
                   for i in range(2)]
            WA["stack"] = rg(stv)
            for i, x in enumerate(WA["stack"].slots):
                x.k = i
            WA["hl"] = rg([x.bitcast(F16).rearrange("p (a t) -> p a t", a=2)
                           for x in (BIG[:, 8192:9216], WB[:, 4096:5120])])
            WA["V"] = rg([WB[:, 2048 + 1024 * i:3072 + 1024 * i].rearrange("p (j n) -> p j n", j=8) for i in range(2)])
            WA["P"] = rg([WB[:, 6144 + 1024 * i:7168 + 1024 * i] for i in range(3)]
                         + [MA[:, 1024 * i:1024 * i + 1024] for i in range(3)]
                         + [SEL[:, 2048 * i:2048 * i + 2048].bitcast(F32) for i in range(2)]
                         + [WB[:, 5120:6144], BC[:, 0:2048].bitcast(F32)])
            WA["os"] = rg([OS[:, 128 * i:128 * i + 128] for i in range(2)])
            WA["DT"] = rg([MA[:, 3072 + 1024 * i:4096 + 1024 * i] for i in range(2)])
            WA["O"] = [sl(MA[:, 5120:9216].rearrange("p (i n) -> p i n", i=8)),
                       sl(HR[:, :].rearrange("p (i n) -> p i n", i=8))]
            WA["oT"] = rg([MA[:, 9216 + 512 * i:9728 + 512 * i] for i in range(2)])
            WA["sq"] = rg([MA[:, 10240 + 512 * i:10752 + 512 * i] for i in range(2)])
            WA["rb"] = rg([MA[:, 11264 + 40 * i:11304 + 40 * i].rearrange("p (a b) -> p a b", b=8) for i in range(3)])
            WA["l"] = rg([MA[:, 11904 + 16 * i:11920 + 16 * i] for i in range(8)])
            WA["ob"] = Ring([])
            WA["ob"].slots = [bank[7]]
            attention_setup()
            WA["stack"].slots[0].free += WA["free"]
            attention()

        if "D" in phases:
            bt = barrier_tokens()
            w_sem3 = sem("w_sem3")
            wq_sem = sem("wq_sem")
            raw = WB[:, 6144:9216]
            lw = dma(raw, d["wqkv3"].rearrange("p a e h -> p (a e h)"), wq_sem, bt)
            dma(WB[:, 3072:4096], d["wo3"].rearrange("p e h -> p (e h)"), w_sem3)
            dma(WB[:, 4096:5120], d["w13"].rearrange("p e h -> p (e h)"), w_sem3)
            WD["wqkv"] = []
            for a in range(3):
                k = slice(1024 * a, 1024 * a + 1024)
                WD["wqkv"] += split(*(wqkv3[:, y, a, :, :].rearrange("p e h -> p (e h)") for y in range(2)), raw[:, k],
                                    WS, lw, None)
            WD["w"] = dma(WB[:, 5120:6144], d["w23"].rearrange("p e h -> p (e h)"), w_sem3)

            def sl(ap):
                s = Slot(ap)
                s.free = list(bt)
                return s

            def rg(aps):
                r = Ring([])
                r.slots = [sl(a) for a in aps]
                return r
            for s in big.slots + hr.slots:
                s.free = s.free + list(bt)
            j8 = lambda ap: ap.rearrange("p (j c) -> p j c", c=128)
            big.slots = big.slots[0:2]
            at_ = lambda k: BIG[:, 1024 * k:1024 * k + 1024]
            WD["stream"] = []
            for k in range(2):
                m0 = 5120 * k
                r = {x: sl(MA[:, m0 + 1024 * i:m0 + 1024 * i + 1024]) for i, x in enumerate(("hs", "n1", "q", "k", "v"))}
                for x in ("hs", "n1", "v"):
                    r[x].ap = j8(r[x].ap)
                r["sc"] = rg([at_(2 + k)[:, 512 * i:512 * i + 512] for i in range(2)])
                r["sT"] = rg([at_(4 + k)[:, 512 * i:512 * i + 512] for i in range(2)])
                r["g"] = sl(at_(7)[:, 512 * k:512 * k + 512].rearrange("p (j n) -> p j n", j=8))
                r["L"] = at_(8)[:, 32 * k:32 * k + 32]
                r["Lfree"] = bt
                r["xT"] = xT_ring.slots[k]
                WD["stream"].append(r)
            WD["P"] = rg([WB[:, 6144:7168], WB[:, 7168:8192]])
            WD["PT"] = rg([WB[:, 8192:9216], at_(6)])
            for x in WD["P"].slots + WD["PT"].slots:
                x.free = x.free + WD["wqkv"]
            experts_setup()
            s_o = sem("s_o")
            ov = out.rearrange("(n p) c -> p n c", p=128)
            outs = []
            merge((0, chain(soft(0, 0), soft(2, 0))), (0, chain(soft(1, 1), soft(3, 1))))
        else:
            s_o = sem("s_o")
            ov = out.rearrange("(n p) c -> p n c", p=128)
            outs = [dma(ov[:, 8 * b:8 * b + 8, :], X[:, 8 * b:8 * b + 8, :], s_o, xtok[b]) for b in range(NB)]

        sems = {}
        for q, steps in queues.items():
            n = 0
            for s in steps:
                if s.sem is not None:
                    sems[id(s.sem)] = s.count = sems.get(id(s.sem), 0) + 16
                elif s.awaited:
                    n += 1
                    s.count = n

        block = ctx.enter_context(nc.Block())

        def play(q, e):
            seen = {}
            for s in queues[q]:
                need = {}
                for a in s.after:
                    k = a.sem if a.sem is not None else own[a.queue]
                    if a.count > need.get(id(k), (0,))[0]:
                        need[id(k)] = (a.count, k)
                for i, (v, k) in need.items():
                    if v > seen.get(i, 0):
                        e.wait_ge(k, v)
                        seen[i] = v
                ins = s.emit(e)
                if s.sem is not None:
                    ins.then_inc(s.sem, 16)
                elif s.awaited:
                    ins.then_inc(own[q], 1)

        @block.tensor
        def _(e):
            play("pe", e)

        @block.scalar
        def _(e):
            play("act", e)

        @block.vector
        def _(e):
            play("dve", e)

        @block.gpsimd
        def _(e):
            play("pool", e)

        @block.sync
        def _(e):
            play("sp", e)
            e.wait_ge(s_o, 16 * len(outs))


def layout(i):
    a = {k: np.asarray(v) for k, v in i.items()}
    asc = np.ascontiguousarray
    r = {}
    r["x"] = a["L0_attn_x"].reshape(NB * T, C)
    r["winT"] = a["L0_attn_W_in"].T
    r["convw"] = a["L0_attn_conv_w"].reshape(2, 128, 3).transpose(1, 0, 2)
    r["convb"] = a["L0_attn_conv_b"].reshape(2, 128).T
    wx = a["L0_attn_W_xproj"].reshape(40, 2, 128).transpose(2, 1, 0)
    r["wx"] = np.concatenate([wx[:, :, 0:32]] * 3 + [wx[:, :, 32:40]], axis=2)
    r["wdt"] = a["L0_attn_W_dt"].T
    r["bdt"] = a["L0_attn_b_dt"].reshape(2, 128).T
    r["alog"] = a["L0_attn_A_log"].reshape(2, 128, 16).transpose(1, 0, 2)
    r["dcol"] = a["L0_attn_D"].reshape(2, 128).T
    r["woT"] = a["L0_attn_W_out"].reshape(128, 2, 128).transpose(2, 1, 0)
    r["gwT"] = a["L0_ffn_gate_w"].T
    r["w1"] = np.concatenate([a["L0_ffn_W1"], a["L0_ffn_sW1"][None]], 0).transpose(1, 0, 2)
    r["b1"] = np.concatenate([a["L0_ffn_b1"], a["L0_ffn_sb1"][None]], 0).reshape(9, 4, 128).transpose(2, 0, 1)
    r["w2"] = np.concatenate([a["L0_ffn_W2"], a["L0_ffn_sW2"][None]], 0).reshape(9, 4, 128, 128).transpose(2, 0, 1, 3)
    r["b2"] = np.concatenate([a["L0_ffn_b2"], a["L0_ffn_sb2"][None]], 0)
    r["wqk"] = np.concatenate([a["L1_attn_Wq"], a["L1_attn_Wkv"][:, 0:512]], 1)
    r["wv"] = a["L1_attn_Wkv"][:, 512:]
    r["wout"] = a["L1_attn_Wout"].reshape(4, 128, 128).transpose(1, 0, 2)
    r["lam"] = np.stack([a["L1_attn_lambda_" + k] for k in ("q1", "k1", "q2", "k2")])
    r["gam"] = np.concatenate([a["L1_attn_gamma"]] * 2)[:, None]
    r["lnp"] = np.stack([a["L1_ffn_ln1_w"], a["L1_ffn_ln1_b"], a["L1_ffn_ln2_w"], a["L1_ffn_ln2_b"]])
    r["sims"] = np.stack([a["L1_ffn_smha_sim"], a["L1_ffn_moe_sim"]], 1)
    r["gates"] = np.stack([a["L1_ffn_smha_gates"], a["L1_ffn_moe_gates"]])
    r["wqkv3"] = np.stack([a["L1_ffn_q_proj"], a["L1_ffn_k_proj"], a["L1_ffn_v_proj"]]).transpose(2, 0, 1, 3)
    r["wo3"] = a["L1_ffn_o_proj"].transpose(1, 0, 2)
    r["w13"] = a["L1_ffn_w1"].transpose(1, 0, 2)
    r["w23"] = a["L1_ffn_w2"].transpose(1, 0, 2)
    r["ident"] = np.eye(128, dtype=np.float32)
    r["iota8"] = np.broadcast_to(np.arange(8, dtype=np.float32), (128, 8))
    r["tri"] = np.where(np.tril(np.ones((128, 128), bool)), np.float32(0), np.float32(-1e30)).astype(np.float32)
    return {k: asc(v) for k, v in r.items()}


def kernel(**inputs):
    import concourse.bacc as _bacc
    from concourse.bass_utils import run_bass_kernel_spmd as _run

    nc = _bacc.Bacc("TRN2", target_bir_lowering=False, num_devices=1)
    arrays = layout(inputs)
    d = {k: nc.dram_tensor(k + "_dram", v.shape, mybir.dt.from_np(v.dtype), kind="ExternalInput").ap()
         for k, v in arrays.items()}
    o = nc.dram_tensor("out_dram", (NB * T, C), F32, kind="ExternalOutput").ap()
    program(nc, d, o)
    r = _run(nc, [{k + "_dram": v for k, v in arrays.items()}], core_ids=[0])
    return r.results[0]["out_dram"].reshape(NB, T, C)
```
